# Optimizing a Trainium2 kernel written in Bass

```python
import numpy as np
import jax
import jax.numpy as jnp

def _softmax(x, axis=-1):
    return jax.nn.softmax(x, axis=axis)

def _gelu(x):
    return jax.nn.gelu(x, approximate=True)

def _silu(x):
    return jax.nn.silu(x)

def _sigmoid(x):
    return jax.nn.sigmoid(x)

def _layernorm(x, axis=-1, eps=1e-05):
    m = jnp.mean(x, axis=axis, keepdims=True)
    v = jnp.var(x, axis=axis, keepdims=True)
    return (x - m) / jnp.sqrt(v + eps)

def _scatter_add(tgt, idx, src, axis=0):
    return tgt.at[idx].add(src)

def _segment_sum(src, seg, n):
    return jax.ops.segment_sum(src, seg, n)
kernel_name = 'mk_vit_tower_postln_d1_tok_img1024_r4_b4d672'

def setup_inputs(seed: int=0):
    np.random.seed(seed)
    _w = jnp.asarray

    def _rec_inputs():
        import jax
        import jax.numpy as jnp
        _rk = jax.random.key(seed)
        x = -0.000169711 + 1.00022 * jax.random.normal(jax.random.fold_in(_rk, 1), (128, 3, 84, 84), jnp.float32)
        return x
    x = _rec_inputs()

    def _L0_tok_setup():
        import jax, jax.numpy as jnp
        import numpy as np
        C = 256
        H8 = 8
        DH = C // H8
        PS = 14
        CS = 3
        IMG = 168
        B = 4

        def _ln(x, g, b):
            mu = jnp.mean(x, axis=-1, keepdims=True)
            xc = x - mu
            var = jnp.mean(xc * xc, axis=-1, keepdims=True)
            return xc * jax.lax.rsqrt(var + 1e-05) * g + b

        def _forward(pixel_values, conv_w, class_emb, la_ln_q_g, la_ln_q_b, la_wq, la_ln_kv_g, la_ln_kv_b, la_wkv, la_proj_w, la_proj_b, ga_ln_q_g, ga_ln_q_b, ga_wq, ga_ln_kv_g, ga_ln_kv_b, ga_wkv, ga_proj_w, ga_proj_b, mod_w, mod_b):
            b = pixel_values.shape[0]
            pe = jax.lax.conv_general_dilated(pixel_values, conv_w, (PS, PS), 'VALID', dimension_numbers=('NCHW', 'OIHW', 'NCHW'))
            HP = pe.shape[2]
            h = HP // CS
            hw, N = (h * h, CS * CS)
            scale = C ** (-0.5)
            grid = pe.reshape(b, C, h, CS, h, CS)
            red = grid.mean(axis=(3, 5)).reshape(b, C, hw).transpose(0, 2, 1)
            win = grid.transpose(0, 2, 4, 3, 5, 1).reshape(b, hw, N, C)
            q = _ln(red, la_ln_q_g, la_ln_q_b) @ la_wq
            q = q.reshape(b, hw, H8, DH).transpose(0, 2, 1, 3)
            kv = _ln(win, la_ln_kv_g, la_ln_kv_b) @ la_wkv
            kv = kv.reshape(b, hw, N, 2, H8, DH).transpose(3, 0, 4, 1, 2, 5)
            k_, v_ = (kv[0], kv[1])
            attn = jax.nn.softmax(jnp.einsum('bhnd,bhnkd->bhnk', q * scale, k_), axis=-1)
            agg = jnp.einsum('bhnk,bhnkd->bhnd', attn, v_)
            agg = agg.transpose(0, 2, 1, 3).reshape(b, hw, C)
            local_out = red + agg @ la_proj_w + la_proj_b
            cls = jnp.broadcast_to(class_emb, (b, 1, C))
            gq = (_ln(cls, ga_ln_q_g, ga_ln_q_b) @ ga_wq).reshape(b, H8, DH)
            gkv = _ln(local_out, ga_ln_kv_g, ga_ln_kv_b) @ ga_wkv
            gkv = gkv.reshape(b, hw, 2, H8, DH).transpose(2, 0, 3, 1, 4)
            gk, gv = (gkv[0], gkv[1])
            gattn = jax.nn.softmax(jnp.einsum('bhd,bhnd->bhn', gq * scale, gk), axis=-1)
            gagg = jnp.einsum('bhn,bhnd->bhd', gattn, gv).reshape(b, 1, C)
            cls_out = cls + gagg @ ga_proj_w + ga_proj_b
            patch_out = local_out @ mod_w + mod_b
            return jnp.concatenate([patch_out, cls_out], axis=1)
        key = jax.random.key(seed)
        ks = jax.random.split(key, 16)
        nrm = lambda k, shape: jax.random.normal(k, shape, jnp.float32) * 0.02
        return {'pixel_values': jax.random.normal(ks[0], (B, 3, IMG, IMG), jnp.float32), 'pixel_masks': jnp.ones((B, 1, IMG, IMG), jnp.float32), 'conv_w': nrm(ks[1], (C, 3, PS, PS)), 'class_emb': nrm(ks[2], (C,)), 'la_ln_q_g': jnp.ones((C,)), 'la_ln_q_b': jnp.zeros((C,)), 'la_wq': nrm(ks[3], (C, C)), 'la_ln_kv_g': jnp.ones((C,)), 'la_ln_kv_b': jnp.zeros((C,)), 'la_wkv': nrm(ks[4], (C, 2 * C)), 'la_proj_w': nrm(ks[5], (C, C)), 'la_proj_b': jnp.zeros((C,)), 'ga_ln_q_g': jnp.ones((C,)), 'ga_ln_q_b': jnp.zeros((C,)), 'ga_wq': nrm(ks[6], (C, C)), 'ga_ln_kv_g': jnp.ones((C,)), 'ga_ln_kv_b': jnp.zeros((C,)), 'ga_wkv': nrm(ks[7], (C, 2 * C)), 'ga_proj_w': nrm(ks[8], (C, C)), 'ga_proj_b': jnp.zeros((C,)), 'mod_w': nrm(ks[9], (C, C)), 'mod_b': jnp.zeros((C,))}
    _L0_tok_all = _L0_tok_setup()
    _L0_tok_in = {k: v for k, v in _L0_tok_all.items() if k in ('pixel_masks', 'conv_w', 'class_emb', 'la_ln_q_g', 'la_ln_q_b', 'la_wq', 'la_ln_kv_g', 'la_ln_kv_b', 'la_wkv', 'la_proj_w', 'la_proj_b', 'ga_ln_q_g', 'ga_ln_q_b', 'ga_wq', 'ga_ln_kv_g', 'ga_ln_kv_b', 'ga_wkv', 'ga_proj_w', 'ga_proj_b', 'mod_w', 'mod_b')}
    del _L0_tok_all

    def _L0_attn_setup():
        import jax, jax.numpy as jnp
        import numpy as np
        D_MODEL = 256
        NUM_HEADS = 16
        MAX_LEN = 512
        BATCH = 2
        SEQ_LEN = 512
        key = jax.random.key(seed)
        ks = jax.random.split(key, 6)
        s = 0.02
        return {'x': jax.random.normal(ks[0], (BATCH, SEQ_LEN, D_MODEL), dtype=jnp.float32), 'Wq': jax.random.normal(ks[1], (D_MODEL, D_MODEL), dtype=jnp.float32) * s, 'bq': jnp.zeros((D_MODEL,), dtype=jnp.float32), 'Wk': jax.random.normal(ks[2], (D_MODEL, D_MODEL), dtype=jnp.float32) * s, 'bk': jnp.zeros((D_MODEL,), dtype=jnp.float32), 'Wv': jax.random.normal(ks[3], (D_MODEL, D_MODEL), dtype=jnp.float32) * s, 'bv': jnp.zeros((D_MODEL,), dtype=jnp.float32), 'rel_emb': jax.random.normal(ks[4], (NUM_HEADS, 2 * MAX_LEN - 1), dtype=jnp.float32)}
    _L0_attn_all = _L0_attn_setup()
    _L0_attn_in = {k: v for k, v in _L0_attn_all.items() if k in ('Wq', 'bq', 'Wk', 'bk', 'Wv', 'bv', 'rel_emb')}
    del _L0_attn_all

    def _L0_ffn_setup():
        import jax, jax.numpy as jnp
        import numpy as np
        N_EMBD = 256
        N_EXPERTS = 8
        TOP_K = 2
        B, T = (4, 512)
        key = jax.random.key(seed)
        ks = jax.random.split(key, 8)
        C, E, H = (N_EMBD, N_EXPERTS, 4 * N_EMBD)
        s_in = 1.0 / np.sqrt(C)
        s_hid = 1.0 / np.sqrt(H)
        x = jax.random.normal(ks[0], (B, T, C), dtype=jnp.float32)
        W1 = jax.random.uniform(ks[1], (E, C, H), minval=-s_in, maxval=s_in, dtype=jnp.float32)
        b1 = jax.random.uniform(ks[2], (E, H), minval=-s_in, maxval=s_in, dtype=jnp.float32)
        W2 = jax.random.uniform(ks[3], (E, H, C), minval=-s_hid, maxval=s_hid, dtype=jnp.float32)
        b2 = jax.random.uniform(ks[4], (E, C), minval=-s_hid, maxval=s_hid, dtype=jnp.float32)
        Wg = jax.random.uniform(ks[5], (C, E), minval=-s_in, maxval=s_in, dtype=jnp.float32)
        bg = jax.random.uniform(ks[6], (E,), minval=-s_in, maxval=s_in, dtype=jnp.float32)
        return {'x': x, 'W1': W1, 'b1': b1, 'W2': W2, 'b2': b2, 'Wg': Wg, 'bg': bg}
    _L0_ffn_all = _L0_ffn_setup()
    _L0_ffn_in = {k: v for k, v in _L0_ffn_all.items() if k in ('W1', 'b1', 'W2', 'b2', 'Wg', 'bg')}
    del _L0_ffn_all
    return {'x': x, 'L0_tok_pixel_masks': _L0_tok_in['pixel_masks'], 'L0_tok_conv_w': _L0_tok_in['conv_w'], 'L0_tok_class_emb': _L0_tok_in['class_emb'], 'L0_tok_la_ln_q_g': _L0_tok_in['la_ln_q_g'], 'L0_tok_la_ln_q_b': _L0_tok_in['la_ln_q_b'], 'L0_tok_la_wq': _L0_tok_in['la_wq'], 'L0_tok_la_ln_kv_g': _L0_tok_in['la_ln_kv_g'], 'L0_tok_la_ln_kv_b': _L0_tok_in['la_ln_kv_b'], 'L0_tok_la_wkv': _L0_tok_in['la_wkv'], 'L0_tok_la_proj_w': _L0_tok_in['la_proj_w'], 'L0_tok_la_proj_b': _L0_tok_in['la_proj_b'], 'L0_tok_ga_ln_q_g': _L0_tok_in['ga_ln_q_g'], 'L0_tok_ga_ln_q_b': _L0_tok_in['ga_ln_q_b'], 'L0_tok_ga_wq': _L0_tok_in['ga_wq'], 'L0_tok_ga_ln_kv_g': _L0_tok_in['ga_ln_kv_g'], 'L0_tok_ga_ln_kv_b': _L0_tok_in['ga_ln_kv_b'], 'L0_tok_ga_wkv': _L0_tok_in['ga_wkv'], 'L0_tok_ga_proj_w': _L0_tok_in['ga_proj_w'], 'L0_tok_ga_proj_b': _L0_tok_in['ga_proj_b'], 'L0_tok_mod_w': _L0_tok_in['mod_w'], 'L0_tok_mod_b': _L0_tok_in['mod_b'], 'L0_attn_Wq': _L0_attn_in['Wq'], 'L0_attn_bq': _L0_attn_in['bq'], 'L0_attn_Wk': _L0_attn_in['Wk'], 'L0_attn_bk': _L0_attn_in['bk'], 'L0_attn_Wv': _L0_attn_in['Wv'], 'L0_attn_bv': _L0_attn_in['bv'], 'L0_attn_rel_emb': _L0_attn_in['rel_emb'], 'L0_ffn_W1': _L0_ffn_in['W1'], 'L0_ffn_b1': _L0_ffn_in['b1'], 'L0_ffn_W2': _L0_ffn_in['W2'], 'L0_ffn_b2': _L0_ffn_in['b2'], 'L0_ffn_Wg': _L0_ffn_in['Wg'], 'L0_ffn_bg': _L0_ffn_in['bg']}

def reference(x, L0_tok_pixel_masks, L0_tok_conv_w, L0_tok_class_emb, L0_tok_la_ln_q_g, L0_tok_la_ln_q_b, L0_tok_la_wq, L0_tok_la_ln_kv_g, L0_tok_la_ln_kv_b, L0_tok_la_wkv, L0_tok_la_proj_w, L0_tok_la_proj_b, L0_tok_ga_ln_q_g, L0_tok_ga_ln_q_b, L0_tok_ga_wq, L0_tok_ga_ln_kv_g, L0_tok_ga_ln_kv_b, L0_tok_ga_wkv, L0_tok_ga_proj_w, L0_tok_ga_proj_b, L0_tok_mod_w, L0_tok_mod_b, L0_attn_Wq, L0_attn_bq, L0_attn_Wk, L0_attn_bk, L0_attn_Wv, L0_attn_bv, L0_attn_rel_emb, L0_ffn_W1, L0_ffn_b1, L0_ffn_W2, L0_ffn_b2, L0_ffn_Wg, L0_ffn_bg):
    import jax
    import jax.numpy as jnp

    def _L0_tok_ref(pixel_values, pixel_masks, conv_w, class_emb, la_ln_q_g, la_ln_q_b, la_wq, la_ln_kv_g, la_ln_kv_b, la_wkv, la_proj_w, la_proj_b, ga_ln_q_g, ga_ln_q_b, ga_wq, ga_ln_kv_g, ga_ln_kv_b, ga_wkv, ga_proj_w, ga_proj_b, mod_w, mod_b):
        import jax, jax.numpy as jnp
        import numpy as np
        C = 256
        H8 = 8
        DH = C // H8
        PS = 14
        CS = 3
        IMG = 168
        B = 4

        def _ln(x, g, b):
            mu = jnp.mean(x, axis=-1, keepdims=True)
            xc = x - mu
            var = jnp.mean(xc * xc, axis=-1, keepdims=True)
            return xc * jax.lax.rsqrt(var + 1e-05) * g + b

        def _forward(pixel_values, conv_w, class_emb, la_ln_q_g, la_ln_q_b, la_wq, la_ln_kv_g, la_ln_kv_b, la_wkv, la_proj_w, la_proj_b, ga_ln_q_g, ga_ln_q_b, ga_wq, ga_ln_kv_g, ga_ln_kv_b, ga_wkv, ga_proj_w, ga_proj_b, mod_w, mod_b):
            b = pixel_values.shape[0]
            pe = jax.lax.conv_general_dilated(pixel_values, conv_w, (PS, PS), 'VALID', dimension_numbers=('NCHW', 'OIHW', 'NCHW'))
            HP = pe.shape[2]
            h = HP // CS
            hw, N = (h * h, CS * CS)
            scale = C ** (-0.5)
            grid = pe.reshape(b, C, h, CS, h, CS)
            red = grid.mean(axis=(3, 5)).reshape(b, C, hw).transpose(0, 2, 1)
            win = grid.transpose(0, 2, 4, 3, 5, 1).reshape(b, hw, N, C)
            q = _ln(red, la_ln_q_g, la_ln_q_b) @ la_wq
            q = q.reshape(b, hw, H8, DH).transpose(0, 2, 1, 3)
            kv = _ln(win, la_ln_kv_g, la_ln_kv_b) @ la_wkv
            kv = kv.reshape(b, hw, N, 2, H8, DH).transpose(3, 0, 4, 1, 2, 5)
            k_, v_ = (kv[0], kv[1])
            attn = jax.nn.softmax(jnp.einsum('bhnd,bhnkd->bhnk', q * scale, k_), axis=-1)
            agg = jnp.einsum('bhnk,bhnkd->bhnd', attn, v_)
            agg = agg.transpose(0, 2, 1, 3).reshape(b, hw, C)
            local_out = red + agg @ la_proj_w + la_proj_b
            cls = jnp.broadcast_to(class_emb, (b, 1, C))
            gq = (_ln(cls, ga_ln_q_g, ga_ln_q_b) @ ga_wq).reshape(b, H8, DH)
            gkv = _ln(local_out, ga_ln_kv_g, ga_ln_kv_b) @ ga_wkv
            gkv = gkv.reshape(b, hw, 2, H8, DH).transpose(2, 0, 3, 1, 4)
            gk, gv = (gkv[0], gkv[1])
            gattn = jax.nn.softmax(jnp.einsum('bhd,bhnd->bhn', gq * scale, gk), axis=-1)
            gagg = jnp.einsum('bhn,bhnd->bhd', gattn, gv).reshape(b, 1, C)
            cls_out = cls + gagg @ ga_proj_w + ga_proj_b
            patch_out = local_out @ mod_w + mod_b
            return jnp.concatenate([patch_out, cls_out], axis=1)
        del pixel_masks
        return _forward(pixel_values, conv_w, class_emb, la_ln_q_g, la_ln_q_b, la_wq, la_ln_kv_g, la_ln_kv_b, la_wkv, la_proj_w, la_proj_b, ga_ln_q_g, ga_ln_q_b, ga_wq, ga_ln_kv_g, ga_ln_kv_b, ga_wkv, ga_proj_w, ga_proj_b, mod_w, mod_b)

    def _L0_attn_ref(x, Wq, bq, Wk, bk, Wv, bv, rel_emb):
        import jax, jax.numpy as jnp
        import numpy as np
        D_MODEL = 256
        NUM_HEADS = 16
        MAX_LEN = 512
        BATCH = 2
        SEQ_LEN = 512
        B, L, D = x.shape
        H = rel_emb.shape[0]
        dk = D // H

        def heads(y):
            return y.reshape(B, L, H, dk).transpose(0, 2, 1, 3)
        q = heads(x @ Wq + bq)
        k = heads(x @ Wk + bk)
        v = heads(x @ Wv + bv)
        scores = jnp.einsum('bhid,bhjd->bhij', q, k) / jnp.sqrt(jnp.float32(dk))
        pos = jnp.arange(L)
        rel_idx = pos[:, None] - pos[None, :] + (L - 1)
        bias = rel_emb[:, rel_idx]
        attn = jax.nn.softmax(scores + bias[None], axis=-1)
        out = jnp.einsum('bhij,bhjd->bhid', attn, v)
        return out.transpose(0, 2, 1, 3).reshape(B, L, D)

    def _L0_ffn_ref(x, W1, b1, W2, b2, Wg, bg):
        import jax, jax.numpy as jnp
        import numpy as np
        N_EMBD = 256
        N_EXPERTS = 8
        TOP_K = 2
        B, T = (4, 512)
        gate_scores = jax.nn.softmax(jnp.einsum('btc,ce->bte', x, Wg) + bg, axis=-1)
        h = jax.nn.relu(jnp.einsum('btc,ech->bteh', x, W1) + b1)
        expert_out = jnp.einsum('bteh,ehc->btec', h, W2) + b2
        topk_scores, topk_idx = jax.lax.top_k(gate_scores, TOP_K)
        top_probs = jax.nn.softmax(topk_scores, axis=-1)
        sel = jnp.take_along_axis(expert_out, topk_idx[..., None], axis=2)
        out = jnp.sum(sel * top_probs[..., None], axis=2)
        return out
    h = _L0_tok_ref(x, L0_tok_pixel_masks, L0_tok_conv_w, L0_tok_class_emb, L0_tok_la_ln_q_g, L0_tok_la_ln_q_b, L0_tok_la_wq, L0_tok_la_ln_kv_g, L0_tok_la_ln_kv_b, L0_tok_la_wkv, L0_tok_la_proj_w, L0_tok_la_proj_b, L0_tok_ga_ln_q_g, L0_tok_ga_ln_q_b, L0_tok_ga_wq, L0_tok_ga_ln_kv_g, L0_tok_ga_ln_kv_b, L0_tok_ga_wkv, L0_tok_ga_proj_w, L0_tok_ga_proj_b, L0_tok_mod_w, L0_tok_mod_b)
    h = _layernorm(h + _L0_attn_ref(h, L0_attn_Wq, L0_attn_bq, L0_attn_Wk, L0_attn_bk, L0_attn_Wv, L0_attn_bv, L0_attn_rel_emb), axis=-1)
    h = _layernorm(h + _L0_ffn_ref(h, L0_ffn_W1, L0_ffn_b1, L0_ffn_W2, L0_ffn_b2, L0_ffn_Wg, L0_ffn_bg), axis=-1)
    return h

_drawn_inputs = setup_inputs


def setup_inputs(seed=0):
    import zlib

    import numpy as np

    out = dict(_drawn_inputs(seed))
    spreads = {'L0_tok_pixel_masks': (1.0, 0.2),
     'L0_tok_la_ln_q_g': (1.0, 0.6),
     'L0_tok_la_ln_q_b': (0.0, 2.0),
     'L0_tok_la_ln_kv_g': (1.0, 0.2),
     'L0_tok_la_ln_kv_b': (0.0, 0.1),
     'L0_tok_la_proj_b': (0.0, 0.1),
     'L0_tok_ga_ln_q_g': (1.0, 0.6),
     'L0_tok_ga_ln_q_b': (0.0, 0.8),
     'L0_tok_ga_ln_kv_g': (1.0, 0.2),
     'L0_tok_ga_ln_kv_b': (0.0, 0.1),
     'L0_tok_ga_proj_b': (0.0, 0.1),
     'L0_tok_mod_b': (0.0, 0.1),
     'L0_attn_bq': (0.0, 0.8),
     'L0_attn_bk': (0.0, 2.0),
     'L0_attn_bv': (0.0, 0.1)}
    factors = {'L0_tok_la_wq': 5.646,
     'L0_tok_ga_wq': 6.561,
     'L0_attn_Wq': 35.421,
     'L0_attn_Wk': 8.0,
     'L0_ffn_b1': 5.709,
     'L0_ffn_b2': 4.632}
    for name, (base, spread) in spreads.items():
        noise = np.random.default_rng([zlib.crc32(name.encode()), seed]).standard_normal(out[name].shape)
        drawn = base * np.exp(spread * noise) if base else spread * noise
        out[name] = jnp.asarray(drawn.astype(out[name].dtype))
    for name, factor in factors.items():
        out[name] = (out[name] * factor).astype(out[name].dtype)
    return out
```

```python
from contextlib import ExitStack

import concourse.bass as bass
from concourse import mybir

ALU = mybir.AluOpType
ACT = mybir.ActivationFunctionType
F32 = mybir.dt.float32
F32R = mybir.dt.float32r
U32 = mybir.dt.uint32
AX_X = mybir.AxisListType.X

EPS = 1e-5


def build(nc, x, conv_w, class_emb, q_g, q_b, wq, kv_g, kv_b, wkv, proj_w, proj_b, gq_g, gq_b, gwq,
          gkv_g, gkv_b, gwkv, gproj_w, gproj_b, mod_w, mod_b, aWq, abq, aWk, abk, aWv, abv, rel,
          W1, b1, W2, b2, Wg, bg, out):
    B, CIN, IMG, _ = x.shape
    C = conv_w.shape[0]
    PS = conv_w.shape[2]
    P = 128
    KC = C // P
    GRID = IMG // PS
    CS = 3
    NW = (GRID // CS) ** 2
    NP = CS * CS
    NT = NW * NP
    H8 = 8
    DH = C // H8
    T = NW + 1
    H16 = rel.shape[0]
    DK = C // H16
    E, _, HID = W1.shape
    J = HID // P
    assert B == P and C == 256 and GRID == 2 * CS and NW == 4 and E == 8

    LINES = CIN * PS
    CL = P // PS
    K = CL * PS
    NK = -(-LINES // CL)
    START = [min(k * CL, LINES - CL) for k in range(NK)]
    OVER = ((NK - 1) * CL - START[-1]) * PS
    CW = C + 2
    GROUPS = [(0, 3), (3, NK)]
    TOK = T * P
    HALF = TOK // 2
    BANKS = -(-T // 2)

    with ExitStack() as ctx:
        def sb(name, shape, dt=F32):
            return ctx.enter_context(nc.sbuf_tensor(name, shape, dt))

        def sem(name):
            return ctx.enter_context(nc.semaphore(name))

        psum = ctx.enter_context(nc.psum_tensor("psum", [P, 8, 512], F32))
        PATCH_BANK = (0, 1, 2)
        CONV_BANK = (3, 4)
        TURN_BANK = 5
        RESULT_BANK = (6, 7)
        HIDDEN_BANK = (0, 2)
        EXPERT_BANK = 4
        GATE_BANK = 7

        ident = sb("ident", [P, P])
        minus_half = sb("minus_half", [P, 16])
        iota8i = sb("iota8i", [P, E], mybir.dt.int32)
        iota8 = sb("iota8", [P, E])
        wg_sb = sb("wg_sb", [P, KC, E])
        b2_sb = sb("b2_sb", [E, C])
        qkv_w = sb("qkv_w", [P, KC, 3 * C])
        rows_in = sb("rows_in", [E * J + 2 * KC, P])
        cols = sb("cols", [P, E * J + 2 * KC])
        b1_cols = cols[:, 0:E * J].rearrange("p (e j) -> p e j", e=E)
        kvg_cols = cols[:, E * J:E * J + KC]
        kvb_cols = cols[:, E * J + KC:E * J + 2 * KC]
        row = {name: sb("row_" + name, [P, width]) for name, width in (
            ("q_g", C), ("q_b", C), ("proj_b", C), ("gkv_g", C), ("gkv_b", C), ("gproj_b", C), ("mod_b", C),
            ("class", C), ("qkv_b", 3 * C), ("bg", E))}
        rel_rows = sb("rel_rows", [P, H16, 2 * T - 1])
        conv_mean = sb("conv_mean", [P, 2, NK])
        sumsq = sb("sumsq", [P, NW, NP + 1])
        var_eps = sb("var_eps", [P, NW, NP + 1])
        rstd = sb("rstd", [P, NW, NP + 1])
        mu9 = sb("mu9", [P, NW])
        qbk = sb("qbk", [P, H8])
        stat8 = sb("stat8", [P, 3, H8])
        bn = sb("bn", [P, T, 6])
        mv = sb("mv", [P, T, 2])
        ve = sb("ve", [P, T])
        rs = sb("rs", [P, T])
        gprob = sb("gprob", [P, NW, H8])
        gscore = sb("gscore", [P, 3, NW, H8])
        gstat = sb("gstat", [P, 3, H8])
        hs = sb("hs", [P, T, C])
        aq = sb("aq", [P, T, C])
        akv = sb("akv", [P, T, 2 * C])

        tokenizer_memory = ExitStack()

        def sbt(name, shape, dt=F32):
            return tokenizer_memory.enter_context(nc.sbuf_tensor(name, shape, dt))

        lines = sbt("lines", [P, CS, LINES, IMG])
        patches = sbt("patches", [P, 3, LINES * PS])
        conv_hi = sbt("conv_hi", [P, NK, CW], F32R)
        conv_lo = sbt("conv_lo", [P, NK, CW], F32R)
        patch_hi = sbt("patch_hi", [P, 2, NK, P], F32R)
        patch_lo = sbt("patch_lo", [P, 2, NK, P], F32R)
        cen = sbt("cen", [P, 3, CW])
        wkv_hi = sbt("wkv_hi", [P, KC, 2 * C], F32R)
        wkv_lo = sbt("wkv_lo", [P, KC, 2 * C], F32R)
        turn_hi = sbt("turn_hi", [P, 2, C], F32R)
        turn_lo = sbt("turn_lo", [P, 2, C], F32R)
        kv = sbt("kv", [P, 2, NP, 2 * C])
        wq_sb = sbt("wq_sb", [P, KC, C])
        proj_sb = sbt("proj_sb", [P, KC, C])
        gwkv_sb = sbt("gwkv_sb", [P, KC, 2 * C])
        gproj_sb = sbt("gproj_sb", [P, KC, C])
        mod_sb = sbt("mod_sb", [P, KC, C])
        kv_bias = sbt("kv_bias", [P, 2 * C])
        turn_f = sbt("turn_f", [P, 3, C])
        res = sbt("res", [P, 3, C])
        qkv_res = sbt("qkv_res", [P, 3 * C])
        q_sb = sbt("q_sb", [P, 2, C])
        gq_sb = sbt("gq_sb", [P, C])
        redsum = sbt("redsum", [P, 2, CW])
        redp = sbt("redp", [P, 2, C])
        redln = sbt("redln", [P, C])
        score = sbt("score", [P, 3, NP, H8])
        probe = sbt("probe", [P, 2, NP, H8])
        agg = sbt("agg", [P, C])
        kvln = sbt("kvln", [P, C])
        gagg = sbt("gagg", [P, C])
        junk = sbt("junk", [P, C])
        work = sbt("work", [P, C])
        start_memory = ExitStack()

        def sbs(name, shape, dt=F32):
            return start_memory.enter_context(nc.sbuf_tensor(name, shape, dt))

        conv_raw = sbs("conv_raw", [P, KC, LINES * PS])
        wkv_raw = sbs("wkv_raw", [P, KC, 2 * C])
        kvb_wide = sbs("kvb_wide", [P, KC, P])
        gwq_sb = sbs("gwq_sb", [P, KC, C])
        row["gq_g"] = sbs("row_gq_g", [P, C])
        row["gq_b"] = sbs("row_gq_b", [P, C])
        class_ln = sbs("class_ln", [P, C])
        start_memory.close()
        prod = sbt("prod", [P, NP, C])
        gkv_sb = sbt("gkv_sb", [P, NW, 2 * C])
        local = sbt("local", [P, 2, C])
        tokenizer_memory.close()

        w1_raw = sb("w1_raw", [P, KC, HID])
        w2_raw = sb("w2_raw", [P, J, C])
        w1_hi, w1_lo, w2_hi, w2_lo = [], [], [], []
        for u in range(2):
            for parts, name, shape in ((w1_hi, "w1_hi", [P, KC, HID]), (w1_lo, "w1_lo", [P, KC, HID]),
                                       (w2_hi, "w2_hi", [P, J, C]), (w2_lo, "w2_lo", [P, J, C])):
                parts.append(sb(f"{name}{u}", shape, F32R))
        att_prod = sb("att_prod", [P, 2, T, C])
        att_s = sb("att_s", [P, 3, T, H16, T])
        att_m = sb("att_m", [P, 3, T, H16])
        att_o = sb("att_o", [P, T, C])
        h1 = sb("h1", [P, T, C])
        xt_f = sb("xt_f", [P, KC, TOK])
        xt_hi = sb("xt_hi", [P, KC, TOK], F32R)
        xt_lo = sb("xt_lo", [P, KC, TOK], F32R)
        g8 = sb("g8", [P, 6, T, E])
        gt = sb("gt", [P, 10, T])
        top_at = sb("top_at", [P, T, E], U32)
        gates = sb("gates", [P, T, E])
        gates_t = sb("gates_t", [E, T, P])
        acc = sb("acc", [P, T, C])
        h_f = sb("h_f", [P, 2, TOK])
        h_hi = sb("h_hi", [P, 2, TOK], F32R)
        h_lo = sb("h_lo", [P, 2, TOK], F32R)
        fin = sb("fin", [P, T, C])

        first_loaded = sem("first_loaded")
        early_loaded = sem("early_loaded")
        wkv_loaded = sem("wkv_loaded")
        late_loaded = sem("late_loaded")
        lines_loaded = [sem(f"lines_loaded_{r}") for r in range(CS)]
        w1_loaded = sem("w1_loaded")
        w2_loaded = sem("w2_loaded")
        stored = sem("stored")
        ident_made = sem("ident_made")
        consts_made = sem("consts_made")
        conv_w_turned = sem("conv_w_turned")
        conv_w_centred = sem("conv_w_centred")
        conv_w_split = sem("conv_w_split")
        conv_mean_made = sem("conv_mean_made")
        conv_hi_done = sem("conv_hi_done")
        cols_turned = sem("cols_turned")
        cols_copied = sem("cols_copied")
        kvb_widened = sem("kvb_widened")
        kv_bias_made = sem("kv_bias_made")
        kv_bias_copied = sem("kv_bias_copied")
        wkv_split = sem("wkv_split")
        patches_gathered = sem("patches_gathered")
        patch_turned = sem("patch_turned")
        patch_hi_done = sem("patch_hi_done")
        patch_lo_done = sem("patch_lo_done")
        conv_done = sem("conv_done")
        cen_copied = sem("cen_copied")
        sumsq_done = sem("sumsq_done")
        red_summed = sem("red_summed")
        turned = sem("turned")
        turn_copied = sem("turn_copied")
        turn_lo_done = sem("turn_lo_done")
        projected = sem("projected")
        result_copied = sem("result_copied")
        var_done = sem("var_done")
        rstd_done = sem("rstd_done")
        redln_done = sem("redln_done")
        redp_done = sem("redp_done")
        pool_scored = sem("pool_scored")
        pool_weighed = sem("pool_weighed")
        shifted = sem("shifted")
        exp_done = sem("exp_done")
        probs_done = sem("probs_done")
        agg_done = sem("agg_done")
        local_done = sem("local_done")
        kvln_done = sem("kvln_done")
        class_ln_done = sem("class_ln_done")
        gagg_done = sem("gagg_done")
        token_done = sem("token_done")
        qkv_done = sem("qkv_done")
        pool_prod_done = sem("pool_prod_done")
        pool_prod_used = sem("pool_prod_used")
        h1_done = sem("h1_done")
        xt_copied = sem("xt_copied")
        xt_turned = sem("xt_turned")
        xt_split = sem("xt_split")
        gate_scored = sem("gate_scored")
        gates_done = sem("gates_done")
        gates_turned = sem("gates_turned")
        gates_t_copied = sem("gates_t_copied")
        gate_bias_done = sem("gate_bias_done")
        gate_bias_used = sem("gate_bias_used")
        w_hi_done = sem("w_hi_done")
        w_lo_done = sem("w_lo_done")
        hidden_done = sem("hidden_done")
        relu_done = sem("relu_done")
        h_hi_done = sem("h_hi_done")
        h_split = sem("h_split")
        hidden_used = sem("hidden_used")
        acc_ready = sem("acc_ready")
        fin_done = sem("fin_done")
        dve_chain = sem("dve_chain")
        pool_chain = sem("pool_chain")

        RED, QUERY, SCORE, WEIGH, SUM, PROJ, LOCAL, MOD, GKV, TOKEN, GSCORE, QKV, QKVB = (
            10, 11, 13, 16, 18, 21, 23, 24, 25, 26, 27, 27, 29)
        CLASSQ = 6
        GATT = NP * (NW - 1) + GSCORE + 1
        CLASSO = GATT + 2
        SPLIT0 = NT + 2
        STEPS = CLASSO + 6

        def extras(s):
            found = [(kind, w) for w in range(NW) for kind, at in
                     (("query", QUERY), ("proj", PROJ), ("mod", MOD), ("gkv", GKV), ("qkv", QKV))
                     if s == NP * w + at]
            if s == CLASSQ:
                found.append(("gquery", 0))
            if s == CLASSO:
                found.append(("gproj", 0))
            if s == CLASSO + 3:
                found.append(("qkv", NW))
            return found

        turn_order = []
        result_order = []
        for s in range(STEPS):
            if 0 <= s - 2 < NT:
                turn_order.append(("kv", s - 2))
                result_order.append(("kv", s - 2, 0))
            for kind, w in extras(s - 1):
                result_order.append((kind, w, 0))
                if kind == "qkv":
                    result_order.append((kind, w, 1))
            turn_order += extras(s)
        kv_turns = [sum(k == "kv" for k, _ in turn_order[:i]) for i in range(len(turn_order) + 1)]
        plain_turns = [i - n for i, n in enumerate(kv_turns)]

        def copied(kind, w, part=0):
            return result_order.index((kind, w, part)) + 1

        def slot_of(t):
            w, n = divmod(t, NP)
            return n // CS, ((w % 2) * CS + n % CS) * PS

        VAR_ORDER = [found for s in range(STEPS) for found in
                     [("class", 0)] * (s == CLASSQ - 1)
                     + [("red", w) for w in range(NW) if s == NP * w + RED]
                     + [("local", w) for w in range(NW) if s == NP * w + LOCAL]]
        VAR_ORDER += ["attention", "output"]
        POW_ORDER = VAR_ORDER
        LATE = 26
        POOL_ROWS = 2
        DVE_ORDER = [2, 0, 3, 4, 1]

        def attention_product(eng, half, i, b):
            if half == 0:
                return eng.tensor_tensor(att_prod[:, b], akv[:, :, 0:C],
                                         aq[:, i, :].unsqueeze(1).broadcast_to([P, T, C]), ALU.mult)
            return eng.tensor_tensor(att_prod[:, b].rearrange("p j (h d) -> p j h d", h=H16),
                                     akv[:, :, C:2 * C].rearrange("p j (h d) -> p j h d", h=H16),
                                     att_s[:, 1, i].rearrange("p h j -> p j h").unsqueeze(3).broadcast_to(
                                         [P, T, H16, DK]), ALU.mult)

        block = ctx.enter_context(nc.Block())

        @block.sync
        def _(sp):
            rows_of = x.rearrange("b c (r k) x -> r b c (k x)", k=PS)

            def load_lines(hy, r):
                sp.dma_start(lines[:, r].rearrange("p (c k) x -> p c (k x)", c=CIN),
                             rows_of[hy * CS + r]).then_inc(lines_loaded[r], 16)

            def load(dst, src, which):
                sp.dma_start(dst, src).then_inc(which, 16)

            load(conv_raw[:], conv_w.rearrange("(h o) c y x -> o h (c y x)", o=P), first_loaded)
            load(rows_in[0:E * J], b1.rearrange("e (j p) -> (e j) p", p=P), early_loaded)
            load(rows_in[E * J:E * J + KC], kv_g.rearrange("(k p) -> k p", p=P), early_loaded)
            load(rows_in[E * J + KC:E * J + 2 * KC], kv_b.rearrange("(k p) -> k p", p=P), early_loaded)
            load_lines(0, 0)
            load(wkv_raw[:], wkv.rearrange("(k p) n -> p k n", p=P), wkv_loaded)
            load_lines(0, 1)
            load_lines(0, 2)
            for name, src in (("class", class_emb), ("gq_g", gq_g), ("gq_b", gq_b), ("q_g", q_g), ("q_b", q_b),
                              ("proj_b", proj_b), ("gkv_g", gkv_g), ("gkv_b", gkv_b), ("gproj_b", gproj_b),
                              ("mod_b", mod_b), ("bg", bg)):
                load(row[name][:], src.partition_broadcast(P), late_loaded)
            for dst, src in ((gwq_sb[:], gwq), (wq_sb[:], wq), (proj_sb[:], proj_w), (gwkv_sb[:], gwkv),
                             (mod_sb[:], mod_w), (gproj_sb[:], gproj_w), (qkv_w[:, :, 0:C], aWq),
                             (qkv_w[:, :, C:2 * C], aWk), (qkv_w[:, :, 2 * C:3 * C], aWv), (wg_sb[:], Wg)):
                load(dst, src.rearrange("(k p) n -> p k n", p=P), late_loaded)
            for n, src in enumerate((abq, abk, abv)):
                load(row["qkv_b"][:, n * C:(n + 1) * C], src.partition_broadcast(P), late_loaded)
            load(rel_rows[:], rel[:, 0:2 * T - 1].partition_broadcast(P), late_loaded)
            load(b2_sb[:], b2, late_loaded)
            for r in range(CS):
                sp.wait_ge(patches_gathered, NP + CS * r + CS)
                load_lines(1, r)
            sp.wait_ge(patches_gathered, NT)
            sp.dma_start(w1_raw[:], W1[0].rearrange("(k p) h -> p k h", p=P)).then_inc(w1_loaded, 16)
            sp.dma_start(w2_raw[:], W2[0].rearrange("(j p) c -> p j c", p=P)).then_inc(w2_loaded, 16)
            w1_rows = W1.rearrange("e (k p) h -> e p k h", p=P)
            w2_rows = W2.rearrange("e (j p) c -> e p j c", p=P)
            with sp.Fori(1, E) as e:
                sp.wait_ge(w_lo_done, J * e - J // 2)
                sp.dma_start(w1_raw[:], w1_rows[bass.ds(e, 1)].rearrange("e p k h -> (e p) k h")
                             ).then_inc(w1_loaded, 16)
                sp.wait_ge(w_lo_done, J * e)
                sp.dma_start(w2_raw[:], w2_rows[bass.ds(e, 1)].rearrange("e p j c -> (e p) j c")
                             ).then_inc(w2_loaded, 16)
            for i in range(T):
                sp.wait_ge(fin_done, i + 1)
                sp.dma_start(out[:, i, :], fin[:, i, :]).then_inc(stored, 16)
            sp.wait_ge(stored, 16 * T)

        def piece(j):
            if j < J // 2:
                k, h = divmod(j, J // 2 // KC)
                wide = HID * KC // (J // 2)
                cut = slice(h * wide, (h + 1) * wide)
                return w1_raw[:, k, cut], lambda u: w1_hi[u][:, k, cut], lambda u: w1_lo[u][:, k, cut]
            a = (j - J // 2) * 2
            return w2_raw[:, a:a + 2, :], lambda u: w2_hi[u][:, a:a + 2, :], lambda u: w2_lo[u][:, a:a + 2, :]

        @block.scalar
        def _(act):
            act.wait_ge(cols_turned, 1)
            nc.scalar.activation(cols[:], psum[:, RESULT_BANK[0], 0:E * J + 2 * KC], ACT.Copy).then_inc(cols_copied, 1)
            act.wait_ge(conv_mean_made, 1)
            for k in range(NK):
                nc.scalar.activation(conv_hi[0:K, k, 0:C], psum[0:K, k, 0:C], ACT.Identity,
                                     bias=conv_mean[0:K, 1, k:k + 1]).then_inc(conv_hi_done, 1)

            def patch_highs(t):
                if t >= 2:
                    act.wait_ge(conv_done, t - 1)
                for g, (a, b) in enumerate(GROUPS):
                    act.wait_ge(patch_turned, 2 * t + g + 1)
                    nc.scalar.activation(patch_hi[0:K, t % 2, a:b, :],
                                         psum[0:K, PATCH_BANK[(2 * t + g) % 3], 0:(b - a) * P],
                                         ACT.Copy).then_inc(patch_hi_done, 1)

            def copy_centred(t):
                act.wait_ge(conv_done, t + 1)
                if t >= 3:
                    act.wait_ge(turned, turn_order.index(("kv", t - 3)) + 1)
                    act.wait_ge(sumsq_done, t - 2)
                    act.wait_ge(red_summed, t - 2)
                nc.scalar.activation(cen[:, t % 3, :], psum[:, CONV_BANK[t % 2], 0:CW], ACT.Copy).then_inc(cen_copied, 1)

            def copy_turned(item):
                i = turn_order.index(item)
                act.wait_ge(turned, i + 1)
                if item[0] == "kv":
                    dst = turn_hi[:, item[1] % 2, :]
                else:
                    dst = turn_f[:, plain_turns[i] % 3, :]
                nc.scalar.activation(dst, psum[:, TURN_BANK, 0:C], ACT.Copy).then_inc(turn_copied, 1)

            def copy_result(kind, w, part):
                i = result_order.index((kind, w, part))
                act.wait_ge(projected, i + 1)
                src = psum[:, RESULT_BANK[i % 2], :]
                if kind == "kv":
                    v, n = divmod(w, NP)
                    if v >= 2 and n == 0:
                        act.wait_ge(agg_done, v - 1)
                        act.wait_ge(pool_weighed, v - 1)
                    nc.scalar.activation(kv[:, v % 2, n, :], src, ACT.Copy).then_inc(result_copied, 1)
                elif kind == "query":
                    nc.scalar.activation(q_sb[:, w % 2, :], src[:, 0:C], ACT.Copy, scale=C ** -0.5
                                         ).then_inc(result_copied, 1)
                elif kind == "gquery":
                    nc.scalar.activation(gq_sb[:], src[:, 0:C], ACT.Copy, scale=C ** -0.5).then_inc(result_copied, 1)
                elif kind == "gkv":
                    nc.scalar.activation(gkv_sb[:, w, :], src, ACT.Copy).then_inc(result_copied, 1)
                elif kind == "qkv":
                    dst = qkv_res[:, 0:2 * C] if part == 0 else qkv_res[:, 2 * C:3 * C]
                    if w >= 1:
                        act.wait_ge(qkv_done, w)
                    nc.scalar.activation(dst, src[:, 0:dst.shape[1]], ACT.Copy).then_inc(result_copied, 1)
                else:
                    nc.scalar.activation(res[:, ("proj", "mod", "gproj").index(kind), :], src[:, 0:C],
                                         ACT.Copy).then_inc(result_copied, 1)

            for s in range(STEPS):
                if s < NT:
                    patch_highs(s)
                if s == 0:
                    act.wait_ge(kv_bias_made, 1)
                    nc.scalar.activation(kv_bias[:], psum[:, RESULT_BANK[1], :], ACT.Copy).then_inc(kv_bias_copied, 1)
                if 0 <= s - 2 < NT:
                    copy_turned(("kv", s - 2))
                if 0 <= s - 1 < NT:
                    copy_centred(s - 1)
                if 0 <= s - 2 < NT:
                    copy_result("kv", s - 2, 0)
                for kind, w in extras(s - 1):
                    copy_result(kind, w, 0)
                    if kind == "qkv":
                        copy_result(kind, w, 1)
                for item in extras(s):
                    copy_turned(item)
                for w in range(NW):
                    if s == NP * w + SCORE + 2:
                        act.wait_ge(shifted, w + 1)
                        nc.scalar.activation(score[:, 2], score[:, 1], ACT.Exp).then_inc(exp_done, 1)
                if SPLIT0 <= s < SPLIT0 + J:
                    j = s - SPLIT0
                    act.wait_ge(w1_loaded if j < J // 2 else w2_loaded, 16)
                    raw, hi, _ = piece(j)
                    nc.scalar.activation(hi(0), raw, ACT.Copy).then_inc(w_hi_done, 1)
                if s == GATT:
                    act.wait_ge(shifted, NW + 1)
                    nc.scalar.activation(gscore[:, 2], gscore[:, 1], ACT.Exp).then_inc(exp_done, 1)

            act.wait_ge(shifted, NW + 2)
            nc.scalar.activation(att_s[:, 2], att_s[:, 1], ACT.Exp).then_inc(exp_done, 1)
            for i in range(T):
                act.wait_ge(xt_turned, i + 1)
                nc.scalar.activation(xt_f[:, :, i * P:(i + 1) * P],
                                     psum[:, RESULT_BANK[i % 2], 0:C].rearrange("p (k t) -> p k t", k=KC),
                                     ACT.Copy).then_inc(xt_copied, 1)
            act.wait_ge(shifted, NW + 3)
            nc.scalar.activation(g8[:, 2], g8[:, 1], ACT.Exp).then_inc(exp_done, 1)
            act.wait_ge(shifted, NW + 4)
            nc.scalar.activation(gt[:, 6], gt[:, 5], ACT.Exp).then_inc(exp_done, 1)

            def relu(e, j):
                act.wait_ge(hidden_done, J * e + j + 1)
                if j >= 2:
                    act.wait_ge(h_split, J * e + j - 1)
                b = HIDDEN_BANK[j % 2]
                nc.scalar.activation(h_f[:, j % 2, :].rearrange("p (a t) -> p a t", a=2),
                                     psum[:, b:b + 2, 0:HALF], ACT.Relu,
                                     bias=b1_cols[:, bass.ds(e, 1), j]).then_inc(relu_done, 1)

            def split_high(e, u, j):
                raw, hi, _ = piece(j)
                if j == 0:
                    act.wait_ge(w1_loaded, 16 * e + 16)
                if j == J // 2:
                    act.wait_ge(w2_loaded, 16 * e + 16)
                nc.scalar.activation(hi(u), raw, ACT.Copy).then_inc(w_hi_done, 1)

            def expert(e, u, more):
                for j in range(J):
                    relu(e, j)
                    if more:
                        split_high(e + 1, 1 - u, j)

            with act.Fori(0, E // 2 - 1) as i:
                expert(2 * i, 0, True)
                expert(2 * i + 1, 1, True)
            expert(E - 2, 0, True)
            expert(E - 1, 1, False)

        @block.tensor
        def _(pe):
            pe.wait_ge(ident_made, 1)
            pe.wait_ge(first_loaded, 16)
            for k in range(NK):
                for h in range(KC):
                    last = nc.tensor.transpose(psum[0:K, k, h * P:(h + 1) * P],
                                               conv_raw[:, h, START[k] * PS:START[k] * PS + K], ident[:])
            last.then_inc(conv_w_turned, 1)
            pe.wait_ge(early_loaded, 16 * 3)
            n = E * J + 2 * KC
            nc.tensor.transpose(psum[:, RESULT_BANK[0], 0:n], rows_in[:], ident[0:n, 0:n]).then_inc(cols_turned, 1)

            def kv_bias_product():
                pe.wait_ge(kvb_widened, 1)
                pe.wait_ge(wkv_loaded, 16)
                for k in range(KC):
                    last = nc.tensor.matmul(psum[:, RESULT_BANK[1], :], kvb_wide[:, k, :], wkv_raw[:, k, :],
                                            start=(k == 0), stop=(k == KC - 1))
                last.then_inc(kv_bias_made, 1)

            def turn_patches(t):
                pe.wait_ge(patches_gathered, t + 1)
                for g, (a, b) in enumerate(GROUPS):
                    bank = PATCH_BANK[(2 * t + g) % 3]
                    if 2 * t + g < 3:
                        pe.wait_ge(conv_w_centred, 2 * t + g + 1)
                    else:
                        pe.wait_ge(patch_lo_done, 2 * t + g - 2)
                    for k in range(a, b):
                        last = nc.tensor.transpose(psum[0:K, bank, (k - a) * P:(k - a + 1) * P],
                                                   patches[:, t % 3, START[k] * PS:START[k] * PS + K], ident[:])
                    last.then_inc(patch_turned, 1)

            def convolve(t):
                pe.wait_ge(patch_lo_done, 2 * t + 2)
                if t == 0:
                    pe.wait_ge(conv_w_split, 2)
                if t >= 2:
                    pe.wait_ge(cen_copied, t - 1)
                dst = psum[:, CONV_BANK[t % 2], 0:CW]
                passes = [(p, w) for k in range(NK) for p, w in
                          ((patch_hi[0:K, t % 2, k, :], conv_hi[0:K, k, :]),
                           (patch_hi[0:K, t % 2, k, :], conv_lo[0:K, k, :]),
                           (patch_lo[0:K, t % 2, k, :], conv_hi[0:K, k, :]))]
                for m, (p, w) in enumerate(passes):
                    last = nc.tensor.matmul(dst, p, w, start=(m == 0), stop=(m == len(passes) - 1))
                last.then_inc(conv_done, 1)

            def turn(item):
                i = turn_order.index(item)
                kind, w = item
                if i >= 1:
                    pe.wait_ge(turn_copied, i)
                    if turn_order[i - 1][0] == "kv":
                        pe.wait_ge(turn_lo_done, kv_turns[i])
                if kind == "kv":
                    pe.wait_ge(cen_copied, w + 1)
                    src = cen[:, w % 3, 0:C]
                elif kind == "query":
                    pe.wait_ge(redln_done, w + 1)
                    src = redln[:]
                elif kind == "proj":
                    pe.wait_ge(agg_done, w + 1)
                    src = agg[:]
                elif kind == "mod":
                    pe.wait_ge(local_done, w + 1)
                    src = local[:, w % 2, :]
                elif kind == "gkv":
                    pe.wait_ge(kvln_done, w + 1)
                    src = kvln[:]
                elif kind == "gquery":
                    pe.wait_ge(class_ln_done, 1)
                    src = class_ln[:]
                elif kind == "gproj":
                    pe.wait_ge(gagg_done, 1)
                    src = gagg[:]
                else:
                    pe.wait_ge(token_done, w + 1)
                    src = hs[:, w, :]
                for k in range(KC):
                    last = nc.tensor.transpose(psum[:, TURN_BANK, k * P:(k + 1) * P],
                                               src[:, k * P:(k + 1) * P], ident[:])
                last.then_inc(turned, 1)

            def project(kind, w, part):
                i = result_order.index((kind, w, part))
                ti = turn_order.index((kind, w))
                pe.wait_ge(turn_copied, ti + 1)
                if i >= 2:
                    pe.wait_ge(result_copied, i - 1)
                elif i == 0:
                    pe.wait_ge(cols_copied, 1)
                else:
                    pe.wait_ge(kv_bias_copied, 1)
                bank = RESULT_BANK[i % 2]
                if kind == "kv":
                    pe.wait_ge(turn_lo_done, w + 1)
                    if w == 0:
                        pe.wait_ge(wkv_split, 1)
                    b = w % 2
                    passes = [(p, wt) for k in range(KC) for p, wt in
                              ((turn_hi[:, b, k * P:(k + 1) * P], wkv_hi[:, k, :]),
                               (turn_hi[:, b, k * P:(k + 1) * P], wkv_lo[:, k, :]),
                               (turn_lo[:, b, k * P:(k + 1) * P], wkv_hi[:, k, :]))]
                    width = 2 * C
                else:
                    b = plain_turns[ti] % 3
                    wt, width = {"query": (wq_sb[:], C), "proj": (proj_sb[:], C), "mod": (mod_sb[:], C),
                                 "gkv": (gwkv_sb[:], 2 * C), "gquery": (gwq_sb[:], C), "gproj": (gproj_sb[:], C),
                                 "qkv": (qkv_w[:, :, 0:2 * C] if part == 0 else qkv_w[:, :, 2 * C:3 * C],
                                         2 * C if part == 0 else C)}[kind]
                    passes = [(turn_f[:, b, k * P:(k + 1) * P], wt[:, k, :]) for k in range(KC)]
                for m, (p, m_w) in enumerate(passes):
                    last = nc.tensor.matmul(psum[:, bank, 0:width], p, m_w, start=(m == 0),
                                            stop=(m == len(passes) - 1))
                last.then_inc(projected, 1)

            for s in range(STEPS):
                if s < NT:
                    turn_patches(s)
                if s == 0:
                    kv_bias_product()
                if s == CLASSQ:
                    pe.wait_ge(late_loaded, 16 * LATE)
                if 0 <= s - 2 < NT:
                    turn(("kv", s - 2))
                if 0 <= s - 1 < NT:
                    convolve(s - 1)
                if 0 <= s - 2 < NT:
                    project("kv", s - 2, 0)
                for kind, w in extras(s - 1):
                    project(kind, w, 0)
                    if kind == "qkv":
                        project(kind, w, 1)
                for item in extras(s):
                    turn(item)

            for i in range(T):
                pe.wait_ge(h1_done, i + 1)
                if i >= 2:
                    pe.wait_ge(xt_copied, i - 1)
                for k in range(KC):
                    last = nc.tensor.transpose(psum[:, RESULT_BANK[i % 2], k * P:(k + 1) * P],
                                               h1[:, i, k * P:(k + 1) * P], ident[:])
                last.then_inc(xt_turned, 1)
            pe.wait_ge(xt_copied, T)
            for i in range(T):
                for k in range(KC):
                    last = nc.tensor.matmul(psum[:, GATE_BANK, i * E:(i + 1) * E],
                                            xt_f[:, k, i * P:(i + 1) * P], wg_sb[:, k, :],
                                            start=(k == 0), stop=(k == KC - 1))
            last.then_inc(gate_scored, 1)
            pe.wait_ge(xt_split, 2)

            def hidden(e, u, j):
                if j >= 2:
                    pe.wait_ge(relu_done, J * e + j - 1)
                b = HIDDEN_BANK[j % 2]
                cut = slice(j * P, (j + 1) * P)
                passes = [(w, xt) for k in range(KC) for w, xt in
                          ((w1_hi[u][:, k, cut], xt_hi[:, k, :]), (w1_hi[u][:, k, cut], xt_lo[:, k, :]),
                           (w1_lo[u][:, k, cut], xt_hi[:, k, :]))]
                for m, (w, xt) in enumerate(passes):
                    for a in range(2):
                        last = nc.tensor.matmul(psum[:, b + a, 0:HALF], w, xt[:, a * HALF:(a + 1) * HALF],
                                                start=(m == 0), stop=(m == len(passes) - 1))
                last.then_inc(hidden_done, 1)

            def outer(e, u, j):
                pe.wait_ge(h_split, J * e + j + 1)
                if j == 0:
                    pe.wait_ge(w_lo_done, J * e + J)
                for i in range(T):
                    if j == 0 and i % 2 == 0:
                        pe.wait_ge(acc_ready, BANKS * e + i // 2 + 1)
                    dst = psum[:, EXPERT_BANK + i // 2, (i % 2) * C:(i % 2 + 1) * C]
                    cut = slice(i * P, (i + 1) * P)
                    passes = ((h_hi[:, j % 2, cut], w2_hi[u][:, j, :]), (h_hi[:, j % 2, cut], w2_lo[u][:, j, :]),
                              (h_lo[:, j % 2, cut], w2_hi[u][:, j, :]))
                    for m, (h, w) in enumerate(passes):
                        last = nc.tensor.matmul(dst, h, w, start=(j == 0 and m == 0 and i % 2 == 0),
                                                stop=(j == J - 1 and m == 2), skip_group_check=True)
                last.then_inc(hidden_used, 1)

            def turn_gates(tiles):
                for i in tiles:
                    last = nc.tensor.transpose(psum[0:E, GATE_BANK, (i % 4) * P:(i % 4 + 1) * P], gates[:, i, :],
                                               ident[:])
                last.then_inc(gates_turned, 1)

            def second_bias(tiles):
                for i in tiles:
                    last = nc.tensor.matmul(psum[:, GATE_BANK, (i % 2) * C:(i % 2 + 1) * C], gates_t[:, i, :],
                                            b2_sb[:], start=True, stop=True, skip_group_check=True)
                last.then_inc(gate_bias_done, 1)

            def beside(j):
                if j == 1:
                    pe.wait_ge(gates_done, 1)
                    turn_gates(range(0, 4))
                if j == 3:
                    pe.wait_ge(gates_t_copied, 1)
                    turn_gates(range(4, T))
                if j in (5, 6, 7):
                    if j == 5:
                        pe.wait_ge(gates_t_copied, 2)
                    else:
                        pe.wait_ge(gate_bias_used, j - 5)
                    second_bias(range(2 * (j - 5), min(2 * (j - 5) + 2, T)))

            def expert(e, u, more=True, beside=lambda j: None):
                for j in range(1, J):
                    hidden(e, u, j)
                    outer(e, u, j - 1)
                    beside(j)
                if more:
                    pe.wait_ge(w_lo_done, J * e + J + J // 2)
                    hidden(e + 1, 1 - u, 0)
                outer(e, u, J - 1)

            pe.wait_ge(w_lo_done, J // 2)
            hidden(0, 0, 0)
            with pe.Fori(0, E // 2 - 1) as i:
                expert(2 * i, 0)
                expert(2 * i + 1, 1)
            expert(E - 2, 0, beside=beside)
            expert(E - 1, 1, more=False)

        @block.gpsimd
        def _(pool):
            chain = [0]

            def link(ins):
                chain[0] += 1
                ins.then_inc(pool_chain, 1)
                pool.wait_ge(pool_chain, chain[0])

            link(nc.gpsimd.memset(ident[:], 0.0))
            nc.gpsimd.affine_select(out=ident[:], in_=ident[:], compare_op=ALU.not_equal, fill=1.0, base=0,
                                    pattern=[[-1, P]], channel_multiplier=1).then_inc(ident_made, 1)
            nc.gpsimd.memset(minus_half[:], -0.5)
            nc.gpsimd.iota(iota8i[:], pattern=[[1, E]], base=0, channel_multiplier=0).then_inc(consts_made, 1)
            pool.wait_ge(consts_made, 1)
            nc.gpsimd.tensor_copy(iota8[:], iota8i[:]).then_inc(consts_made, 1)
            def power(dst, src, done):
                nc.gpsimd.tensor_tensor(dst, src, minus_half[:, 0:src.shape[1]], ALU.pow).then_inc(done, 1)

            def sum_reduced(t):
                w, n = divmod(t, NP)
                pool.wait_ge(cen_copied, t + 1)
                if n == 0:
                    nc.gpsimd.tensor_copy(redsum[:, w % 2, :], cen[:, t % 3, :]).then_inc(red_summed, 1)
                else:
                    pool.wait_ge(red_summed, t)
                    nc.gpsimd.tensor_tensor(redsum[:, w % 2, :], redsum[:, w % 2, :], cen[:, t % 3, :], ALU.add
                                            ).then_inc(red_summed, 1)

            def gather_patches(t):
                r, col = slot_of(t)
                w, n = divmod(t, NP)
                if n % CS == 0:
                    pool.wait_ge(lines_loaded[r], 16 * (w // 2 + 1))
                if t >= 3:
                    pool.wait_ge(patch_turned, 2 * (t - 2))
                nc.gpsimd.tensor_scalar(patches[:, t % 3, :].rearrange("p (l x) -> p l x", x=PS),
                                        lines[:, r, :, col:col + PS], 1.0, 0.0, ALU.mult, ALU.add
                                        ).then_inc(patches_gathered, 1)

            gather_patches(0)
            pool.wait_ge(cols_copied, 1)
            for k in range(KC):
                last = nc.gpsimd.tensor_copy(kvb_wide[:, k, :], kvb_cols[:, k:k + 1].broadcast_to([P, P]))
            last.then_inc(kvb_widened, 1)
            for s in range(STEPS):
                if s + 1 < NT:
                    gather_patches(s + 1)
                if 0 <= s - 1 < NT:
                    sum_reduced(s - 1)
                for w in range(NW):
                    at = s - NP * w
                    if at == RED:
                        pool.wait_ge(var_done, VAR_ORDER.index(("red", w)) + 1)
                        power(rstd[:, w, :], var_eps[:, w, :], rstd_done)
                        link(nc.gpsimd.tensor_scalar(mu9[:, w:w + 1], redsum[:, w % 2, C:C + 1], 1.0 / NP, None,
                                                     ALU.mult))
                        link(nc.gpsimd.tensor_scalar(redp[:, w % 2, :], redsum[:, w % 2, 0:C], 1.0 / NP,
                                                     mu9[:, w:w + 1], ALU.mult, ALU.add))
                        if w == 0:
                            pool.wait_ge(late_loaded, 16 * LATE)
                        nc.gpsimd.tensor_tensor(redp[:, w % 2, :], redp[:, w % 2, :], row["proj_b"][:], ALU.add
                                                ).then_inc(redp_done, 1)
                    if at == SCORE:
                        pool.wait_ge(result_copied, copied("query", w))
                        pool.wait_ge(result_copied, copied("kv", NP * w + NP - 1))
                        if w >= 1:
                            pool.wait_ge(agg_done, w)
                        nc.gpsimd.tensor_tensor(prod[:, 6:9, :], kv[:, w % 2, 6:9, 0:C],
                                                q_sb[:, w % 2, :].unsqueeze(1).broadcast_to([P, 3, C]), ALU.mult
                                                ).then_inc(pool_scored, 1)
                    if at == WEIGH:
                        pool.wait_ge(probs_done, w + 1)
                        nc.gpsimd.tensor_tensor(
                            prod[:, 6:9, :].rearrange("p n (h d) -> p n h d", h=H8),
                            kv[:, w % 2, 6:9, C:2 * C].rearrange("p n (h d) -> p n h d", h=H8),
                            probe[:, 1, 6:9, :].unsqueeze(3).broadcast_to([P, 3, H8, DH]), ALU.mult
                        ).then_inc(pool_weighed, 1)
                    if at == LOCAL:
                        pool.wait_ge(var_done, VAR_ORDER.index(("local", w)) + 1)
                        power(rs[:, w:w + 1], ve[:, w:w + 1], rstd_done)
                if s == CLASSQ - 1:
                    pool.wait_ge(var_done, VAR_ORDER.index(("class", 0)) + 1)
                    power(rs[:, NW:T], ve[:, NW:T], rstd_done)
                if SPLIT0 <= s < SPLIT0 + J:
                    j = s - SPLIT0
                    raw, hi, lo = piece(j)
                    pool.wait_ge(w_hi_done, j + 1)
                    nc.gpsimd.tensor_tensor(lo(0), raw, hi(0).bitcast(F32), ALU.subtract).then_inc(w_lo_done, 1)

            for half in (0, 1):
                if half == 1:
                    pool.wait_ge(probs_done, NW + 2)
                for i in range(POOL_ROWS):
                    if half == 0:
                        pool.wait_ge(qkv_done, T)
                    if i or half:
                        pool.wait_ge(pool_prod_used, POOL_ROWS * half + i)
                    attention_product(nc.gpsimd, half, i, 1).then_inc(pool_prod_done, 1)
            pool.wait_ge(var_done, len(VAR_ORDER) - 1)
            power(rs[:], ve[:], rstd_done)
            pool.wait_ge(var_done, len(VAR_ORDER))
            power(rs[:], ve[:], rstd_done)

        @block.vector
        def _(dve):
            chain = [0]

            def link(ins):
                chain[0] += 1
                return ins.then_inc(dve_chain, 1)

            def settle():
                dve.wait_ge(dve_chain, chain[0])

            V = nc.vector
            dve.wait_ge(conv_w_turned, 1)
            link(V.tensor_reduce(conv_mean[0:K, 0, :], psum[0:K, 0:NK, 0:C], AX_X, ALU.add))
            settle()
            V.tensor_scalar(conv_mean[0:K, 1, :], conv_mean[0:K, 0, :], -1.0 / C, None, ALU.mult
                            ).then_inc(conv_mean_made, 1)
            link(V.tensor_scalar(conv_mean[0:K, 0, :], conv_mean[0:K, 0, :], 1.0 / C, None, ALU.mult))
            dve.wait_ge(conv_mean_made, 1)
            settle()
            mean_twice = conv_mean[0:K, 0, :].unsqueeze(2).broadcast_to([K, NK, 2])
            link(V.tensor_copy(conv_hi[0:K, :, C:CW], mean_twice))
            settle()
            link(V.tensor_tensor(conv_lo[0:K, :, C:CW], mean_twice, conv_hi[0:K, :, C:CW].bitcast(F32), ALU.subtract))
            for k in range(NK):
                dve.wait_ge(conv_hi_done, k + 1)
                V.scalar_tensor_tensor(out=conv_lo[0:K, k, 0:C], in0=psum[0:K, k, 0:C],
                                       scalar=conv_mean[0:K, 1, k:k + 1], in1=conv_hi[0:K, k, 0:C].bitcast(F32),
                                       op0=ALU.add, op1=ALU.subtract).then_inc(conv_w_centred, 1)
            dve.wait_ge(conv_w_centred, NK)
            settle()
            V.memset(conv_hi[0:OVER, NK - 1, :].bitcast(F32), 0.0).then_inc(conv_w_split, 1)
            V.memset(conv_lo[0:OVER, NK - 1, :].bitcast(F32), 0.0).then_inc(conv_w_split, 1)

            def split_wkv():
                dve.wait_ge(wkv_loaded, 16)
                dve.wait_ge(cols_copied, 1)
                for k in range(KC):
                    link(V.tensor_scalar(wkv_hi[:, k, :], wkv_raw[:, k, :], kvg_cols[:, k:k + 1], None, ALU.mult))
                settle()
                for k in range(KC):
                    last = V.scalar_tensor_tensor(out=wkv_lo[:, k, :], in0=wkv_raw[:, k, :], scalar=kvg_cols[:, k:k + 1],
                                                  in1=wkv_hi[:, k, :].bitcast(F32), op0=ALU.mult, op1=ALU.subtract)
                last.then_inc(wkv_split, 1)

            def patch_lows(t):
                for g, (a, b) in enumerate(GROUPS):
                    dve.wait_ge(patch_hi_done, 2 * t + g + 1)
                    V.tensor_tensor(patch_lo[0:K, t % 2, a:b, :],
                                    psum[0:K, PATCH_BANK[(2 * t + g) % 3], 0:(b - a) * P].rearrange(
                                        "p (k t) -> p k t", t=P),
                                    patch_hi[0:K, t % 2, a:b, :].bitcast(F32), ALU.subtract).then_inc(patch_lo_done, 1)

            def turn_low(t):
                dve.wait_ge(turn_copied, turn_order.index(("kv", t)) + 1)
                V.tensor_tensor(turn_lo[:, t % 2, :], psum[:, TURN_BANK, 0:C], turn_hi[:, t % 2, :].bitcast(F32),
                                ALU.subtract).then_inc(turn_lo_done, 1)

            def square_sum(t):
                w, n = divmod(t, NP)
                dve.wait_ge(cen_copied, t + 1)
                if t >= 1:
                    dve.wait_ge(sumsq_done, t)
                c = cen[:, t % 3, 0:C]
                V.tensor_tensor_reduce(junk[:], c, c, 1.0, 0.0, ALU.mult, ALU.add,
                                       sumsq[:, w, n:n + 1]).then_inc(sumsq_done, 1)

            def layer_norm_stats(src, i):
                link(V.bn_stats(bn[:, i, :], src))
                settle()
                link(V.bn_aggr(mv[:, i, :], bn[:, i, :]))
                settle()
                V.tensor_scalar(ve[:, i:i + 1], mv[:, i, 1:2], EPS, None, ALU.add).then_inc(var_done, 1)

            def layer_norm(dst, src, i, gain, bias, done):
                link(V.tensor_scalar(work[:], src, mv[:, i, 0:1], rs[:, i:i + 1], ALU.subtract, ALU.mult))
                settle()
                link(V.tensor_tensor(work[:], work[:], gain, ALU.mult))
                settle()
                V.tensor_tensor(dst, work[:], bias, ALU.add).then_inc(done, 1)

            def reduced_query(w):
                dve.wait_ge(rstd_done, POW_ORDER.index(("red", w)) + 1)
                link(V.tensor_scalar(work[:], redsum[:, w % 2, 0:C], 1.0 / NP, rstd[:, w, NP:NP + 1], ALU.mult, ALU.mult))
                settle()
                link(V.tensor_tensor(work[:], work[:], row["q_g"][:], ALU.mult))
                settle()
                V.tensor_tensor(redln[:], work[:], row["q_b"][:], ALU.add).then_inc(redln_done, 1)

            def heads(ap):
                return ap.rearrange("p n (h d) -> p n h d", h=H8)

            def score_products(w, c):
                n = slice(3 * c, 3 * c + 3)
                if c == 2:
                    dve.wait_ge(pool_scored, w + 1)
                else:
                    link(V.tensor_tensor(prod[:, n, :], kv[:, w % 2, n, 0:C],
                                         q_sb[:, w % 2, :].unsqueeze(1).broadcast_to([P, 3, C]), ALU.mult))
                    settle()
                link(V.tensor_reduce(score[:, 0, n, :], heads(prod[:, n, :]), AX_X, ALU.add))

            def softmax_shift(w):
                by_patch = rstd[:, w, 0:NP].unsqueeze(2).broadcast_to([P, NP, H8])
                settle()
                link(V.tensor_tensor(score[:, 0], score[:, 0], by_patch, ALU.mult))
                settle()
                link(V.tensor_tensor(score[:, 0], score[:, 0], qbk[:].unsqueeze(1).broadcast_to([P, NP, H8]), ALU.add))
                settle()
                link(V.tensor_reduce(stat8[:, 0, :], score[:, 0].rearrange("p n h -> p h n"), AX_X, ALU.max))
                settle()
                V.tensor_tensor(score[:, 1], score[:, 0], stat8[:, 0, :].unsqueeze(1).broadcast_to([P, NP, H8]),
                                ALU.subtract).then_inc(shifted, 1)

            def softmax_weights(w):
                dve.wait_ge(exp_done, w + 1)
                link(V.tensor_reduce(stat8[:, 1, :], score[:, 2].rearrange("p n h -> p h n"), AX_X, ALU.add))
                settle()
                link(V.reciprocal(stat8[:, 2, :], stat8[:, 1, :]))
                settle()
                link(V.tensor_tensor(probe[:, 0], score[:, 2],
                                     stat8[:, 2, :].unsqueeze(1).broadcast_to([P, NP, H8]), ALU.mult))
                settle()
                V.tensor_tensor(probe[:, 1], probe[:, 0], rstd[:, w, 0:NP].unsqueeze(2).broadcast_to([P, NP, H8]),
                                ALU.mult).then_inc(probs_done, 1)

            def weigh_values(w, c):
                n = slice(3 * c, 3 * c + 3)
                dve.wait_ge(probs_done, w + 1)
                link(V.tensor_tensor(heads(prod[:, n, :]), heads(kv[:, w % 2, n, C:2 * C]),
                                     probe[:, 1, n, :].unsqueeze(3).broadcast_to([P, 3, H8, DH]), ALU.mult))

            def sum_values(w, part):
                cut = slice(part * C // 2, (part + 1) * C // 2)
                settle()
                dve.wait_ge(pool_weighed, w + 1)
                link(V.tensor_reduce(agg[:, cut], prod[:, :, cut].rearrange("p n c -> p c n"), AX_X, ALU.add))
                if part == 1:
                    settle()
                    V.tensor_tensor(agg[:], agg[:], kv_bias[:, C:2 * C], ALU.add).then_inc(agg_done, 1)

            def take_qkv(w):
                dve.wait_ge(result_copied, copied("qkv", w, 1))
                V.tensor_tensor(aq[:, w, :], qkv_res[:, 0:C], row["qkv_b"][:, 0:C], ALU.add)
                V.tensor_tensor(akv[:, T - 1 - w, :], qkv_res[:, C:3 * C], row["qkv_b"][:, C:3 * C], ALU.add
                                ).then_inc(qkv_done, 1)

            for s in range(STEPS):
                if s < NT:
                    patch_lows(s)
                if s == 0:
                    split_wkv()
                if 0 <= s - 2 < NT:
                    turn_low(s - 2)
                if 0 <= s - 1 < NT:
                    square_sum(s - 1)
                if s == CLASSQ - 1:
                    dve.wait_ge(late_loaded, 16 * LATE)
                    layer_norm_stats(row["class"][:], NW)
                if s == CLASSQ:
                    dve.wait_ge(rstd_done, POW_ORDER.index(("class", 0)) + 1)
                    layer_norm(class_ln[:], row["class"][:], NW, row["gq_g"][:], row["gq_b"][:], class_ln_done)
                for w in range(NW):
                    at = s - NP * w
                    if at == RED:
                        dve.wait_ge(sumsq_done, NP * (w + 1))
                        dve.wait_ge(red_summed, NP * (w + 1))
                        link(V.tensor_tensor_reduce(work[:], redsum[:, w % 2, 0:C], redsum[:, w % 2, 0:C], 1.0, 0.0, ALU.mult,
                                                    ALU.add, sumsq[:, w, NP:NP + 1]))
                        link(V.tensor_scalar(var_eps[:, w, 0:NP], sumsq[:, w, 0:NP], 1.0 / C, EPS, ALU.mult, ALU.add))
                        settle()
                        V.tensor_scalar(var_eps[:, w, NP:NP + 1], sumsq[:, w, NP:NP + 1], 1.0 / (C * NP * NP), EPS,
                                        ALU.mult, ALU.add).then_inc(var_done, 1)
                    if at == RED + 1:
                        reduced_query(w)
                    if at == SCORE:
                        dve.wait_ge(result_copied, copied("query", w))
                        if w == 0:
                            dve.wait_ge(kv_bias_copied, 1)
                        link(V.tensor_tensor(work[:], q_sb[:, w % 2, :], kv_bias[:, 0:C], ALU.mult))
                        settle()
                        link(V.tensor_reduce(qbk[:], work[:].rearrange("p (h d) -> p h d", h=H8), AX_X, ALU.add))
                        score_products(w, 0)
                    if at == SCORE + 1:
                        score_products(w, 1)
                    if at == SCORE + 2:
                        score_products(w, 2)
                        softmax_shift(w)
                    if at == WEIGH:
                        softmax_weights(w)
                        weigh_values(w, 0)
                    if at == WEIGH + 1:
                        weigh_values(w, 1)
                    if at == SUM:
                        sum_values(w, 0)
                    if at == SUM + 1:
                        sum_values(w, 1)
                    if at == LOCAL:
                        dve.wait_ge(result_copied, copied("proj", w))
                        dve.wait_ge(redp_done, w + 1)
                        V.tensor_tensor(local[:, w % 2, :], res[:, 0, :], redp[:, w % 2, :], ALU.add).then_inc(local_done, 1)
                        dve.wait_ge(local_done, w + 1)
                        layer_norm_stats(local[:, w % 2, :], w)
                    if at == LOCAL + 1:
                        dve.wait_ge(rstd_done, POW_ORDER.index(("local", w)) + 1)
                        layer_norm(kvln[:], local[:, w % 2, :], w, row["gkv_g"][:], row["gkv_b"][:], kvln_done)
                    if at == TOKEN:
                        dve.wait_ge(result_copied, copied("mod", w))
                        V.tensor_tensor(hs[:, w, :], res[:, 1, :], row["mod_b"][:], ALU.add).then_inc(token_done, 1)
                    if at == GSCORE:
                        dve.wait_ge(result_copied, copied("gkv", w))
                        link(V.tensor_tensor(work[:], gkv_sb[:, w, 0:C], gq_sb[:], ALU.mult))
                        settle()
                        link(V.tensor_reduce(gscore[:, 0, w, :], work[:].rearrange("p (h d) -> p h d", h=H8), AX_X,
                                             ALU.add))
                    if at == QKVB:
                        take_qkv(w)
                if s == GATT:
                    settle()
                    link(V.tensor_reduce(gstat[:, 0, :], gscore[:, 0].rearrange("p n h -> p h n"), AX_X, ALU.max))
                    settle()
                    V.tensor_tensor(gscore[:, 1], gscore[:, 0], gstat[:, 0, :].unsqueeze(1).broadcast_to([P, NW, H8]),
                                    ALU.subtract).then_inc(shifted, 1)
                    dve.wait_ge(exp_done, NW + 1)
                    link(V.tensor_reduce(gstat[:, 1, :], gscore[:, 2].rearrange("p n h -> p h n"), AX_X, ALU.add))
                    settle()
                    link(V.reciprocal(gstat[:, 2, :], gstat[:, 1, :]))
                    settle()
                    V.tensor_tensor(gprob[:], gscore[:, 2], gstat[:, 2, :].unsqueeze(1).broadcast_to([P, NW, H8]),
                                    ALU.mult).then_inc(probs_done, 1)
                    dve.wait_ge(probs_done, NW + 1)
                    link(V.tensor_tensor(heads(prod[:, 0:NW, :]), heads(gkv_sb[:, :, C:2 * C]),
                                         gprob[:].unsqueeze(3).broadcast_to([P, NW, H8, DH]), ALU.mult))
                    settle()
                    V.tensor_reduce(gagg[:], prod[:, 0:NW, :].rearrange("p n c -> p c n"), AX_X, ALU.add
                                    ).then_inc(gagg_done, 1)
                if s == CLASSO + 2:
                    dve.wait_ge(result_copied, copied("gproj", 0))
                    link(V.tensor_tensor(work[:], res[:, 2, :], row["gproj_b"][:], ALU.add))
                    settle()
                    V.tensor_tensor(hs[:, NW, :], work[:], row["class"][:], ALU.add).then_inc(token_done, 1)
                if s == CLASSO + 5:
                    take_qkv(NW)

            for n in range(2 * T):
                half, i = divmod(n, T)
                if n == 0:
                    dve.wait_ge(qkv_done, T)
                if n == T:
                    settle()
                    dve.wait_ge(pool_prod_used, POOL_ROWS)
                    for k in range(T):
                        link(V.scalar_tensor_tensor(out=att_s[:, 0, k], in0=att_s[:, 0, k], scalar=DK ** -0.5,
                                                    in1=rel_rows[:, :, k:k + T], op0=ALU.mult, op1=ALU.add))
                    settle()
                    link(V.tensor_reduce(att_m[:, 0], att_s[:, 0], AX_X, ALU.max))
                    settle()
                    over_keys = [P, T, H16, T]
                    V.tensor_tensor(att_s[:, 1], att_s[:, 0], att_m[:, 0].unsqueeze(3).broadcast_to(over_keys),
                                    ALU.subtract).then_inc(shifted, 1)
                    dve.wait_ge(exp_done, NW + 2)
                    link(V.tensor_reduce(att_m[:, 1], att_s[:, 2], AX_X, ALU.add))
                    settle()
                    link(V.reciprocal(att_m[:, 2], att_m[:, 1]))
                    settle()
                    V.tensor_tensor(att_s[:, 1], att_s[:, 2], att_m[:, 2].unsqueeze(3).broadcast_to(over_keys),
                                    ALU.mult).then_inc(probs_done, 1)
                    dve.wait_ge(probs_done, NW + 2)
                row_i = DVE_ORDER[i]
                if row_i < POOL_ROWS:
                    dve.wait_ge(pool_prod_done, POOL_ROWS * half + row_i + 1)
                    b = 1
                else:
                    settle()
                    link(attention_product(V, half, row_i, 0))
                    settle()
                    b = 0
                if half == 0:
                    ins = V.tensor_reduce(att_s[:, 0, row_i].rearrange("p h j -> p j h"),
                                          att_prod[:, b].rearrange("p j (h d) -> p j h d", h=H16), AX_X, ALU.add)
                else:
                    ins = V.tensor_reduce(att_o[:, row_i, :], att_prod[:, b].rearrange("p j c -> p c j"), AX_X, ALU.add)
                if b == 1:
                    ins.then_inc(pool_prod_used, 1)
                else:
                    link(ins)
            settle()
            dve.wait_ge(pool_prod_used, 2 * POOL_ROWS)
            link(V.tensor_tensor(att_o[:], att_o[:], hs[:], ALU.add))
            settle()

            def normalise(src, dst, which, done):
                for i in range(T):
                    link(V.bn_stats(bn[:, i, :], src[:, i, :]))
                settle()
                for i in range(T):
                    link(V.bn_aggr(mv[:, i, :], bn[:, i, :]))
                settle()
                V.tensor_scalar(ve[:], mv[:, :, 1], EPS, None, ALU.add).then_inc(var_done, 1)
                dve.wait_ge(rstd_done, POW_ORDER.index(which) + 1)
                for i in range(T):
                    V.tensor_scalar(dst[:, i, :], src[:, i, :], mv[:, i, 0:1], rs[:, i:i + 1], ALU.subtract, ALU.mult
                                    ).then_inc(done, 1)

            normalise(att_o, h1, "attention", h1_done)
            dve.wait_ge(h1_done, T)
            for b in range(BANKS):
                cut = slice(2 * b, min(2 * b + 2, T))
                V.tensor_copy(acc[:, cut, :], h1[:, cut, :]).then_inc(acc_ready, 1)
            dve.wait_ge(xt_copied, T)
            V.tensor_copy(xt_hi[:], xt_f[:]).then_inc(xt_split, 1)
            dve.wait_ge(xt_split, 1)
            V.tensor_tensor(xt_lo[:], xt_f[:], xt_hi[:].bitcast(F32), ALU.subtract).then_inc(xt_split, 1)

            dve.wait_ge(gate_scored, 1)
            per_token = [P, T, E]
            link(V.tensor_tensor(g8[:, 0], psum[:, GATE_BANK, 0:T * E].rearrange("p (t e) -> p t e", e=E),
                                 row["bg"][:].unsqueeze(1).broadcast_to(per_token), ALU.add))
            settle()
            link(V.tensor_reduce(gt[:, 0], g8[:, 0], AX_X, ALU.max))
            settle()
            V.tensor_tensor(g8[:, 1], g8[:, 0], gt[:, 0].unsqueeze(2).broadcast_to(per_token), ALU.subtract
                            ).then_inc(shifted, 1)
            dve.wait_ge(exp_done, NW + 3)
            link(V.tensor_reduce(gt[:, 1], g8[:, 2], AX_X, ALU.add))
            settle()
            link(V.reciprocal(gt[:, 2], gt[:, 1]))
            settle()
            link(V.tensor_tensor(g8[:, 3], g8[:, 2], gt[:, 2].unsqueeze(2).broadcast_to(per_token), ALU.mult))
            settle()
            for i in range(T):
                link(V.max(g8[:, 4, i], g8[:, 3, i]))
            settle()
            for i in range(T):
                link(V.max_index(top_at[:, i], g8[:, 4, i], g8[:, 3, i]))
            V.tensor_tensor(gt[:, 5], g8[:, 4, :, 1], g8[:, 4, :, 0], ALU.subtract).then_inc(shifted, 1)
            settle()
            link(V.tensor_copy(gt[:, 3:5], top_at[:, :, 0:2].rearrange("p t k -> p k t")))
            dve.wait_ge(exp_done, NW + 4)
            link(V.tensor_scalar(gt[:, 7], gt[:, 6], 1.0, None, ALU.add))
            settle()
            link(V.reciprocal(gt[:, 8], gt[:, 7]))
            settle()
            link(V.tensor_tensor(gt[:, 9], gt[:, 6], gt[:, 8], ALU.mult))
            settle()
            dve.wait_ge(consts_made, 2)
            for i in range(T):
                for k in range(2):
                    link(V.tensor_scalar(g8[:, 5 * (1 - k), i], iota8[:], gt[:, 3 + k, i:i + 1], gt[:, 8 + k, i:i + 1],
                                         ALU.is_equal, ALU.mult))
            settle()
            V.tensor_tensor(gates[:], g8[:, 0], g8[:, 5], ALU.add).then_inc(gates_done, 1)
            dve.wait_ge(gates_done, 1)

            def split_hidden(e, j, first=False):
                dve.wait_ge(relu_done, J * e + j + 1)
                if j != 1 and not (j == 0 and first):
                    dve.wait_ge(hidden_used, J * e + j - 1)
                V.tensor_copy(h_hi[:, j % 2, :], h_f[:, j % 2, :]).then_inc(h_hi_done, 1)
                dve.wait_ge(h_hi_done, J * e + j + 1)
                V.tensor_tensor(h_lo[:, j % 2, :], h_f[:, j % 2, :], h_hi[:, j % 2, :].bitcast(F32), ALU.subtract
                                ).then_inc(h_split, 1)

            def split_low(e, u, j):
                raw, hi, lo = piece(j)
                dve.wait_ge(w_hi_done, J * e + j + 1)
                V.tensor_tensor(lo(u), raw, hi(u).bitcast(F32), ALU.subtract).then_inc(w_lo_done, 1)

            def add_expert(e):
                dve.wait_ge(hidden_used, J * e + J)
                dve.wait_ge(acc_ready, BANKS * e + BANKS)
                for i in range(T):
                    last = V.scalar_tensor_tensor(out=acc[:, i, :],
                                                  in0=psum[:, EXPERT_BANK + i // 2, (i % 2) * C:(i % 2 + 1) * C],
                                                  scalar=gates[:, i, bass.ds(e, 1)], in1=acc[:, i, :],
                                                  op0=ALU.mult, op1=ALU.add)
                    if i % 2 == 1 or i == T - 1:
                        last.then_inc(acc_ready, 1)

            def beside(j):
                if j in (2, 4):
                    dve.wait_ge(gates_turned, j // 2)
                    a, b = (0, 4) if j == 2 else (4, T)
                    V.tensor_copy(gates_t[:, a:b, :], psum[0:E, GATE_BANK, 0:(b - a) * P].rearrange(
                        "e (i t) -> e i t", t=P)).then_inc(gates_t_copied, 1)
                if j in (6, 7, 8):
                    n = j - 6
                    a, b = 2 * n, min(2 * n + 2, T)
                    dve.wait_ge(gate_bias_done, n + 1)
                    dve.wait_ge(acc_ready, BANKS * (E - 2) + BANKS)
                    V.tensor_tensor(acc[:, a:b, :], psum[:, GATE_BANK, 0:(b - a) * C].rearrange("p (i c) -> p i c", c=C),
                                    acc[:, a:b, :], ALU.add).then_inc(gate_bias_used, 1)
                    if j == J:
                        dve.wait_ge(gate_bias_used, BANKS)

            def expert(e, u, more=True, beside=lambda j: None):
                if more:
                    split_low(e + 1, 1 - u, 0)
                for j in range(1, J):
                    split_hidden(e, j)
                    if more:
                        split_low(e + 1, 1 - u, j)
                    beside(j)
                if more:
                    split_hidden(e + 1, 0)
                beside(J)
                add_expert(e)

            split_hidden(0, 0, first=True)
            with dve.Fori(0, E // 2 - 1) as i:
                expert(2 * i, 0)
                expert(2 * i + 1, 1)
            expert(E - 2, 0, beside=beside)
            expert(E - 1, 1, more=False)
            dve.wait_ge(acc_ready, BANKS * E + BANKS)
            normalise(acc, fin, "output", fin_done)


_INS = [
    "x", "L0_tok_conv_w", "L0_tok_class_emb", "L0_tok_la_ln_q_g", "L0_tok_la_ln_q_b", "L0_tok_la_wq",
    "L0_tok_la_ln_kv_g", "L0_tok_la_ln_kv_b", "L0_tok_la_wkv", "L0_tok_la_proj_w", "L0_tok_la_proj_b",
    "L0_tok_ga_ln_q_g", "L0_tok_ga_ln_q_b", "L0_tok_ga_wq", "L0_tok_ga_ln_kv_g", "L0_tok_ga_ln_kv_b",
    "L0_tok_ga_wkv", "L0_tok_ga_proj_w", "L0_tok_ga_proj_b", "L0_tok_mod_w", "L0_tok_mod_b",
    "L0_attn_Wq", "L0_attn_bq", "L0_attn_Wk", "L0_attn_bk", "L0_attn_Wv", "L0_attn_bv", "L0_attn_rel_emb",
    "L0_ffn_W1", "L0_ffn_b1", "L0_ffn_W2", "L0_ffn_b2", "L0_ffn_Wg", "L0_ffn_bg",
]
_OUT_SHAPE = (128, 5, 256)


def kernel(**inputs):
    import numpy as _np
    import concourse.bacc as _bacc
    from concourse import mybir as _mybir
    from concourse.bass_utils import run_bass_kernel_spmd as _run

    nc = _bacc.Bacc("TRN2", target_bir_lowering=False, num_devices=1,
                    dynamic_dma_scratch_size=1024)
    arrays, args = {}, []
    for name in _INS:
        a = _np.ascontiguousarray(inputs[name])
        arrays[f"in_{name}_dram"] = a
        args.append(nc.dram_tensor(f"in_{name}_dram", a.shape, _mybir.dt.from_np(a.dtype), kind="ExternalInput").ap())
    args.append(nc.dram_tensor("out_0_dram", _OUT_SHAPE, _mybir.dt.float32, kind="ExternalOutput").ap())
    build(nc, *args)
    r = _run(nc, [arrays], core_ids=[0])
    return r.results[0]["out_0_dram"]
```

```python
from contextlib import ExitStack

import concourse.bass as bass
from concourse import mybir

ALU = mybir.AluOpType
ACT = mybir.ActivationFunctionType
F32 = mybir.dt.float32
F32R = mybir.dt.float32r
U32 = mybir.dt.uint32
AX_X = mybir.AxisListType.X

EPS = 1e-5


def build(nc, x, conv_w, class_emb, q_g, q_b, wq, kv_g, kv_b, wkv, proj_w, proj_b, gq_g, gq_b, gwq,
          gkv_g, gkv_b, gwkv, gproj_w, gproj_b, mod_w, mod_b, aWq, abq, aWk, abk, aWv, abv, rel,
          W1, b1, W2, b2, Wg, bg, out):
    B, CIN, IMG, _ = x.shape
    C = conv_w.shape[0]
    PS = conv_w.shape[2]
    P = 128
    KC = C // P
    GRID = IMG // PS
    CS = 3
    NW = (GRID // CS) ** 2
    NP = CS * CS
    NT = NW * NP
    H8 = 8
    DH = C // H8
    T = NW + 1
    H16 = rel.shape[0]
    DK = C // H16
    E, _, HID = W1.shape
    J = HID // P
    assert B == P and C == 256 and GRID == 2 * CS and NW == 4 and E == 8

    LINES = CIN * PS
    CL = P // PS
    K = CL * PS
    NK = -(-LINES // CL)
    START = [min(k * CL, LINES - CL) for k in range(NK)]
    OVER = ((NK - 1) * CL - START[-1]) * PS
    CW = C + 2
    GROUPS = [(0, 3), (3, NK)]
    TOK = T * P
    HALF = TOK // 2
    KV_LAG = 2
    CEN_RING = KV_LAG + 1
    POOL_QUERIES = (1, 0)
    DVE_QUERIES = (2, 3, 4)
    PE_SUMS = (2, 1, 0)
    DVE_SUMS = (3, 4)
    XT_ORDER = (1, 2, 3, 4, 0)
    BANKS = -(-T // 2)

    with ExitStack() as ctx:
        def sb(name, shape, dt=F32):
            return ctx.enter_context(nc.sbuf_tensor(name, shape, dt))

        def sem(name):
            return ctx.enter_context(nc.semaphore(name))

        psum = ctx.enter_context(nc.psum_tensor("psum", [P, 8, 512], F32))
        PATCH_BANK = (0, 1, 2)
        CONV_BANK = (3, 4)
        TURN_BANK = 5
        RESULT_BANK = (6, 7)
        XT_BANK = (4, 5, 6)
        HIDDEN_BANK = (0, 2)
        EXPERT_BANK = 4
        GATE_BANK = 7

        ident = sb("ident", [P, P])
        minus_half = sb("minus_half", [P, 16])
        iota8i = sb("iota8i", [P, E], mybir.dt.int32)
        iota8 = sb("iota8", [P, E])
        wg_sb = sb("wg_sb", [P, KC, E])
        ones = sb("ones", [P, 1])
        qkv_w = sb("qkv_w", [P, KC, 3 * C])
        rows_in = sb("rows_in", [E * J + 2 * KC, P])
        cols = sb("cols", [P, E * J + 2 * KC])
        b1_cols = cols[:, 0:E * J].rearrange("p (e j) -> p e j", e=E)
        kvg_cols = cols[:, E * J:E * J + KC]
        kvb_cols = cols[:, E * J + KC:E * J + 2 * KC]
        row = {name: sb("row_" + name, [P, width]) for name, width in (
            ("q_g", C), ("q_b", C), ("proj_b", C), ("gkv_g", C), ("gkv_b", C), ("gproj_b", C), ("mod_b", C),
            ("class", C), ("qkv_b", 3 * C), ("bg", E))}
        rel_rows = sb("rel_rows", [P, H16, 2 * T - 1])
        conv_mean = sb("conv_mean", [P, 2, NK])
        sumsq = sb("sumsq", [P, NW, NP + 1])
        var_eps = sb("var_eps", [P, NW, NP + 1])
        rstd = sb("rstd", [P, NW, NP + 1])
        mu9 = sb("mu9", [P, NW])
        qbk = sb("qbk", [P, H8])
        stat8 = sb("stat8", [P, 3, H8])
        bn = sb("bn", [P, T, 6])
        mv = sb("mv", [P, T, 2])
        ve = sb("ve", [P, T])
        rs = sb("rs", [P, T])
        gprob = sb("gprob", [P, NW, H8])
        gscore = sb("gscore", [P, 3, NW, H8])
        gstat = sb("gstat", [P, 3, H8])
        hs = sb("hs", [P, T, C])
        aq = sb("aq", [P, T, C])
        akv = sb("akv", [P, T, 2 * C])

        att_raw = sb("att_raw", [P, T, H16, T])

        tokenizer_memory = ExitStack()

        def sbt(name, shape, dt=F32):
            return tokenizer_memory.enter_context(nc.sbuf_tensor(name, shape, dt))

        lines = sbt("lines", [P, CS, LINES, IMG])
        patches = sbt("patches", [P, 3, LINES * PS])
        conv_hi = sbt("conv_hi", [P, NK, CW], F32R)
        conv_lo = sbt("conv_lo", [P, NK, CW], F32R)
        patch_hi = sbt("patch_hi", [P, 2, NK, P], F32R)
        patch_lo = sbt("patch_lo", [P, 2, NK, P], F32R)
        cen = sbt("cen", [P, CEN_RING, CW])
        wkv_hi = sbt("wkv_hi", [P, KC, 2 * C], F32R)
        wkv_lo = sbt("wkv_lo", [P, KC, 2 * C], F32R)
        turn_hi = sbt("turn_hi", [P, 2, C], F32R)
        turn_lo = sbt("turn_lo", [P, 2, C], F32R)
        kv = sbt("kv", [P, 2, NP, 2 * C])
        wq_sb = sbt("wq_sb", [P, KC, C])
        proj_sb = sbt("proj_sb", [P, KC, C])
        gwkv_sb = sbt("gwkv_sb", [P, KC, 2 * C])
        gproj_sb = sbt("gproj_sb", [P, KC, C])
        mod_sb = sbt("mod_sb", [P, KC, C])
        kv_bias = sbt("kv_bias", [P, 2 * C])
        turn_f = sbt("turn_f", [P, 3, C])
        res = sbt("res", [P, 3, C])
        qkv_res = sbt("qkv_res", [P, 3 * C])
        q_sb = sbt("q_sb", [P, 2, C])
        gq_sb = sbt("gq_sb", [P, C])
        redsum = sbt("redsum", [P, 2, CW])
        redp = sbt("redp", [P, 2, C])
        redln = sbt("redln", [P, C])
        score = sbt("score", [P, 3, NP, H8])
        probe = sbt("probe", [P, 2, NP, H8])
        agg = sbt("agg", [P, C])
        kvln = sbt("kvln", [P, C])
        gagg = sbt("gagg", [P, C])
        junk = sbt("junk", [P, C])
        work = sbt("work", [P, C])
        start_memory = ExitStack()

        def sbs(name, shape, dt=F32):
            return start_memory.enter_context(nc.sbuf_tensor(name, shape, dt))

        conv_raw = sbs("conv_raw", [P, KC, LINES * PS])
        wkv_raw = sbs("wkv_raw", [P, KC, 2 * C])
        kvb_wide = sbs("kvb_wide", [P, KC, P])
        gwq_sb = sbs("gwq_sb", [P, KC, C])
        row["gq_g"] = sbs("row_gq_g", [P, C])
        row["gq_b"] = sbs("row_gq_b", [P, C])
        class_ln = sbs("class_ln", [P, C])
        start_memory.close()
        prod = sbt("prod", [P, NP, C])
        gkv_sb = sbt("gkv_sb", [P, NW, 2 * C])
        local = sbt("local", [P, 2, C])
        tokenizer_memory.close()

        w1_raw = sb("w1_raw", [P, KC, HID])
        w2_raw = sb("w2_raw", [P, J, C])
        w1_hi, w1_lo, w2_hi, w2_lo = [], [], [], []
        for u in range(2):
            for parts, name, shape in ((w1_hi, "w1_hi", [P, KC, HID]), (w1_lo, "w1_lo", [P, KC, HID]),
                                       (w2_hi, "w2_hi", [P, J, C]), (w2_lo, "w2_lo", [P, J, C])):
                parts.append(sb(f"{name}{u}", shape, F32R))
        att_prod = sb("att_prod", [P, T, T, C])
        att_s = sb("att_s", [P, 3, T, H16, T])
        att_m = sb("att_m", [P, 3, T, H16])
        att_o = sb("att_o", [P, len(DVE_SUMS), C])
        h1 = sb("h1", [P, T, C])
        xt_f = sb("xt_f", [P, KC, TOK])
        xt_hi = sb("xt_hi", [P, KC, TOK], F32R)
        xt_lo = sb("xt_lo", [P, KC, TOK], F32R)
        g8 = sb("g8", [P, 6, T, E])
        gt = sb("gt", [P, 10, T])
        top_at = sb("top_at", [P, T, E], U32)
        gates = sb("gates", [P, T, E])
        gates_t = sb("gates_t", [T * E, P])
        b2_wide = sb("b2_wide", [T * E, T, C])
        gate_sums = sb("gate_sums", [P, E])
        order = sb("order", [1, 4, E])
        table = sb("table", [1, E], mybir.dt.int32)
        acc = sb("acc", [P, T, C])
        h_f = sb("h_f", [P, 2, TOK])
        h_hi = sb("h_hi", [P, 2, TOK], F32R)
        h_lo = sb("h_lo", [P, 2, TOK], F32R)
        fin = sb("fin", [P, T, C])

        first_loaded = sem("first_loaded")
        early_loaded = sem("early_loaded")
        wkv_loaded = sem("wkv_loaded")
        late_loaded = sem("late_loaded")
        lines_loaded = [sem(f"lines_loaded_{r}") for r in range(CS)]
        w1_loaded = sem("w1_loaded")
        w2_loaded = sem("w2_loaded")
        stored = sem("stored")
        ident_made = sem("ident_made")
        consts_made = sem("consts_made")
        conv_w_turned = sem("conv_w_turned")
        conv_w_centred = sem("conv_w_centred")
        conv_w_split = sem("conv_w_split")
        conv_mean_made = sem("conv_mean_made")
        conv_hi_done = sem("conv_hi_done")
        cols_turned = sem("cols_turned")
        cols_copied = sem("cols_copied")
        kvb_widened = sem("kvb_widened")
        kv_bias_made = sem("kv_bias_made")
        kv_bias_copied = sem("kv_bias_copied")
        wkv_split = sem("wkv_split")
        patches_gathered = sem("patches_gathered")
        patch_turned = sem("patch_turned")
        patch_hi_done = sem("patch_hi_done")
        patch_lo_done = sem("patch_lo_done")
        conv_done = sem("conv_done")
        cen_copied = sem("cen_copied")
        sumsq_done = sem("sumsq_done")
        red_summed = sem("red_summed")
        turned = sem("turned")
        turn_copied = sem("turn_copied")
        turn_lo_done = sem("turn_lo_done")
        projected = sem("projected")
        result_copied = sem("result_copied")
        var_done = sem("var_done")
        rstd_done = sem("rstd_done")
        redln_done = sem("redln_done")
        redp_done = sem("redp_done")
        pool_scored = sem("pool_scored")
        pool_weighed = sem("pool_weighed")
        shifted = sem("shifted")
        exp_done = sem("exp_done")
        probs_done = sem("probs_done")
        agg_done = sem("agg_done")
        local_done = sem("local_done")
        kvln_done = sem("kvln_done")
        class_ln_done = sem("class_ln_done")
        gagg_done = sem("gagg_done")
        token_done = sem("token_done")
        qkv_done = sem("qkv_done")
        pool_paired = sem("pool_paired")
        pairs_scored = sem("pairs_scored")
        pool_valued = sem("pool_valued")
        dve_valued = sem("dve_valued")
        values_summed = sem("values_summed")
        h1_done = sem("h1_done")
        xt_copied = sem("xt_copied")
        xt_turned = sem("xt_turned")
        xt_split = sem("xt_split")
        gate_scored = sem("gate_scored")
        gates_done = sem("gates_done")
        gates_turned = sem("gates_turned")
        gates_t_copied = sem("gates_t_copied")
        gates_summed = sem("gates_summed")
        table_made = sem("table_made")
        b2_cleared = sem("b2_cleared")
        b2_loaded = sem("b2_loaded")
        gate_bias_done = sem("gate_bias_done")
        gate_bias_used = sem("gate_bias_used")
        w_hi_done = sem("w_hi_done")
        w_lo_done = sem("w_lo_done")
        hidden_done = sem("hidden_done")
        relu_done = sem("relu_done")
        h_hi_done = sem("h_hi_done")
        h_split = sem("h_split")
        hidden_used = sem("hidden_used")
        acc_ready = sem("acc_ready")
        fin_done = sem("fin_done")
        dve_chain = sem("dve_chain")
        pool_chain = sem("pool_chain")

        RED, QUERY, SCORE, WEIGH, SUM, PROJ, LOCAL, MOD, GKV, TOKEN, GSCORE, QKV, QKVB = (
            10, 11, 13, 16, 18, 21, 23, 24, 25, 26, 27, 27, 29)
        CLASSQ = 6
        GATT = NP * (NW - 1) + GSCORE + 1
        CLASSO = GATT + 2
        SPLIT0 = NT + 2
        STEPS = CLASSO + 6

        def extras(s):
            found = [(kind, w) for w in range(NW) for kind, at in
                     (("query", QUERY), ("proj", PROJ), ("mod", MOD), ("gkv", GKV), ("qkv", QKV))
                     if s == NP * w + at]
            if s == CLASSQ:
                found.append(("gquery", 0))
            if s == CLASSO:
                found.append(("gproj", 0))
            if s == CLASSO + 3:
                found.append(("qkv", NW))
            return found

        turn_order = []
        result_order = []
        for s in range(STEPS):
            if 0 <= s - KV_LAG < NT:
                turn_order.append(("kv", s - KV_LAG))
                result_order.append(("kv", s - KV_LAG, 0))
            for kind, w in extras(s - 1):
                result_order.append((kind, w, 0))
                if kind == "qkv":
                    result_order.append((kind, w, 1))
            turn_order += extras(s)
        kv_turns = [sum(k == "kv" for k, _ in turn_order[:i]) for i in range(len(turn_order) + 1)]
        plain_turns = [i - n for i, n in enumerate(kv_turns)]

        def copied(kind, w, part=0):
            return result_order.index((kind, w, part)) + 1

        def slot_of(t):
            w, n = divmod(t, NP)
            return n // CS, ((w % 2) * CS + n % CS) * PS

        VAR_ORDER = [found for s in range(STEPS) for found in
                     [("class", 0)] * (s == CLASSQ - 1)
                     + [("red", w) for w in range(NW) if s == NP * w + RED]
                     + [("local", w) for w in range(NW) if s == NP * w + LOCAL]]
        VAR_ORDER += ["attention", "attention_last", "output"]
        FIRST = (E - 2, E - 1)
        OTHERS = E - 2
        COUNT = OTHERS
        LATE = 25
        POOL_PAIRS = 3

        def pairs_step(w):
            return NP * w + QKVB + 1 if w < NW else CLASSO + 5

        def pair_products(eng, w, own, a, b):
            if own:
                return eng.tensor_tensor(prod[:, 0:w + 1, :], akv[:, T - 1 - w:T, 0:C],
                                         aq[:, w, :].unsqueeze(1).broadcast_to([P, w + 1, C]), ALU.mult)
            return eng.tensor_tensor(prod[:, w + 1 + a:w + 1 + b, :], aq[:, a:b, :],
                                     akv[:, T - 1 - w, 0:C].unsqueeze(1).broadcast_to([P, b - a, C]), ALU.mult)

        def weigh_tokens(eng, i):
            return eng.tensor_tensor(att_prod[:, i].rearrange("p j (h d) -> p j h d", h=H16),
                                     akv[:, :, C:2 * C].rearrange("p j (h d) -> p j h d", h=H16),
                                     att_s[:, 1, i].rearrange("p h j -> p j h").unsqueeze(3).broadcast_to(
                                         [P, T, H16, DK]), ALU.mult)

        block = ctx.enter_context(nc.Block())

        @block.sync
        def _(sp):
            rows_of = x.rearrange("b c (r k) x -> r b c (k x)", k=PS)

            def load_lines(hy, r):
                sp.dma_start(lines[:, r].rearrange("p (c k) x -> p c (k x)", c=CIN),
                             rows_of[hy * CS + r]).then_inc(lines_loaded[r], 16)

            def load(dst, src, which):
                sp.dma_start(dst, src).then_inc(which, 16)

            load(conv_raw[:], conv_w.rearrange("(h o) c y x -> o h (c y x)", o=P), first_loaded)
            load(rows_in[0:E * J], b1.rearrange("e (j p) -> (e j) p", p=P), early_loaded)
            load(rows_in[E * J:E * J + KC], kv_g.rearrange("(k p) -> k p", p=P), early_loaded)
            load(rows_in[E * J + KC:E * J + 2 * KC], kv_b.rearrange("(k p) -> k p", p=P), early_loaded)
            load_lines(0, 0)
            load(wkv_raw[:], wkv.rearrange("(k p) n -> p k n", p=P), wkv_loaded)
            load_lines(0, 1)
            load_lines(0, 2)
            for name, src in (("class", class_emb), ("gq_g", gq_g), ("gq_b", gq_b), ("q_g", q_g), ("q_b", q_b),
                              ("proj_b", proj_b), ("gkv_g", gkv_g), ("gkv_b", gkv_b), ("gproj_b", gproj_b),
                              ("mod_b", mod_b), ("bg", bg)):
                load(row[name][:], src.partition_broadcast(P), late_loaded)
            for dst, src in ((gwq_sb[:], gwq), (wq_sb[:], wq), (proj_sb[:], proj_w), (gwkv_sb[:], gwkv),
                             (mod_sb[:], mod_w), (gproj_sb[:], gproj_w), (qkv_w[:, :, 0:C], aWq),
                             (qkv_w[:, :, C:2 * C], aWk), (qkv_w[:, :, 2 * C:3 * C], aWv), (wg_sb[:], Wg)):
                load(dst, src.rearrange("(k p) n -> p k n", p=P), late_loaded)
            for n, src in enumerate((abq, abk, abv)):
                load(row["qkv_b"][:, n * C:(n + 1) * C], src.partition_broadcast(P), late_loaded)
            load(rel_rows[:], rel[:, 0:2 * T - 1].partition_broadcast(P), late_loaded)
            for r in range(CS):
                sp.wait_ge(patches_gathered, NP + CS * r + CS)
                load_lines(1, r)
            sp.wait_ge(patches_gathered, NT)
            sp.dma_start(w1_raw[:], W1[FIRST[0]].rearrange("(k p) h -> p k h", p=P)).then_inc(w1_loaded, 16)
            sp.dma_start(w2_raw[:], W2[FIRST[0]].rearrange("(j p) c -> p j c", p=P)).then_inc(w2_loaded, 16)
            w1_rows = W1.rearrange("e (k p) h -> e p k h", p=P)
            w2_rows = W2.rearrange("e (j p) c -> e p j c", p=P)

            def load_expert(k, e):
                sp.wait_ge(w_lo_done, J * k - J // 2)
                sp.dma_start(w1_raw[:], w1_rows[bass.ds(e, 1)].rearrange("e p k h -> (e p) k h")
                             ).then_inc(w1_loaded, 16)
                sp.wait_ge(w_lo_done, J * k)
                sp.dma_start(w2_raw[:], w2_rows[bass.ds(e, 1)].rearrange("e p j c -> (e p) j c")
                             ).then_inc(w2_loaded, 16)

            load_expert(1, FIRST[1])
            sp.wait_ge(b2_cleared, 1)
            for i in range(T):
                sp.dma_start(b2_wide[i * E:(i + 1) * E, i, :], b2).then_inc(b2_loaded, 16)
            sp.wait_ge(table_made, 1)
            pairs = sp.value_load(table[0:1, COUNT:COUNT + 1], min_val=2, max_val=OTHERS // 2)
            with sp.Fori(0, 2 * pairs) as i:
                load_expert(i + 2, sp.value_load(table[0:1, bass.ds(i, 1)], min_val=0, max_val=OTHERS - 1))
            for i in range(T):
                sp.wait_ge(fin_done, i + 1)
                sp.dma_start(out[:, i, :], fin[:, i, :]).then_inc(stored, 16)
            sp.wait_ge(stored, 16 * T)

        def piece(j):
            if j < J // 2:
                k, h = divmod(j, J // 2 // KC)
                wide = HID * KC // (J // 2)
                cut = slice(h * wide, (h + 1) * wide)
                return w1_raw[:, k, cut], lambda u: w1_hi[u][:, k, cut], lambda u: w1_lo[u][:, k, cut]
            a = (j - J // 2) * 2
            return w2_raw[:, a:a + 2, :], lambda u: w2_hi[u][:, a:a + 2, :], lambda u: w2_lo[u][:, a:a + 2, :]

        @block.scalar
        def _(act):
            act.wait_ge(cols_turned, 1)
            nc.scalar.activation(cols[:], psum[:, RESULT_BANK[0], 0:E * J + 2 * KC], ACT.Copy).then_inc(cols_copied, 1)
            act.wait_ge(conv_mean_made, 1)
            for k in range(NK):
                nc.scalar.activation(conv_hi[0:K, k, 0:C], psum[0:K, k, 0:C], ACT.Identity,
                                     bias=conv_mean[0:K, 1, k:k + 1]).then_inc(conv_hi_done, 1)

            def patch_highs(t):
                if t >= 2:
                    act.wait_ge(conv_done, t - 1)
                for g, (a, b) in enumerate(GROUPS):
                    act.wait_ge(patch_turned, 2 * t + g + 1)
                    nc.scalar.activation(patch_hi[0:K, t % 2, a:b, :],
                                         psum[0:K, PATCH_BANK[(2 * t + g) % 3], 0:(b - a) * P],
                                         ACT.Copy).then_inc(patch_hi_done, 1)

            def copy_centred(t):
                act.wait_ge(conv_done, t + 1)
                if t >= CEN_RING:
                    act.wait_ge(turned, turn_order.index(("kv", t - CEN_RING)) + 1)
                    act.wait_ge(sumsq_done, t - CEN_RING + 1)
                    act.wait_ge(red_summed, t - CEN_RING + 1)
                nc.scalar.activation(cen[:, t % CEN_RING, :], psum[:, CONV_BANK[t % 2], 0:CW], ACT.Copy).then_inc(cen_copied, 1)

            def copy_turned(item):
                i = turn_order.index(item)
                act.wait_ge(turned, i + 1)
                if item[0] == "kv":
                    dst = turn_hi[:, item[1] % 2, :]
                else:
                    dst = turn_f[:, plain_turns[i] % 3, :]
                nc.scalar.activation(dst, psum[:, TURN_BANK, 0:C], ACT.Copy).then_inc(turn_copied, 1)

            def copy_result(kind, w, part):
                i = result_order.index((kind, w, part))
                act.wait_ge(projected, i + 1)
                src = psum[:, RESULT_BANK[i % 2], :]
                if kind == "kv":
                    v, n = divmod(w, NP)
                    if v >= 2 and n == 0:
                        act.wait_ge(agg_done, v - 1)
                        act.wait_ge(pool_weighed, v - 1)
                    nc.scalar.activation(kv[:, v % 2, n, :], src, ACT.Copy).then_inc(result_copied, 1)
                elif kind == "query":
                    nc.scalar.activation(q_sb[:, w % 2, :], src[:, 0:C], ACT.Copy, scale=C ** -0.5
                                         ).then_inc(result_copied, 1)
                elif kind == "gquery":
                    nc.scalar.activation(gq_sb[:], src[:, 0:C], ACT.Copy, scale=C ** -0.5).then_inc(result_copied, 1)
                elif kind == "gkv":
                    nc.scalar.activation(gkv_sb[:, w, :], src, ACT.Copy).then_inc(result_copied, 1)
                elif kind == "qkv":
                    dst = qkv_res[:, 0:2 * C] if part == 0 else qkv_res[:, 2 * C:3 * C]
                    if w >= 1:
                        act.wait_ge(qkv_done, w)
                    nc.scalar.activation(dst, src[:, 0:dst.shape[1]], ACT.Copy).then_inc(result_copied, 1)
                else:
                    nc.scalar.activation(res[:, ("proj", "mod", "gproj").index(kind), :], src[:, 0:C],
                                         ACT.Copy).then_inc(result_copied, 1)

            for s in range(STEPS):
                if s < NT:
                    patch_highs(s)
                if s == 0:
                    act.wait_ge(kv_bias_made, 1)
                    nc.scalar.activation(kv_bias[:], psum[:, RESULT_BANK[1], :], ACT.Copy).then_inc(kv_bias_copied, 1)
                if 0 <= s - KV_LAG < NT:
                    copy_turned(("kv", s - KV_LAG))
                if 0 <= s - 1 < NT:
                    copy_centred(s - 1)
                if 0 <= s - KV_LAG < NT:
                    copy_result("kv", s - KV_LAG, 0)
                for kind, w in extras(s - 1):
                    copy_result(kind, w, 0)
                    if kind == "qkv":
                        copy_result(kind, w, 1)
                for item in extras(s):
                    copy_turned(item)
                for w in range(NW):
                    if s == NP * w + SCORE + 2:
                        act.wait_ge(shifted, w + 1)
                        nc.scalar.activation(score[:, 2], score[:, 1], ACT.Exp).then_inc(exp_done, 1)
                if SPLIT0 <= s < SPLIT0 + J:
                    j = s - SPLIT0
                    act.wait_ge(w1_loaded if j < J // 2 else w2_loaded, 16)
                    raw, hi, _ = piece(j)
                    nc.scalar.activation(hi(0), raw, ACT.Copy).then_inc(w_hi_done, 1)
                if s == GATT:
                    act.wait_ge(shifted, NW + 1)
                    nc.scalar.activation(gscore[:, 2], gscore[:, 1], ACT.Exp).then_inc(exp_done, 1)

            act.wait_ge(shifted, NW + 2)
            nc.scalar.activation(att_s[:, 2], att_s[:, 1], ACT.Exp).then_inc(exp_done, 1)
            for n, i in enumerate(XT_ORDER):
                act.wait_ge(xt_turned, n + 1)
                src = psum[:, XT_BANK[n % 3], 0:C].rearrange("p (k t) -> p k t", k=KC)
                nc.scalar.activation(xt_hi[:, :, i * P:(i + 1) * P], src, ACT.Copy)
                nc.scalar.activation(xt_f[:, :, i * P:(i + 1) * P], src, ACT.Copy).then_inc(xt_copied, 1)
            act.wait_ge(shifted, NW + 3)
            nc.scalar.activation(g8[:, 2], g8[:, 1], ACT.Exp).then_inc(exp_done, 1)

            def relu(k, e, j):
                act.wait_ge(hidden_done, J * k + j + 1)
                if j >= 2:
                    act.wait_ge(h_split, J * k + j - 1)
                b = HIDDEN_BANK[j % 2]
                nc.scalar.activation(h_f[:, j % 2, :].rearrange("p (a t) -> p a t", a=2),
                                     psum[:, b:b + 2, 0:HALF], ACT.Relu,
                                     bias=b1_cols[:, bass.ds(e, 1), j]).then_inc(relu_done, 1)

            def split_high(k, u, j):
                raw, hi, _ = piece(j)
                if j == 0:
                    act.wait_ge(w1_loaded, 16 * k + 16)
                if j == J // 2:
                    act.wait_ge(w2_loaded, 16 * k + 16)
                nc.scalar.activation(hi(u), raw, ACT.Copy).then_inc(w_hi_done, 1)

            def pair_exp():
                act.wait_ge(shifted, NW + 4)
                nc.scalar.activation(gt[:, 6], gt[:, 5], ACT.Exp).then_inc(exp_done, 1)

            def expert(k, e, u, more=True, beside=lambda j: None):
                for j in range(J):
                    beside(j)
                    relu(k, e, j)
                    if more:
                        split_high(k + 1, 1 - u, j)

            def expert_at(i):
                return act.value_load(table[0:1, bass.ds(i, 1)], min_val=0, max_val=OTHERS - 1)

            expert(0, FIRST[0], 0, beside=lambda j: pair_exp() if j == 3 else None)
            expert(1, FIRST[1], 1)
            act.wait_ge(table_made, 1)
            pairs = act.value_load(table[0:1, COUNT:COUNT + 1], min_val=2, max_val=OTHERS // 2)
            with act.Fori(0, pairs - 1) as i:
                expert(2 * i + 2, expert_at(2 * i), 0)
                expert(2 * i + 3, expert_at(2 * i + 1), 1)
            expert(2 * pairs, expert_at(2 * pairs - 2), 0)
            expert(2 * pairs + 1, expert_at(2 * pairs - 1), 1, more=False)

        @block.tensor
        def _(pe):
            pe.wait_ge(ident_made, 1)
            pe.wait_ge(first_loaded, 16)
            for k in range(NK):
                for h in range(KC):
                    last = nc.tensor.transpose(psum[0:K, k, h * P:(h + 1) * P],
                                               conv_raw[:, h, START[k] * PS:START[k] * PS + K], ident[:])
            last.then_inc(conv_w_turned, 1)
            pe.wait_ge(early_loaded, 16 * 3)
            n = E * J + 2 * KC
            nc.tensor.transpose(psum[:, RESULT_BANK[0], 0:n], rows_in[:], ident[0:n, 0:n]).then_inc(cols_turned, 1)

            def kv_bias_product():
                pe.wait_ge(kvb_widened, 1)
                pe.wait_ge(wkv_loaded, 16)
                for k in range(KC):
                    last = nc.tensor.matmul(psum[:, RESULT_BANK[1], :], kvb_wide[:, k, :], wkv_raw[:, k, :],
                                            start=(k == 0), stop=(k == KC - 1))
                last.then_inc(kv_bias_made, 1)

            def turn_patches(t):
                pe.wait_ge(patches_gathered, t + 1)
                for g, (a, b) in enumerate(GROUPS):
                    bank = PATCH_BANK[(2 * t + g) % 3]
                    if 2 * t + g < 3:
                        pe.wait_ge(conv_w_centred, 2 * t + g + 1)
                    else:
                        pe.wait_ge(patch_lo_done, 2 * t + g - 2)
                    for k in range(a, b):
                        last = nc.tensor.transpose(psum[0:K, bank, (k - a) * P:(k - a + 1) * P],
                                                   patches[:, t % 3, START[k] * PS:START[k] * PS + K], ident[:])
                    last.then_inc(patch_turned, 1)

            def convolve(t):
                pe.wait_ge(patch_lo_done, 2 * t + 2)
                if t == 0:
                    pe.wait_ge(conv_w_split, 2)
                if t >= 2:
                    pe.wait_ge(cen_copied, t - 1)
                dst = psum[:, CONV_BANK[t % 2], 0:CW]
                passes = [(p, w) for k in range(NK) for p, w in
                          ((patch_hi[0:K, t % 2, k, :], conv_hi[0:K, k, :]),
                           (patch_hi[0:K, t % 2, k, :], conv_lo[0:K, k, :]),
                           (patch_lo[0:K, t % 2, k, :], conv_hi[0:K, k, :]))]
                for m, (p, w) in enumerate(passes):
                    last = nc.tensor.matmul(dst, p, w, start=(m == 0), stop=(m == len(passes) - 1))
                last.then_inc(conv_done, 1)

            def turn(item):
                i = turn_order.index(item)
                kind, w = item
                if i >= 1:
                    pe.wait_ge(turn_copied, i)
                    if turn_order[i - 1][0] == "kv":
                        pe.wait_ge(turn_lo_done, kv_turns[i])
                if kind == "kv":
                    pe.wait_ge(cen_copied, w + 1)
                    src = cen[:, w % CEN_RING, 0:C]
                elif kind == "query":
                    pe.wait_ge(redln_done, w + 1)
                    src = redln[:]
                elif kind == "proj":
                    pe.wait_ge(agg_done, w + 1)
                    src = agg[:]
                elif kind == "mod":
                    pe.wait_ge(local_done, w + 1)
                    src = local[:, w % 2, :]
                elif kind == "gkv":
                    pe.wait_ge(kvln_done, w + 1)
                    src = kvln[:]
                elif kind == "gquery":
                    pe.wait_ge(class_ln_done, 1)
                    src = class_ln[:]
                elif kind == "gproj":
                    pe.wait_ge(gagg_done, 1)
                    src = gagg[:]
                else:
                    pe.wait_ge(token_done, w + 1)
                    src = hs[:, w, :]
                for k in range(KC):
                    last = nc.tensor.transpose(psum[:, TURN_BANK, k * P:(k + 1) * P],
                                               src[:, k * P:(k + 1) * P], ident[:])
                last.then_inc(turned, 1)

            def project(kind, w, part):
                i = result_order.index((kind, w, part))
                ti = turn_order.index((kind, w))
                pe.wait_ge(turn_copied, ti + 1)
                if i >= 2:
                    pe.wait_ge(result_copied, i - 1)
                elif i == 0:
                    pe.wait_ge(cols_copied, 1)
                else:
                    pe.wait_ge(kv_bias_copied, 1)
                bank = RESULT_BANK[i % 2]
                if kind == "kv":
                    pe.wait_ge(turn_lo_done, w + 1)
                    if w == 0:
                        pe.wait_ge(wkv_split, 1)
                    b = w % 2
                    passes = [(p, wt) for k in range(KC) for p, wt in
                              ((turn_hi[:, b, k * P:(k + 1) * P], wkv_hi[:, k, :]),
                               (turn_hi[:, b, k * P:(k + 1) * P], wkv_lo[:, k, :]),
                               (turn_lo[:, b, k * P:(k + 1) * P], wkv_hi[:, k, :]))]
                    width = 2 * C
                else:
                    b = plain_turns[ti] % 3
                    wt, width = {"query": (wq_sb[:], C), "proj": (proj_sb[:], C), "mod": (mod_sb[:], C),
                                 "gkv": (gwkv_sb[:], 2 * C), "gquery": (gwq_sb[:], C), "gproj": (gproj_sb[:], C),
                                 "qkv": (qkv_w[:, :, 0:2 * C] if part == 0 else qkv_w[:, :, 2 * C:3 * C],
                                         2 * C if part == 0 else C)}[kind]
                    passes = [(turn_f[:, b, k * P:(k + 1) * P], wt[:, k, :]) for k in range(KC)]
                for m, (p, m_w) in enumerate(passes):
                    last = nc.tensor.matmul(psum[:, bank, 0:width], p, m_w, start=(m == 0),
                                            stop=(m == len(passes) - 1))
                last.then_inc(projected, 1)

            for s in range(STEPS):
                if s < NT:
                    turn_patches(s)
                if s == 0:
                    kv_bias_product()
                if s == CLASSQ:
                    pe.wait_ge(late_loaded, 16 * LATE)
                if 0 <= s - KV_LAG < NT:
                    turn(("kv", s - KV_LAG))
                if 0 <= s - 1 < NT:
                    convolve(s - 1)
                if 0 <= s - KV_LAG < NT:
                    project("kv", s - KV_LAG, 0)
                for kind, w in extras(s - 1):
                    project(kind, w, 0)
                    if kind == "qkv":
                        project(kind, w, 1)
                for item in extras(s):
                    turn(item)

            for n, i in enumerate(PE_SUMS):
                if i in POOL_QUERIES:
                    pe.wait_ge(pool_valued, POOL_QUERIES.index(i) + 1)
                else:
                    pe.wait_ge(dve_valued, DVE_QUERIES.index(i) + 1)
                pe.wait_ge(token_done, T)
                nc.tensor.matmul(psum[:, n, 0:C], ident[:], hs[:, i, :], start=True, stop=False)
                for j in range(T):
                    last = nc.tensor.matmul(psum[:, n, 0:C], ident[:], att_prod[:, i, j, :], start=False,
                                            stop=(j == T - 1))
                last.then_inc(values_summed, 1)

            for n, i in enumerate(XT_ORDER):
                pe.wait_ge(h1_done, n + 1)
                if n >= 3:
                    pe.wait_ge(xt_copied, n - 2)
                    pe.wait_ge(xt_split, n - 2)
                for k in range(KC):
                    last = nc.tensor.transpose(psum[:, XT_BANK[n % 3], k * P:(k + 1) * P],
                                               h1[:, i, k * P:(k + 1) * P], ident[:])
                last.then_inc(xt_turned, 1)
            pe.wait_ge(xt_copied, T)
            for i in range(T):
                for k in range(KC):
                    last = nc.tensor.matmul(psum[:, GATE_BANK, i * E:(i + 1) * E],
                                            xt_f[:, k, i * P:(i + 1) * P], wg_sb[:, k, :],
                                            start=(k == 0), stop=(k == KC - 1))
            last.then_inc(gate_scored, 1)
            pe.wait_ge(xt_split, T)

            def hidden(n_slot, u, j):
                if j >= 2:
                    pe.wait_ge(relu_done, J * n_slot + j - 1)
                b = HIDDEN_BANK[j % 2]
                cut = slice(j * P, (j + 1) * P)
                passes = [(w, xt) for k in range(KC) for w, xt in
                          ((w1_hi[u][:, k, cut], xt_hi[:, k, :]), (w1_hi[u][:, k, cut], xt_lo[:, k, :]),
                           (w1_lo[u][:, k, cut], xt_hi[:, k, :]))]
                for m, (w, xt) in enumerate(passes):
                    for a in range(2):
                        last = nc.tensor.matmul(psum[:, b + a, 0:HALF], w, xt[:, a * HALF:(a + 1) * HALF],
                                                start=(m == 0), stop=(m == len(passes) - 1))
                last.then_inc(hidden_done, 1)

            def outer(n_slot, u, j):
                pe.wait_ge(h_split, J * n_slot + j + 1)
                if j == 0:
                    pe.wait_ge(w_lo_done, J * n_slot + J)
                for i in range(T):
                    if j == 0 and i % 2 == 0:
                        pe.wait_ge(acc_ready, BANKS * n_slot + i // 2 + 1)
                    dst = psum[:, EXPERT_BANK + i // 2, (i % 2) * C:(i % 2 + 1) * C]
                    cut = slice(i * P, (i + 1) * P)
                    passes = ((h_hi[:, j % 2, cut], w2_hi[u][:, j, :]), (h_hi[:, j % 2, cut], w2_lo[u][:, j, :]),
                              (h_lo[:, j % 2, cut], w2_hi[u][:, j, :]))
                    for m, (h, w) in enumerate(passes):
                        last = nc.tensor.matmul(dst, h, w, start=(j == 0 and m == 0 and i % 2 == 0),
                                                stop=(j == J - 1 and m == 2), skip_group_check=True)
                last.then_inc(hidden_used, 1)

            def second_bias(tiles):
                cut = slice(tiles[0], tiles[-1] + 1)
                nc.tensor.matmul(psum[:, GATE_BANK, 0:len(tiles) * C], gates_t[:],
                                 b2_wide[:, cut, :].rearrange("r t c -> r (t c)"),
                                 start=True, stop=True).then_inc(gate_bias_done, 1)

            def beside(n):
                if n == 5:
                    pe.wait_ge(gates_done, 2)
                    nc.tensor.matmul(psum[0:1, GATE_BANK, 0:E], ones[:], gate_sums[:], start=True, stop=True
                                     ).then_inc(gates_summed, 1)
                if n == 7:
                    pe.wait_ge(table_made, 1)
                    nc.tensor.transpose(psum[0:T * E, GATE_BANK, 0:P], gates.rearrange("p t e -> p (t e)"), ident[:]
                                        ).then_inc(gates_turned, 1)
                if n == J + 2:
                    pe.wait_ge(b2_loaded, 16 * T)
                    pe.wait_ge(gates_t_copied, 1)
                    second_bias(range(0, 2))
                if n == J + 4:
                    pe.wait_ge(gate_bias_used, 1)
                    second_bias(range(2, 4))
                if n == J + 6:
                    pe.wait_ge(gate_bias_used, 2)
                    second_bias(range(4, T))

            def expert(k, u, more=True, beside=lambda j: None):
                for j in range(1, J):
                    hidden(k, u, j)
                    outer(k, u, j - 1)
                    beside(j)
                if more:
                    pe.wait_ge(w_lo_done, J * k + J + J // 2)
                    hidden(k + 1, 1 - u, 0)
                outer(k, u, J - 1)

            pe.wait_ge(w_lo_done, J // 2)
            hidden(0, 0, 0)
            expert(0, 0, beside=beside)
            expert(1, 1, beside=lambda j: beside(J + j))
            pairs = pe.value_load(table[0:1, COUNT:COUNT + 1], min_val=2, max_val=OTHERS // 2)
            with pe.Fori(0, pairs - 1) as i:
                expert(2 * i + 2, 0)
                expert(2 * i + 3, 1)
            expert(2 * pairs, 0)
            expert(2 * pairs + 1, 1, more=False)

        @block.gpsimd
        def _(pool):
            chain = [0]

            def link(ins):
                chain[0] += 1
                ins.then_inc(pool_chain, 1)
                pool.wait_ge(pool_chain, chain[0])

            link(nc.gpsimd.memset(ident[:], 0.0))
            nc.gpsimd.affine_select(out=ident[:], in_=ident[:], compare_op=ALU.not_equal, fill=1.0, base=0,
                                    pattern=[[-1, P]], channel_multiplier=1).then_inc(ident_made, 1)
            nc.gpsimd.memset(minus_half[:], -0.5)
            nc.gpsimd.memset(ones[:], 1.0)
            nc.gpsimd.iota(iota8i[:], pattern=[[1, E]], base=0, channel_multiplier=0).then_inc(consts_made, 1)
            pool.wait_ge(consts_made, 1)
            nc.gpsimd.tensor_copy(iota8[:], iota8i[:]).then_inc(consts_made, 1)
            def power(dst, src, done):
                nc.gpsimd.tensor_tensor(dst, src, minus_half[:, 0:src.shape[1]], ALU.pow).then_inc(done, 1)

            def sum_reduced(t):
                w, n = divmod(t, NP)
                pool.wait_ge(cen_copied, t + 1)
                if n == 0:
                    nc.gpsimd.tensor_copy(redsum[:, w % 2, :], cen[:, t % CEN_RING, :]).then_inc(red_summed, 1)
                else:
                    pool.wait_ge(red_summed, t)
                    nc.gpsimd.tensor_tensor(redsum[:, w % 2, :], redsum[:, w % 2, :], cen[:, t % CEN_RING, :], ALU.add
                                            ).then_inc(red_summed, 1)

            def gather_patches(t):
                r, col = slot_of(t)
                w, n = divmod(t, NP)
                if n % CS == 0:
                    pool.wait_ge(lines_loaded[r], 16 * (w // 2 + 1))
                if t >= 3:
                    pool.wait_ge(patch_turned, 2 * (t - 2))
                nc.gpsimd.tensor_scalar(patches[:, t % 3, :].rearrange("p (l x) -> p l x", x=PS),
                                        lines[:, r, :, col:col + PS], 1.0, 0.0, ALU.mult, ALU.add
                                        ).then_inc(patches_gathered, 1)

            gather_patches(0)
            pool.wait_ge(cols_copied, 1)
            for k in range(KC):
                last = nc.gpsimd.tensor_copy(kvb_wide[:, k, :], kvb_cols[:, k:k + 1].broadcast_to([P, P]))
            last.then_inc(kvb_widened, 1)
            for s in range(STEPS):
                if s + 1 < NT:
                    gather_patches(s + 1)
                if 0 <= s - 1 < NT:
                    sum_reduced(s - 1)
                for w in range(NW):
                    at = s - NP * w
                    if at == RED:
                        pool.wait_ge(var_done, VAR_ORDER.index(("red", w)) + 1)
                        power(rstd[:, w, :], var_eps[:, w, :], rstd_done)
                        link(nc.gpsimd.tensor_scalar(mu9[:, w:w + 1], redsum[:, w % 2, C:C + 1], 1.0 / NP, None,
                                                     ALU.mult))
                        link(nc.gpsimd.tensor_scalar(redp[:, w % 2, :], redsum[:, w % 2, 0:C], 1.0 / NP,
                                                     mu9[:, w:w + 1], ALU.mult, ALU.add))
                        if w == 0:
                            pool.wait_ge(late_loaded, 16 * LATE)
                        nc.gpsimd.tensor_tensor(redp[:, w % 2, :], redp[:, w % 2, :], row["proj_b"][:], ALU.add
                                                ).then_inc(redp_done, 1)
                    if at == SCORE:
                        pool.wait_ge(result_copied, copied("query", w))
                        pool.wait_ge(result_copied, copied("kv", NP * w + NP - 1))
                        if w >= 1:
                            pool.wait_ge(agg_done, w)
                        if w >= 2:
                            pool.wait_ge(pairs_scored, w - 1)
                        nc.gpsimd.tensor_tensor(prod[:, 6:9, :], kv[:, w % 2, 6:9, 0:C],
                                                q_sb[:, w % 2, :].unsqueeze(1).broadcast_to([P, 3, C]), ALU.mult
                                                ).then_inc(pool_scored, 1)
                    if at == WEIGH:
                        pool.wait_ge(probs_done, w + 1)
                        nc.gpsimd.tensor_tensor(
                            prod[:, 6:9, :].rearrange("p n (h d) -> p n h d", h=H8),
                            kv[:, w % 2, 6:9, C:2 * C].rearrange("p n (h d) -> p n h d", h=H8),
                            probe[:, 1, 6:9, :].unsqueeze(3).broadcast_to([P, 3, H8, DH]), ALU.mult
                        ).then_inc(pool_weighed, 1)
                    if at == LOCAL:
                        pool.wait_ge(var_done, VAR_ORDER.index(("local", w)) + 1)
                        power(rs[:, w:w + 1], ve[:, w:w + 1], rstd_done)
                for w in range(1, T):
                    if s == pairs_step(w):
                        pool.wait_ge(qkv_done, w + 1)
                        pool.wait_ge(pairs_scored, w)
                        pool.wait_ge(agg_done, min(w + 2, NW))
                        if w + 2 > NW:
                            pool.wait_ge(gagg_done, 1)
                        pair_products(nc.gpsimd, w, False, max(0, w - POOL_PAIRS), w).then_inc(pool_paired, 1)
                if s == CLASSQ - 1:
                    pool.wait_ge(var_done, VAR_ORDER.index(("class", 0)) + 1)
                    power(rs[:, NW:T], ve[:, NW:T], rstd_done)
                if SPLIT0 <= s < SPLIT0 + J:
                    j = s - SPLIT0
                    raw, hi, lo = piece(j)
                    pool.wait_ge(w_hi_done, j + 1)
                    nc.gpsimd.tensor_tensor(lo(0), raw, hi(0).bitcast(F32), ALU.subtract).then_inc(w_lo_done, 1)

            pool.wait_ge(probs_done, NW + 2)
            for i in POOL_QUERIES:
                weigh_tokens(nc.gpsimd, i).then_inc(pool_valued, 1)
            pool.wait_ge(var_done, VAR_ORDER.index("attention") + 1)
            power(rs[:, 1:T], ve[:, 1:T], rstd_done)
            pool.wait_ge(var_done, VAR_ORDER.index("attention_last") + 1)
            power(rs[:, 0:1], ve[:, 0:1], rstd_done)
            pool.wait_ge(h1_done, T)
            nc.gpsimd.memset(b2_wide[:], 0.0).then_inc(b2_cleared, 1)
            for b in range(BANKS):
                cut = slice(2 * b, min(2 * b + 2, T))
                nc.gpsimd.tensor_copy(acc[:, cut, :], h1[:, cut, :]).then_inc(acc_ready, 1)
            pool.wait_ge(var_done, VAR_ORDER.index("output") + 1)
            power(rs[:], ve[:], rstd_done)

        @block.vector
        def _(dve):
            chain = [0]

            def link(ins):
                chain[0] += 1
                return ins.then_inc(dve_chain, 1)

            def settle():
                dve.wait_ge(dve_chain, chain[0])

            V = nc.vector
            dve.wait_ge(conv_w_turned, 1)
            link(V.tensor_reduce(conv_mean[0:K, 0, :], psum[0:K, 0:NK, 0:C], AX_X, ALU.add))
            settle()
            V.tensor_scalar(conv_mean[0:K, 1, :], conv_mean[0:K, 0, :], -1.0 / C, None, ALU.mult
                            ).then_inc(conv_mean_made, 1)
            link(V.tensor_scalar(conv_mean[0:K, 0, :], conv_mean[0:K, 0, :], 1.0 / C, None, ALU.mult))
            dve.wait_ge(conv_mean_made, 1)
            settle()
            mean_twice = conv_mean[0:K, 0, :].unsqueeze(2).broadcast_to([K, NK, 2])
            link(V.tensor_copy(conv_hi[0:K, :, C:CW], mean_twice))
            settle()
            link(V.tensor_tensor(conv_lo[0:K, :, C:CW], mean_twice, conv_hi[0:K, :, C:CW].bitcast(F32), ALU.subtract))
            for k in range(NK):
                dve.wait_ge(conv_hi_done, k + 1)
                V.scalar_tensor_tensor(out=conv_lo[0:K, k, 0:C], in0=psum[0:K, k, 0:C],
                                       scalar=conv_mean[0:K, 1, k:k + 1], in1=conv_hi[0:K, k, 0:C].bitcast(F32),
                                       op0=ALU.add, op1=ALU.subtract).then_inc(conv_w_centred, 1)
            dve.wait_ge(conv_w_centred, NK)
            settle()
            V.memset(conv_hi[0:OVER, NK - 1, :].bitcast(F32), 0.0).then_inc(conv_w_split, 1)
            V.memset(conv_lo[0:OVER, NK - 1, :].bitcast(F32), 0.0).then_inc(conv_w_split, 1)

            def split_wkv():
                dve.wait_ge(wkv_loaded, 16)
                dve.wait_ge(cols_copied, 1)
                for k in range(KC):
                    link(V.tensor_scalar(wkv_hi[:, k, :], wkv_raw[:, k, :], kvg_cols[:, k:k + 1], None, ALU.mult))
                settle()
                for k in range(KC):
                    last = V.scalar_tensor_tensor(out=wkv_lo[:, k, :], in0=wkv_raw[:, k, :], scalar=kvg_cols[:, k:k + 1],
                                                  in1=wkv_hi[:, k, :].bitcast(F32), op0=ALU.mult, op1=ALU.subtract)
                last.then_inc(wkv_split, 1)

            def patch_lows(t):
                for g, (a, b) in enumerate(GROUPS):
                    dve.wait_ge(patch_hi_done, 2 * t + g + 1)
                    V.tensor_tensor(patch_lo[0:K, t % 2, a:b, :],
                                    psum[0:K, PATCH_BANK[(2 * t + g) % 3], 0:(b - a) * P].rearrange(
                                        "p (k t) -> p k t", t=P),
                                    patch_hi[0:K, t % 2, a:b, :].bitcast(F32), ALU.subtract).then_inc(patch_lo_done, 1)

            def turn_low(t):
                dve.wait_ge(turn_copied, turn_order.index(("kv", t)) + 1)
                V.tensor_tensor(turn_lo[:, t % 2, :], psum[:, TURN_BANK, 0:C], turn_hi[:, t % 2, :].bitcast(F32),
                                ALU.subtract).then_inc(turn_lo_done, 1)

            def square_sum(t):
                w, n = divmod(t, NP)
                dve.wait_ge(cen_copied, t + 1)
                if t >= 1:
                    dve.wait_ge(sumsq_done, t)
                c = cen[:, t % CEN_RING, 0:C]
                V.tensor_tensor_reduce(junk[:], c, c, 1.0, 0.0, ALU.mult, ALU.add,
                                       sumsq[:, w, n:n + 1]).then_inc(sumsq_done, 1)

            def layer_norm_stats(src, i):
                link(V.bn_stats(bn[:, i, :], src))
                settle()
                link(V.bn_aggr(mv[:, i, :], bn[:, i, :]))
                settle()
                V.tensor_scalar(ve[:, i:i + 1], mv[:, i, 1:2], EPS, None, ALU.add).then_inc(var_done, 1)

            def layer_norm(dst, src, i, gain, bias, done):
                link(V.tensor_scalar(work[:], src, mv[:, i, 0:1], rs[:, i:i + 1], ALU.subtract, ALU.mult))
                settle()
                link(V.tensor_tensor(work[:], work[:], gain, ALU.mult))
                settle()
                V.tensor_tensor(dst, work[:], bias, ALU.add).then_inc(done, 1)

            def reduced_query(w):
                dve.wait_ge(rstd_done, VAR_ORDER.index(("red", w)) + 1)
                link(V.tensor_scalar(work[:], redsum[:, w % 2, 0:C], 1.0 / NP, rstd[:, w, NP:NP + 1], ALU.mult, ALU.mult))
                settle()
                link(V.tensor_tensor(work[:], work[:], row["q_g"][:], ALU.mult))
                settle()
                V.tensor_tensor(redln[:], work[:], row["q_b"][:], ALU.add).then_inc(redln_done, 1)

            def heads(ap):
                return ap.rearrange("p n (h d) -> p n h d", h=H8)

            def score_products(w, c):
                n = slice(3 * c, 3 * c + 3)
                if c == 2:
                    dve.wait_ge(pool_scored, w + 1)
                else:
                    link(V.tensor_tensor(prod[:, n, :], kv[:, w % 2, n, 0:C],
                                         q_sb[:, w % 2, :].unsqueeze(1).broadcast_to([P, 3, C]), ALU.mult))
                    settle()
                link(V.tensor_reduce(score[:, 0, n, :], heads(prod[:, n, :]), AX_X, ALU.add))

            def softmax_shift(w):
                by_patch = rstd[:, w, 0:NP].unsqueeze(2).broadcast_to([P, NP, H8])
                settle()
                link(V.tensor_tensor(score[:, 0], score[:, 0], by_patch, ALU.mult))
                settle()
                link(V.tensor_tensor(score[:, 0], score[:, 0], qbk[:].unsqueeze(1).broadcast_to([P, NP, H8]), ALU.add))
                settle()
                link(V.tensor_reduce(stat8[:, 0, :], score[:, 0].rearrange("p n h -> p h n"), AX_X, ALU.max))
                settle()
                V.tensor_tensor(score[:, 1], score[:, 0], stat8[:, 0, :].unsqueeze(1).broadcast_to([P, NP, H8]),
                                ALU.subtract).then_inc(shifted, 1)

            def softmax_weights(w):
                dve.wait_ge(exp_done, w + 1)
                link(V.tensor_reduce(stat8[:, 1, :], score[:, 2].rearrange("p n h -> p h n"), AX_X, ALU.add))
                settle()
                link(V.reciprocal(stat8[:, 2, :], stat8[:, 1, :]))
                settle()
                link(V.tensor_tensor(probe[:, 0], score[:, 2],
                                     stat8[:, 2, :].unsqueeze(1).broadcast_to([P, NP, H8]), ALU.mult))
                settle()
                V.tensor_tensor(probe[:, 1], probe[:, 0], rstd[:, w, 0:NP].unsqueeze(2).broadcast_to([P, NP, H8]),
                                ALU.mult).then_inc(probs_done, 1)

            def weigh_values(w, c):
                n = slice(3 * c, 3 * c + 3)
                dve.wait_ge(probs_done, w + 1)
                link(V.tensor_tensor(heads(prod[:, n, :]), heads(kv[:, w % 2, n, C:2 * C]),
                                     probe[:, 1, n, :].unsqueeze(3).broadcast_to([P, 3, H8, DH]), ALU.mult))

            def sum_values(w, part):
                cut = slice(part * C // 2, (part + 1) * C // 2)
                settle()
                dve.wait_ge(pool_weighed, w + 1)
                link(V.tensor_reduce(agg[:, cut], prod[:, :, cut].rearrange("p n c -> p c n"), AX_X, ALU.add))
                if part == 1:
                    settle()
                    V.tensor_tensor(agg[:], agg[:], kv_bias[:, C:2 * C], ALU.add).then_inc(agg_done, 1)

            def take_qkv(w):
                dve.wait_ge(result_copied, copied("qkv", w, 1))
                V.tensor_tensor(aq[:, w, :], qkv_res[:, 0:C], row["qkv_b"][:, 0:C], ALU.add)
                V.tensor_tensor(akv[:, T - 1 - w, :], qkv_res[:, C:3 * C], row["qkv_b"][:, C:3 * C], ALU.add
                                ).then_inc(qkv_done, 1)

            def score_pairs(w):
                dve.wait_ge(qkv_done, w + 1)
                first = max(0, w - POOL_PAIRS)
                settle()
                link(pair_products(V, w, True, 0, w + 1))
                if first:
                    link(pair_products(V, w, False, 0, first))
                settle()
                by_head = prod.rearrange("p n (h d) -> p n h d", h=H16)
                ins = V.tensor_reduce(att_raw[:, w, :, T - 1 - w:T].rearrange("p h j -> p j h"),
                                      by_head[:, 0:w + 1], AX_X, ALU.add)
                if w:
                    link(ins)
                    dve.wait_ge(pool_paired, w)
                    ins = V.tensor_reduce(att_raw[:, 0:w, :, T - 1 - w], by_head[:, w + 1:2 * w + 1], AX_X, ALU.add)
                ins.then_inc(pairs_scored, 1)

            for s in range(STEPS):
                if s < NT:
                    patch_lows(s)
                if s == 0:
                    split_wkv()
                if 0 <= s - KV_LAG < NT:
                    turn_low(s - KV_LAG)
                if 0 <= s - 1 < NT:
                    square_sum(s - 1)
                if s == CLASSQ - 1:
                    dve.wait_ge(late_loaded, 16 * LATE)
                    layer_norm_stats(row["class"][:], NW)
                if s == CLASSQ:
                    dve.wait_ge(rstd_done, VAR_ORDER.index(("class", 0)) + 1)
                    layer_norm(class_ln[:], row["class"][:], NW, row["gq_g"][:], row["gq_b"][:], class_ln_done)
                for w in range(NW):
                    at = s - NP * w
                    if at == RED:
                        dve.wait_ge(sumsq_done, NP * (w + 1))
                        dve.wait_ge(red_summed, NP * (w + 1))
                        link(V.tensor_tensor_reduce(work[:], redsum[:, w % 2, 0:C], redsum[:, w % 2, 0:C], 1.0, 0.0, ALU.mult,
                                                    ALU.add, sumsq[:, w, NP:NP + 1]))
                        link(V.tensor_scalar(var_eps[:, w, 0:NP], sumsq[:, w, 0:NP], 1.0 / C, EPS, ALU.mult, ALU.add))
                        settle()
                        V.tensor_scalar(var_eps[:, w, NP:NP + 1], sumsq[:, w, NP:NP + 1], 1.0 / (C * NP * NP), EPS,
                                        ALU.mult, ALU.add).then_inc(var_done, 1)
                    if at == RED + 1:
                        reduced_query(w)
                    if at == SCORE:
                        dve.wait_ge(result_copied, copied("query", w))
                        if w == 0:
                            dve.wait_ge(kv_bias_copied, 1)
                        link(V.tensor_tensor(work[:], q_sb[:, w % 2, :], kv_bias[:, 0:C], ALU.mult))
                        settle()
                        link(V.tensor_reduce(qbk[:], work[:].rearrange("p (h d) -> p h d", h=H8), AX_X, ALU.add))
                        score_products(w, 0)
                    if at == SCORE + 1:
                        score_products(w, 1)
                    if at == SCORE + 2:
                        score_products(w, 2)
                        softmax_shift(w)
                    if at == WEIGH:
                        softmax_weights(w)
                        weigh_values(w, 0)
                    if at == WEIGH + 1:
                        weigh_values(w, 1)
                    if at == SUM:
                        sum_values(w, 0)
                    if at == SUM + 1:
                        sum_values(w, 1)
                    if at == LOCAL:
                        dve.wait_ge(result_copied, copied("proj", w))
                        dve.wait_ge(redp_done, w + 1)
                        V.tensor_tensor(local[:, w % 2, :], res[:, 0, :], redp[:, w % 2, :], ALU.add).then_inc(local_done, 1)
                        dve.wait_ge(local_done, w + 1)
                        layer_norm_stats(local[:, w % 2, :], w)
                    if at == LOCAL + 1:
                        dve.wait_ge(rstd_done, VAR_ORDER.index(("local", w)) + 1)
                        layer_norm(kvln[:], local[:, w % 2, :], w, row["gkv_g"][:], row["gkv_b"][:], kvln_done)
                    if at == TOKEN:
                        dve.wait_ge(result_copied, copied("mod", w))
                        V.tensor_tensor(hs[:, w, :], res[:, 1, :], row["mod_b"][:], ALU.add).then_inc(token_done, 1)
                    if at == GSCORE:
                        dve.wait_ge(result_copied, copied("gkv", w))
                        link(V.tensor_tensor(work[:], gkv_sb[:, w, 0:C], gq_sb[:], ALU.mult))
                        settle()
                        link(V.tensor_reduce(gscore[:, 0, w, :], work[:].rearrange("p (h d) -> p h d", h=H8), AX_X,
                                             ALU.add))
                    if at == QKVB:
                        take_qkv(w)
                if s == GATT:
                    settle()
                    link(V.tensor_reduce(gstat[:, 0, :], gscore[:, 0].rearrange("p n h -> p h n"), AX_X, ALU.max))
                    settle()
                    V.tensor_tensor(gscore[:, 1], gscore[:, 0], gstat[:, 0, :].unsqueeze(1).broadcast_to([P, NW, H8]),
                                    ALU.subtract).then_inc(shifted, 1)
                    dve.wait_ge(exp_done, NW + 1)
                    link(V.tensor_reduce(gstat[:, 1, :], gscore[:, 2].rearrange("p n h -> p h n"), AX_X, ALU.add))
                    settle()
                    link(V.reciprocal(gstat[:, 2, :], gstat[:, 1, :]))
                    settle()
                    V.tensor_tensor(gprob[:], gscore[:, 2], gstat[:, 2, :].unsqueeze(1).broadcast_to([P, NW, H8]),
                                    ALU.mult).then_inc(probs_done, 1)
                    dve.wait_ge(probs_done, NW + 1)
                    link(V.tensor_tensor(heads(prod[:, 0:NW, :]), heads(gkv_sb[:, :, C:2 * C]),
                                         gprob[:].unsqueeze(3).broadcast_to([P, NW, H8, DH]), ALU.mult))
                    settle()
                    V.tensor_reduce(gagg[:], prod[:, 0:NW, :].rearrange("p n c -> p c n"), AX_X, ALU.add
                                    ).then_inc(gagg_done, 1)
                if s == CLASSO + 2:
                    dve.wait_ge(result_copied, copied("gproj", 0))
                    link(V.tensor_tensor(work[:], res[:, 2, :], row["gproj_b"][:], ALU.add))
                    settle()
                    V.tensor_tensor(hs[:, NW, :], work[:], row["class"][:], ALU.add).then_inc(token_done, 1)
                if s == CLASSO + 5:
                    take_qkv(NW)
                for w in range(T):
                    if s == pairs_step(w):
                        score_pairs(w)

            settle()
            dve.wait_ge(pairs_scored, T)
            over_keys = [P, T, H16, T]
            for k in range(T):
                link(V.scalar_tensor_tensor(out=att_s[:, 0, k], in0=att_raw[:, k], scalar=DK ** -0.5,
                                            in1=rel_rows[:, :, k:k + T], op0=ALU.mult, op1=ALU.add))
            settle()
            link(V.tensor_reduce(att_m[:, 0], att_s[:, 0], AX_X, ALU.max))
            settle()
            V.tensor_tensor(att_s[:, 1], att_s[:, 0], att_m[:, 0].unsqueeze(3).broadcast_to(over_keys),
                            ALU.subtract).then_inc(shifted, 1)
            dve.wait_ge(exp_done, NW + 2)
            link(V.tensor_reduce(att_m[:, 1], att_s[:, 2], AX_X, ALU.add))
            settle()
            link(V.reciprocal(att_m[:, 2], att_m[:, 1]))
            settle()
            V.tensor_tensor(att_s[:, 1], att_s[:, 2], att_m[:, 2].unsqueeze(3).broadcast_to(over_keys),
                            ALU.mult).then_inc(probs_done, 1)
            dve.wait_ge(probs_done, NW + 2)
            for i in DVE_QUERIES:
                weigh_tokens(V, i).then_inc(dve_valued, 1)
            for n, i in enumerate(DVE_SUMS):
                dve.wait_ge(dve_valued, DVE_QUERIES.index(i) + 1)
                link(V.tensor_reduce(att_o[:, n, :], att_prod[:, i].rearrange("p j c -> p c j"), AX_X, ALU.add))
            settle()
            dve.wait_ge(token_done, T)
            link(V.tensor_tensor(att_o[:], att_o[:], hs[:, DVE_SUMS[0]:DVE_SUMS[-1] + 1, :], ALU.add))
            settle()

            def attended(i):
                return psum[:, PE_SUMS.index(i), 0:C] if i in PE_SUMS else att_o[:, DVE_SUMS.index(i), :]

            def stats(i):
                if i in PE_SUMS:
                    dve.wait_ge(values_summed, PE_SUMS.index(i) + 1)
                link(V.bn_stats(bn[:, i, :], attended(i)))
                settle()
                link(V.bn_aggr(mv[:, i, :], bn[:, i, :]))

            for i in DVE_SUMS + PE_SUMS[:-1]:
                stats(i)
            settle()
            V.tensor_scalar(ve[:, 1:T], mv[:, 1:T, 1], EPS, None, ALU.add).then_inc(var_done, 1)
            stats(0)
            settle()
            V.tensor_scalar(ve[:, 0:1], mv[:, 0:1, 1], EPS, None, ALU.add).then_inc(var_done, 1)
            dve.wait_ge(rstd_done, VAR_ORDER.index("attention") + 1)
            for n, i in enumerate(XT_ORDER):
                if i == 0:
                    dve.wait_ge(rstd_done, VAR_ORDER.index("attention_last") + 1)
                V.tensor_scalar(h1[:, i, :], attended(i), mv[:, i, 0:1], rs[:, i:i + 1], ALU.subtract, ALU.mult
                                ).then_inc(h1_done, 1)
            for n, i in enumerate(XT_ORDER):
                dve.wait_ge(xt_copied, n + 1)
                V.tensor_tensor(xt_lo[:, :, i * P:(i + 1) * P],
                                psum[:, XT_BANK[n % 3], 0:C].rearrange("p (k t) -> p k t", k=KC),
                                xt_hi[:, :, i * P:(i + 1) * P].bitcast(F32), ALU.subtract).then_inc(xt_split, 1)

            def normalise(src, dst, which, done):
                for i in range(T):
                    link(V.bn_stats(bn[:, i, :], src[:, i, :]))
                settle()
                for i in range(T):
                    link(V.bn_aggr(mv[:, i, :], bn[:, i, :]))
                settle()
                V.tensor_scalar(ve[:], mv[:, :, 1], EPS, None, ALU.add).then_inc(var_done, 1)
                dve.wait_ge(rstd_done, VAR_ORDER.index(which) + 1)
                for i in range(T):
                    V.tensor_scalar(dst[:, i, :], src[:, i, :], mv[:, i, 0:1], rs[:, i:i + 1], ALU.subtract, ALU.mult
                                    ).then_inc(done, 1)

            per_token = [P, T, E]

            def gate_logits():
                dve.wait_ge(gate_scored, 1)
                link(V.tensor_tensor(g8[:, 0], psum[:, GATE_BANK, 0:T * E].rearrange("p (t e) -> p t e", e=E),
                                     row["bg"][:].unsqueeze(1).broadcast_to(per_token), ALU.add))
                settle()
                link(V.tensor_reduce(gt[:, 0], g8[:, 0], AX_X, ALU.max))
                settle()
                V.tensor_tensor(g8[:, 1], g8[:, 0], gt[:, 0].unsqueeze(2).broadcast_to(per_token), ALU.subtract
                                ).then_inc(shifted, 1)

            def gate_probs():
                dve.wait_ge(exp_done, NW + 3)
                link(V.tensor_reduce(gt[:, 1], g8[:, 2], AX_X, ALU.add))
                settle()
                link(V.reciprocal(gt[:, 2], gt[:, 1]))
                settle()
                link(V.tensor_tensor(g8[:, 3], g8[:, 2], gt[:, 2].unsqueeze(2).broadcast_to(per_token), ALU.mult))
                settle()
                for i in range(T):
                    link(V.max(g8[:, 4, i], g8[:, 3, i]))
                settle()

            def gate_choice():
                for i in range(T):
                    link(V.max_index(top_at[:, i], g8[:, 4, i], g8[:, 3, i]))
                V.tensor_tensor(gt[:, 5], g8[:, 4, :, 1], g8[:, 4, :, 0], ALU.subtract).then_inc(shifted, 1)
                settle()
                link(V.tensor_copy(gt[:, 3:5], top_at[:, :, 0:2].rearrange("p t k -> p k t")))

            def pair_softmax():
                dve.wait_ge(exp_done, NW + 4)
                link(V.tensor_scalar(gt[:, 7], gt[:, 6], 1.0, None, ALU.add))
                settle()
                link(V.reciprocal(gt[:, 8], gt[:, 7]))
                settle()
                link(V.tensor_tensor(gt[:, 9], gt[:, 6], gt[:, 8], ALU.mult))
                settle()
                dve.wait_ge(consts_made, 2)

            def spread_gate(k):
                for i in range(T):
                    link(V.tensor_scalar(g8[:, 5 * (1 - k), i], iota8[:], gt[:, 3 + k, i:i + 1], gt[:, 8 + k, i:i + 1],
                                         ALU.is_equal, ALU.mult))

            def join_gates():
                settle()
                V.tensor_tensor(gates[:], g8[:, 0], g8[:, 5], ALU.add).then_inc(gates_done, 1)
                dve.wait_ge(gates_done, 1)
                V.tensor_reduce(gate_sums[:], gates.rearrange("p t e -> p e t"), AX_X, ALU.add
                                ).then_inc(gates_done, 1)

            def make_table():
                BIG = float(E)
                link(V.memset(order[0:1, 0, :], -1.0))
                settle()
                link(V.tensor_scalar(order[0:1, 0, 0:OTHERS], iota8[0:1, 0:OTHERS], -1.0, BIG - 1, ALU.mult, ALU.add))
                dve.wait_ge(gates_summed, 1)
                link(V.tensor_scalar(order[0:1, 1, :], psum[0:1, GATE_BANK, 0:E], 0.0, BIG, ALU.is_gt, ALU.mult))
                settle()
                link(V.tensor_tensor(order[0:1, 0, 0:OTHERS], order[0:1, 0, 0:OTHERS], order[0:1, 1, 0:OTHERS], ALU.add))
                settle()
                link(V.max(order[0:1, 2, :], order[0:1, 0, :]))
                settle()
                link(V.tensor_scalar(order[0:1, 1, :], order[0:1, 2, :], BIG, BIG, ALU.is_ge, ALU.mult))
                link(V.tensor_scalar(order[0:1, 3, :], order[0:1, 2, :], -1.0, BIG - 1, ALU.mult, ALU.add))
                settle()
                link(V.tensor_tensor(order[0:1, 3, 0:OTHERS], order[0:1, 3, 0:OTHERS], order[0:1, 1, 0:OTHERS], ALU.add))
                link(V.tensor_scalar(order[0:1, 3, COUNT:COUNT + 1], order[0:1, 1, 4:5], 1.0 / BIG, 2.0, ALU.mult, ALU.add))
                settle()
                V.tensor_copy(table[0:1, :], order[0:1, 3, :]).then_inc(table_made, 1)

            def split_hidden(k, j, first=False):
                dve.wait_ge(relu_done, J * k + j + 1)
                if j != 1 and not (j == 0 and first):
                    dve.wait_ge(hidden_used, J * k + j - 1)
                V.tensor_copy(h_hi[:, j % 2, :], h_f[:, j % 2, :]).then_inc(h_hi_done, 1)
                dve.wait_ge(h_hi_done, J * k + j + 1)
                V.tensor_tensor(h_lo[:, j % 2, :], h_f[:, j % 2, :], h_hi[:, j % 2, :].bitcast(F32), ALU.subtract
                                ).then_inc(h_split, 1)

            def split_low(k, u, j):
                raw, hi, lo = piece(j)
                dve.wait_ge(w_hi_done, J * k + j + 1)
                V.tensor_tensor(lo(u), raw, hi(u).bitcast(F32), ALU.subtract).then_inc(w_lo_done, 1)

            def add_expert(k, e):
                dve.wait_ge(hidden_used, J * k + J)
                dve.wait_ge(acc_ready, BANKS * k + BANKS)
                for i in range(T):
                    last = V.scalar_tensor_tensor(out=acc[:, i, :],
                                                  in0=psum[:, EXPERT_BANK + i // 2, (i % 2) * C:(i % 2 + 1) * C],
                                                  scalar=gates[:, i, bass.ds(e, 1)], in1=acc[:, i, :],
                                                  op0=ALU.mult, op1=ALU.add)
                    if i % 2 == 1 or i == T - 1:
                        last.then_inc(acc_ready, 1)

            def beside(n):
                if n == 1:
                    gate_probs()
                if n == 2:
                    gate_choice()
                if n == 3:
                    pair_softmax()
                    spread_gate(0)
                if n == 4:
                    spread_gate(1)
                    join_gates()
                if n == 6:
                    make_table()
                if n == J + 1:
                    dve.wait_ge(gates_turned, 1)
                    V.tensor_copy(gates_t[:], psum[0:T * E, GATE_BANK, 0:P]).then_inc(gates_t_copied, 1)
                if n in (J + 3, J + 5, J + 7):
                    r = (J + 3, J + 5, J + 7).index(n)
                    a, b = 2 * r, min(2 * r + 2, T)
                    dve.wait_ge(gate_bias_done, r + 1)
                    dve.wait_ge(acc_ready, BANKS * 2)
                    V.tensor_tensor(acc[:, a:b, :], psum[:, GATE_BANK, 0:(b - a) * C].rearrange("p (i c) -> p i c", c=C),
                                    acc[:, a:b, :], ALU.add).then_inc(gate_bias_used, 1)
                if n == J + 7:
                    dve.wait_ge(gate_bias_used, BANKS)

            def expert(k, e, u, more=True, beside=lambda j: None):
                if more:
                    split_low(k + 1, 1 - u, 0)
                for j in range(1, J):
                    split_hidden(k, j)
                    if more:
                        split_low(k + 1, 1 - u, j)
                    beside(j)
                if more:
                    split_hidden(k + 1, 0)
                add_expert(k, e)

            def expert_at(i):
                return dve.value_load(table[0:1, bass.ds(i, 1)], min_val=0, max_val=OTHERS - 1)

            gate_logits()
            split_hidden(0, 0, first=True)
            expert(0, FIRST[0], 0, beside=beside)
            expert(1, FIRST[1], 1, beside=lambda j: beside(J + j))
            dve.wait_ge(table_made, 1)
            pairs = dve.value_load(table[0:1, COUNT:COUNT + 1], min_val=2, max_val=OTHERS // 2)
            with dve.Fori(0, pairs - 1) as i:
                expert(2 * i + 2, expert_at(2 * i), 0)
                expert(2 * i + 3, expert_at(2 * i + 1), 1)
            expert(2 * pairs, expert_at(2 * pairs - 2), 0)
            expert(2 * pairs + 1, expert_at(2 * pairs - 1), 1, more=False)
            dve.wait_ge(acc_ready, 2 * BANKS * pairs + 3 * BANKS)
            normalise(acc, fin, "output", fin_done)


_INS = [
    "x", "L0_tok_conv_w", "L0_tok_class_emb", "L0_tok_la_ln_q_g", "L0_tok_la_ln_q_b", "L0_tok_la_wq",
    "L0_tok_la_ln_kv_g", "L0_tok_la_ln_kv_b", "L0_tok_la_wkv", "L0_tok_la_proj_w", "L0_tok_la_proj_b",
    "L0_tok_ga_ln_q_g", "L0_tok_ga_ln_q_b", "L0_tok_ga_wq", "L0_tok_ga_ln_kv_g", "L0_tok_ga_ln_kv_b",
    "L0_tok_ga_wkv", "L0_tok_ga_proj_w", "L0_tok_ga_proj_b", "L0_tok_mod_w", "L0_tok_mod_b",
    "L0_attn_Wq", "L0_attn_bq", "L0_attn_Wk", "L0_attn_bk", "L0_attn_Wv", "L0_attn_bv", "L0_attn_rel_emb",
    "L0_ffn_W1", "L0_ffn_b1", "L0_ffn_W2", "L0_ffn_b2", "L0_ffn_Wg", "L0_ffn_bg",
]
_OUT_SHAPE = (128, 5, 256)


def kernel(**inputs):
    import numpy as _np
    import concourse.bacc as _bacc
    from concourse import mybir as _mybir
    from concourse.bass_utils import run_bass_kernel_spmd as _run

    nc = _bacc.Bacc("TRN2", target_bir_lowering=False, num_devices=1,
                    dynamic_dma_scratch_size=1024)
    arrays, args = {}, []
    for name in _INS:
        a = _np.ascontiguousarray(inputs[name])
        arrays[f"in_{name}_dram"] = a
        args.append(nc.dram_tensor(f"in_{name}_dram", a.shape, _mybir.dt.from_np(a.dtype), kind="ExternalInput").ap())
    args.append(nc.dram_tensor("out_0_dram", _OUT_SHAPE, _mybir.dt.float32, kind="ExternalOutput").ap())
    build(nc, *args)
    r = _run(nc, [arrays], core_ids=[0])
    return r.results[0]["out_0_dram"]
```

```python
from contextlib import ExitStack

import concourse.bass as bass
from concourse import mybir

ALU = mybir.AluOpType
ACT = mybir.ActivationFunctionType
F32 = mybir.dt.float32
F32R = mybir.dt.float32r
U32 = mybir.dt.uint32
AX_X = mybir.AxisListType.X

EPS = 1e-5


def build(nc, x, conv_w, class_emb, q_g, q_b, wq, kv_g, kv_b, wkv, proj_w, proj_b, gq_g, gq_b, gwq,
          gkv_g, gkv_b, gwkv, gproj_w, gproj_b, mod_w, mod_b, aWq, abq, aWk, abk, aWv, abv, rel,
          W1, b1, W2, b2, Wg, bg, out):
    B, CIN, IMG, _ = x.shape
    C = conv_w.shape[0]
    PS = conv_w.shape[2]
    P = 128
    KC = C // P
    GRID = IMG // PS
    CS = 3
    NW = (GRID // CS) ** 2
    NP = CS * CS
    NT = NW * NP
    H8 = 8
    DH = C // H8
    T = NW + 1
    H16 = rel.shape[0]
    DK = C // H16
    E, _, HID = W1.shape
    J = HID // P
    assert B == P and C == 256 and GRID == 2 * CS and NW == 4 and E == 8

    LINES = CIN * PS
    CL = P // PS
    K = CL * PS
    NK = -(-LINES // CL)
    START = [min(k * CL, LINES - CL) for k in range(NK)]
    OVER = ((NK - 1) * CL - START[-1]) * PS
    CW = C + 2
    GROUPS = [(0, 3), (3, NK)]
    TOK = T * P
    HALF = TOK // 2
    KV_LAG = 2
    CEN_RING = KV_LAG + 1
    POOL_QUERIES = (1, 0)
    DVE_QUERIES = (2, 3, 4)
    PE_SUMS = (2, 1, 0)
    DVE_SUMS = (3, 4)
    XT_ORDER = (1, 2, 3, 4, 0)
    BLOCK = 2 * P
    MAX_BLOCKS = 2 * T * P // BLOCK + E - 1
    SPARE = MAX_BLOCKS * BLOCK
    BANKS = -(-T // 2)

    with ExitStack() as ctx:
        def sb(name, shape, dt=F32):
            return ctx.enter_context(nc.sbuf_tensor(name, shape, dt))

        def sem(name):
            return ctx.enter_context(nc.semaphore(name))

        psum = ctx.enter_context(nc.psum_tensor("psum", [P, 8, 512], F32))
        PATCH_BANK = (0, 1, 2)
        CONV_BANK = (3, 4)
        TURN_BANK = 5
        RESULT_BANK = (6, 7)
        WARM_BANK = 3
        XT_BANK = (4, 5, 6)
        HIDDEN_BANK = (0, 2)
        EXPERT_BANK = 4
        GATE_BANK = 7
        BIAS_BANK = 6

        ident = sb("ident", [P, P])
        minus_half = sb("minus_half", [P, 16])
        iota8i = sb("iota8i", [P, E], mybir.dt.int32)
        iota8 = sb("iota8", [P, E])
        wg_sb = sb("wg_sb", [P, KC, E])
        zeros = sb("zeros", [P, C])
        all_ones = sb("all_ones", [P, P])
        before = sb("before", [P, P])
        spare_i = sb("spare_i", [P, T], mybir.dt.int32)
        spare = sb("spare", [P, T])
        blocks_i = sb("blocks_i", [1, MAX_BLOCKS], mybir.dt.int32)
        block_no = sb("block_no", [1, MAX_BLOCKS])
        qkv_w = sb("qkv_w", [P, KC, 3 * C])
        rows_in = sb("rows_in", [E * J + 2 * KC, P])
        cols = sb("cols", [P, E * J + 2 * KC])
        b1_cols = cols[:, 0:E * J].rearrange("p (e j) -> p e j", e=E)
        kvg_cols = cols[:, E * J:E * J + KC]
        kvb_cols = cols[:, E * J + KC:E * J + 2 * KC]
        row = {name: sb("row_" + name, [P, width]) for name, width in (
            ("q_g", C), ("q_b", C), ("proj_b", C), ("gkv_g", C), ("gkv_b", C), ("gproj_b", C), ("mod_b", C),
            ("class", C), ("qkv_b", 3 * C), ("bg", E))}
        rel_rows = sb("rel_rows", [P, H16, 2 * T - 1])
        conv_mean = sb("conv_mean", [P, 2, NK])
        sumsq = sb("sumsq", [P, NW, NP + 1])
        var_eps = sb("var_eps", [P, NW, NP + 1])
        rstd = sb("rstd", [P, NW, NP + 1])
        mu9 = sb("mu9", [P, NW])
        qbk = sb("qbk", [P, H8])
        stat8 = sb("stat8", [P, 3, H8])
        bn = sb("bn", [P, T, 6])
        mv = sb("mv", [P, T, 2])
        ve = sb("ve", [P, T])
        rs = sb("rs", [P, T])
        gprob = sb("gprob", [P, NW, H8])
        gscore = sb("gscore", [P, 3, NW, H8])
        gstat = sb("gstat", [P, 3, H8])
        hs = sb("hs", [P, T, C])
        aq = sb("aq", [P, T, C])
        akv = sb("akv", [P, T, 2 * C])

        att_raw = sb("att_raw", [P, T, H16, T])

        tokenizer_memory = ExitStack()

        def sbt(name, shape, dt=F32):
            return tokenizer_memory.enter_context(nc.sbuf_tensor(name, shape, dt))

        lines = sbt("lines", [P, CS, LINES, IMG])
        patches = sbt("patches", [P, 3, LINES * PS])
        conv_hi = sbt("conv_hi", [P, NK, CW], F32R)
        conv_lo = sbt("conv_lo", [P, NK, CW], F32R)
        patch_hi = sbt("patch_hi", [P, 2, NK, P], F32R)
        patch_lo = sbt("patch_lo", [P, 2, NK, P], F32R)
        cen = sbt("cen", [P, CEN_RING, CW])
        wkv_hi = sbt("wkv_hi", [P, KC, 2 * C], F32R)
        wkv_lo = sbt("wkv_lo", [P, KC, 2 * C], F32R)
        turn_hi = sbt("turn_hi", [P, 2, C], F32R)
        turn_lo = sbt("turn_lo", [P, 2, C], F32R)
        kv = sbt("kv", [P, 2, NP, 2 * C])
        wq_sb = sbt("wq_sb", [P, KC, C])
        proj_sb = sbt("proj_sb", [P, KC, C])
        gwk_sb = sbt("gwk_sb", [P, KC, C])
        gwv_sb = sbt("gwv_sb", [P, KC, H8 + C])
        gproj_sb = sbt("gproj_sb", [P, KC, C])
        mod_sb = sbt("mod_sb", [P, KC, C])
        kv_bias = sbt("kv_bias", [P, 2 * C])
        turn_f = sbt("turn_f", [P, 3, C])
        res = sbt("res", [P, 3, C])
        qkv_res = sbt("qkv_res", [P, 3 * C])
        q_sb = sbt("q_sb", [P, 2, C])
        gq_sb = sbt("gq_sb", [P, C])
        redsum = sbt("redsum", [P, 2, CW])
        redp = sbt("redp", [P, 2, C])
        redln = sbt("redln", [P, C])
        score = sbt("score", [P, 3, NP, H8])
        probe = sbt("probe", [P, 2, NP, H8])
        agg = sbt("agg", [P, C])
        kvln = sbt("kvln", [P, C])
        gagg = sbt("gagg", [P, C])
        junk = sbt("junk", [P, C])
        work = sbt("work", [P, C])
        start_memory = ExitStack()

        def sbs(name, shape, dt=F32):
            return start_memory.enter_context(nc.sbuf_tensor(name, shape, dt))

        conv_raw = sbs("conv_raw", [P, KC, LINES * PS])
        wkv_raw = sbs("wkv_raw", [P, KC, 2 * C])
        kvb_wide = sbs("kvb_wide", [P, KC, P])
        gwq_sb = sbs("gwq_sb", [P, KC, C])
        row["gq_g"] = sbs("row_gq_g", [P, C])
        row["gq_b"] = sbs("row_gq_b", [P, C])
        class_ln = sbs("class_ln", [P, C])
        start_memory.close()
        prod = sbt("prod", [P, NP, C])
        gkv_sb = sbt("gkv_sb", [P, NW, H8 + C])
        local = sbt("local", [P, 2, C])
        tokenizer_memory.close()

        w1_raw = sb("w1_raw", [P, KC, HID])
        w2_raw = sb("w2_raw", [P, J, C])
        w1_hi, w1_lo, w2_hi, w2_lo = [], [], [], []
        for u in range(2):
            for parts, name, shape in ((w1_hi, "w1_hi", [P, KC, HID]), (w1_lo, "w1_lo", [P, KC, HID]),
                                       (w2_hi, "w2_hi", [P, J, C]), (w2_lo, "w2_lo", [P, J, C])):
                parts.append(sb(f"{name}{u}", shape, F32R))
        att_prod = sb("att_prod", [P, T, T, C])
        att_s = sb("att_s", [P, 3, T, H16, T])
        att_m = sb("att_m", [P, 3, T, H16])
        att_o = sb("att_o", [P, len(DVE_SUMS), C])
        h1 = sb("h1", [P, T, C])
        xt_f = sb("xt_f", [P, KC, TOK])
        xt_hi = sb("xt_hi", [P, KC, TOK], F32R)
        xt_lo = sb("xt_lo", [P, KC, TOK], F32R)
        g8 = sb("g8", [P, 6, T, E])
        gt = sb("gt", [P, 10, T])
        top_at = sb("top_at", [P, T, E], U32)
        gates = sb("gates", [P, T, E])
        gates_t = sb("gates_t", [T * E, P])
        b2_wide = sb("b2_wide", [T * E, T, C])
        choice = sb("choice", [P, 2, T, E])
        chosen = sb("chosen", [P, T + 1, E])
        later = sb("later", [P, E, E])
        need = sb("need", [P, 6, E])
        place = sb("place", [P, T, E])
        placed = sb("placed", [P, 2, T, E])
        found = sb("found", [P, 4, 2, T])
        row_to = sb("row_to", [P, 2, T], U32)
        row_from = sb("row_from", [P, 2, T], U32)
        passed = sb("passed", [1, MAX_BLOCKS, E])
        order = sb("order", [1, 2, MAX_BLOCKS + 1])
        table = sb("table", [1, MAX_BLOCKS + 1], mybir.dt.int32)
        x_block = sb("x_block", [P, 2, 2, C])
        xb_hi = sb("xb_hi", [P, 2, KC, BLOCK], F32R)
        xb_lo = sb("xb_lo", [P, 2, KC, BLOCK], F32R)
        y_block = sb("y_block", [P, 2, 2, C])
        acc = sb("acc", [P, T, C])
        h_f = sb("h_f", [P, 2, TOK])
        h_hi = sb("h_hi", [P, 2, TOK], F32R)
        h_lo = sb("h_lo", [P, 2, TOK], F32R)
        fin = h1

        first_loaded = sem("first_loaded")
        early_loaded = sem("early_loaded")
        wkv_loaded = sem("wkv_loaded")
        late_loaded = sem("late_loaded")
        lines_loaded = [sem(f"lines_loaded_{r}") for r in range(CS)]
        w1_loaded = sem("w1_loaded")
        w2_loaded = sem("w2_loaded")
        stored = sem("stored")
        ident_made = sem("ident_made")
        consts_made = sem("consts_made")
        conv_w_turned = sem("conv_w_turned")
        conv_w_centred = sem("conv_w_centred")
        conv_w_split = sem("conv_w_split")
        conv_mean_made = sem("conv_mean_made")
        conv_hi_done = sem("conv_hi_done")
        cols_turned = sem("cols_turned")
        cols_copied = sem("cols_copied")
        kvb_widened = sem("kvb_widened")
        kv_bias_made = sem("kv_bias_made")
        kv_bias_copied = sem("kv_bias_copied")
        wkv_split = sem("wkv_split")
        patches_gathered = sem("patches_gathered")
        patch_turned = sem("patch_turned")
        patch_hi_done = sem("patch_hi_done")
        patch_lo_done = sem("patch_lo_done")
        conv_done = sem("conv_done")
        cen_copied = sem("cen_copied")
        sumsq_done = sem("sumsq_done")
        red_summed = sem("red_summed")
        turned = sem("turned")
        turn_copied = sem("turn_copied")
        turn_lo_done = sem("turn_lo_done")
        projected = sem("projected")
        result_copied = sem("result_copied")
        var_done = sem("var_done")
        rstd_done = sem("rstd_done")
        last_rstd_done = sem("last_rstd_done")
        redln_done = sem("redln_done")
        redp_done = sem("redp_done")
        pool_scored = sem("pool_scored")
        pool_weighed = sem("pool_weighed")
        shifted = sem("shifted")
        exp_done = sem("exp_done")
        probs_done = sem("probs_done")
        agg_done = sem("agg_done")
        local_done = sem("local_done")
        kvln_done = sem("kvln_done")
        class_ln_done = sem("class_ln_done")
        class_keys_done = sem("class_keys_done")
        gagg_done = sem("gagg_done")
        token_done = sem("token_done")
        qkv_done = sem("qkv_done")
        pool_paired = sem("pool_paired")
        pairs_scored = sem("pairs_scored")
        pool_valued = sem("pool_valued")
        dve_valued = sem("dve_valued")
        values_summed = sem("values_summed")
        h1_done = sem("h1_done")
        xt_copied = sem("xt_copied")
        xt_turned = sem("xt_turned")
        xt_split = sem("xt_split")
        gate_scored = sem("gate_scored")
        gates_done = sem("gates_done")
        gates_turned = sem("gates_turned")
        gates_t_copied = sem("gates_t_copied")
        zeros_made = sem("zeros_made")
        chosen_made = sem("chosen_made")
        ranked = sem("ranked")
        rows_found = sem("rows_found")
        x_cleared = sem("x_cleared")
        rows_sent = sem("rows_sent")
        x_loaded = [sem(f"x_loaded_{u}") for u in range(2)]
        x_turned = sem("x_turned")
        xb_hi_done = sem("xb_hi_done")
        xb_split = sem("xb_split")
        bank_free = sem("bank_free")
        y_stored = sem("y_stored")
        rows_fetched = [sem(f"rows_fetched_{i}") for i in range(T)]
        pool_lo_done = sem("pool_lo_done")
        dense_added = sem("dense_added")
        table_made = sem("table_made")
        b2_cleared = sem("b2_cleared")
        b2_loaded = sem("b2_loaded")
        gate_bias_done = sem("gate_bias_done")
        gate_bias_used = sem("gate_bias_used")
        w_hi_done = sem("w_hi_done")
        w_lo_done = sem("w_lo_done")
        hidden_done = sem("hidden_done")
        relu_done = sem("relu_done")
        h_hi_done = sem("h_hi_done")
        h_split = sem("h_split")
        hidden_used = sem("hidden_used")
        acc_ready = sem("acc_ready")
        fin_done = sem("fin_done")
        dve_chain = sem("dve_chain")
        pool_chain = sem("pool_chain")

        RED, QUERY, SCORE, WEIGH, SUM, PROJ = 10, 11, 13, 16, 18, 21
        LOCAL_STEP = (23, 32, 41, 50)
        MOD_STEP = (24, 33, 42, 51)
        GKV_STEP = (25, 34, 43, 52)
        TOKEN_STEP = (26, 35, 44, 53)
        QKV_STEP = (41, 43, 45, 54)
        TAKE_STEP = (44, 46, 47, 56)
        PAIR_STEP = (47, 51, 51, 57)
        WARM = {50: 4, 51: 4, 52: 4, 53: 6, 54: 6, 55: 4, 57: 4, 58: 4}
        WARM_ATTEND = 28
        WARM_TURN = 12
        CLASSQ = 8
        GATT = GKV_STEP[NW - 1] + 1
        CLASSO = GATT + 2
        SPLIT0 = NT + 2
        STEPS = CLASSO + 6

        def extras(s):
            found = [(kind, w) for w in range(NW) for kind, at in
                     (("query", QUERY), ("proj", PROJ)) if s == NP * w + at]
            found += [(kind, w) for kind, steps in (("gkv", GKV_STEP), ("mod", MOD_STEP), ("qkv", QKV_STEP))
                      for w in range(NW) if s == steps[w]]
            if s == CLASSQ:
                found.append(("gquery", 0))
            if s == CLASSO:
                found.append(("gproj", 0))
            if s == CLASSO + 3:
                found.append(("qkv", NW))
            return found

        turn_order = []
        result_order = []
        for s in range(STEPS):
            if 0 <= s - KV_LAG < NT:
                turn_order.append(("kv", s - KV_LAG))
            if 0 <= s - KV_LAG - 1 < NT:
                result_order.append(("kv", s - KV_LAG - 1, 0))
            for kind, w in extras(s - 1):
                result_order.append((kind, w, 0))
                if kind == "qkv":
                    result_order.append((kind, w, 1))
            turn_order += extras(s)
        kv_turns = [sum(k == "kv" for k, _ in turn_order[:i]) for i in range(len(turn_order) + 1)]
        plain_turns = [i - n for i, n in enumerate(kv_turns)]

        def copied(kind, w, part=0):
            return result_order.index((kind, w, part)) + 1

        def slot_of(t):
            w, n = divmod(t, NP)
            return n // CS, ((w % 2) * CS + n % CS) * PS

        VAR_ORDER = [found for s in range(STEPS) for found in
                     [("class", 0)] * (s == CLASSQ - 1)
                     + [("red", w) for w in range(NW) if s == NP * w + RED]
                     + [("local", w) for w in range(NW) if s == LOCAL_STEP[w]]]
        VAR_ORDER += ["attention", "attention_last", "output", "output_last"]
        DENSE = E - 2
        COUNT = MAX_BLOCKS
        PAIRS = (MAX_BLOCKS + 1) // 2
        x_rows = nc.dram_tensor("x_rows", [SPARE + TOK, C], F32, kind="Internal").ap()
        y_rows = nc.dram_tensor("y_rows", [SPARE, C], F32, kind="Internal").ap()
        LATE = 26
        POOL_PAIRS = 3

        def pairs_step(w):
            return PAIR_STEP[w] if w < NW else CLASSO + 5

        def pair_products(eng, w, own, a, b):
            if own:
                return eng.tensor_tensor(prod[:, 0:w + 1, :], akv[:, T - 1 - w:T, 0:C],
                                         aq[:, w, :].unsqueeze(1).broadcast_to([P, w + 1, C]), ALU.mult)
            return eng.tensor_tensor(prod[:, w + 1 + a:w + 1 + b, :], aq[:, a:b, :],
                                     akv[:, T - 1 - w, 0:C].unsqueeze(1).broadcast_to([P, b - a, C]), ALU.mult)

        def chunk(h, j):
            return h[:, j % 4 // 2, j % 2 * HALF:j % 2 * HALF + BLOCK]

        def weigh_tokens(eng, i):
            return eng.tensor_tensor(att_prod[:, i].rearrange("p j (h d) -> p j h d", h=H16),
                                     akv[:, :, C:2 * C].rearrange("p j (h d) -> p j h d", h=H16),
                                     att_s[:, 1, i].rearrange("p h j -> p j h").unsqueeze(3).broadcast_to(
                                         [P, T, H16, DK]), ALU.mult)

        block = ctx.enter_context(nc.Block())

        @block.sync
        def _(sp):
            rows_of = x.rearrange("b c (r k) x -> r b c (k x)", k=PS)

            def load_lines(hy, r):
                sp.dma_start(lines[:, r].rearrange("p (c k) x -> p c (k x)", c=CIN),
                             rows_of[hy * CS + r]).then_inc(lines_loaded[r], 16)

            def load(dst, src, which):
                sp.dma_start(dst, src).then_inc(which, 16)

            load(conv_raw[:], conv_w.rearrange("(h o) c y x -> o h (c y x)", o=P), first_loaded)
            load(rows_in[0:E * J], b1.rearrange("e (j p) -> (e j) p", p=P), early_loaded)
            load(rows_in[E * J:E * J + KC], kv_g.rearrange("(k p) -> k p", p=P), early_loaded)
            load(rows_in[E * J + KC:E * J + 2 * KC], kv_b.rearrange("(k p) -> k p", p=P), early_loaded)
            load_lines(0, 0)
            load(wkv_raw[:], wkv.rearrange("(k p) n -> p k n", p=P), wkv_loaded)
            load_lines(0, 1)
            load_lines(0, 2)
            for name, src in (("class", class_emb), ("gq_g", gq_g), ("gq_b", gq_b), ("q_g", q_g), ("q_b", q_b),
                              ("proj_b", proj_b), ("gkv_g", gkv_g), ("gkv_b", gkv_b), ("gproj_b", gproj_b),
                              ("mod_b", mod_b), ("bg", bg)):
                load(row[name][:], src.partition_broadcast(P), late_loaded)
            for dst, src in ((gwq_sb[:], gwq), (wq_sb[:], wq), (proj_sb[:], proj_w), (gwk_sb[:], gwkv[:, 0:C]), (gwv_sb[:, :, H8:], gwkv[:, C:2 * C]),
                             (mod_sb[:], mod_w), (gproj_sb[:], gproj_w), (qkv_w[:, :, 0:C], aWq),
                             (qkv_w[:, :, C:2 * C], aWk), (qkv_w[:, :, 2 * C:3 * C], aWv), (wg_sb[:], Wg)):
                load(dst, src.rearrange("(k p) n -> p k n", p=P), late_loaded)
            for n, src in enumerate((abq, abk, abv)):
                load(row["qkv_b"][:, n * C:(n + 1) * C], src.partition_broadcast(P), late_loaded)
            load(rel_rows[:], rel[:, 0:2 * T - 1].partition_broadcast(P), late_loaded)
            sp.wait_ge(zeros_made, 1)
            for scratch, cleared in ((x_rows, x_cleared), (y_rows, y_stored)):
                n = scratch.shape[0] // P
                sp.dma_start(scratch.rearrange("(n p) c -> p n c", p=P), zeros[:].unsqueeze(1).broadcast_to([P, n, C])
                             ).then_inc(cleared, 16)
            for r in range(CS):
                sp.wait_ge(patches_gathered, NP + CS * r + CS)
                load_lines(1, r)
            sp.wait_ge(patches_gathered, NT)
            sp.dma_start(w1_raw[:], W1[DENSE].rearrange("(k p) h -> p k h", p=P)).then_inc(w1_loaded, 16)
            sp.dma_start(w2_raw[:], W2[DENSE].rearrange("(j p) c -> p j c", p=P)).then_inc(w2_loaded, 16)
            w1_rows = W1.rearrange("e (k p) h -> e p k h", p=P)
            w2_rows = W2.rearrange("e (j p) c -> e p j c", p=P)

            def load_weights(k, e, first=False):
                for n, (raw, rows, loaded) in enumerate(((w1_raw, w1_rows, w1_loaded), (w2_raw, w2_rows, w2_loaded))):
                    if first:
                        sp.wait_ge(pool_lo_done, J // 2 * (n + 1))
                    else:
                        sp.wait_ge(w_lo_done, J // 2 * (k - 2) + J // 4 * (n + 1))
                    sp.dma_start(raw[:], rows[bass.ds(e, 1)].rearrange("e p k h -> (e p) k h")).then_inc(loaded, 16)

            load_weights(1, E - 1, first=True)
            sp.wait_ge(b2_cleared, 1)
            for i in range(T):
                sp.dma_start(b2_wide[i * E:(i + 1) * E, i, :], b2).then_inc(b2_loaded, 16)
            x_of_block = x_rows[0:SPARE].rearrange("(b a p) c -> b p a c", a=2, p=P)

            def load_tokens(b, u):
                sp.dma_start(x_block[:, u], x_of_block[bass.ds(b, 1)].rearrange("b p a c -> (b p) a c")
                             ).then_inc(x_loaded[u], 16)

            y_of_block = y_rows.rearrange("(b a p) c -> b p a c", a=2, p=P)

            def store_outputs(b, u):
                sp.wait_ge(bank_free, b + 3)
                sp.dma_start(y_of_block[bass.ds(b, 1)].rearrange("b p a c -> (b p) a c"), y_block[:, u]
                             ).then_inc(y_stored, 16)

            sp.wait_ge(rows_sent, 16 * 2 * T)
            load_tokens(0, 0)
            sp.wait_ge(table_made, 1)

            def expert_at(b):
                return sp.value_load(table[0:1, bass.ds(b, 1)], min_val=0, max_val=E - 1)

            load_tokens(1, 1)
            load_weights(2, expert_at(1))
            loops = sp.value_load(table[0:1, COUNT:COUNT + 1], min_val=1, max_val=PAIRS - 1)
            with sp.Fori(0, loops) as i:
                for u in range(2):
                    e = expert_at(2 * i + 2 + u)
                    sp.wait_ge(x_turned, 2 * i + 1 + u)
                    load_tokens(2 * i + 2 + u, u)
                    load_weights(2 * i + 3 + u, e)
                    store_outputs(2 * i + u, u)
            store_outputs(2 * loops, 0)
            store_outputs(2 * loops + 1, 1)
            for i in range(T):
                sp.wait_ge(fin_done, i + 1)
                sp.dma_start(out[:, i, :], fin[:, i, :]).then_inc(stored, 16)
            sp.wait_ge(stored, 16 * T)

        def piece(j):
            if j < J // 2:
                k, h = divmod(j, J // 2 // KC)
                wide = HID * KC // (J // 2)
                cut = slice(h * wide, (h + 1) * wide)
                return w1_raw[:, k, cut], lambda u: w1_hi[u][:, k, cut], lambda u: w1_lo[u][:, k, cut]
            a = (j - J // 2) * 2
            return w2_raw[:, a:a + 2, :], lambda u: w2_hi[u][:, a:a + 2, :], lambda u: w2_lo[u][:, a:a + 2, :]

        @block.scalar
        def _(act):
            act.wait_ge(cols_turned, 1)
            nc.scalar.activation(cols[:], psum[:, RESULT_BANK[0], 0:E * J + 2 * KC], ACT.Copy).then_inc(cols_copied, 1)
            act.wait_ge(conv_mean_made, 1)
            for k in range(NK):
                nc.scalar.activation(conv_hi[0:K, k, 0:C], psum[0:K, k, 0:C], ACT.Identity,
                                     bias=conv_mean[0:K, 1, k:k + 1]).then_inc(conv_hi_done, 1)

            def patch_highs(t):
                if t >= 2:
                    act.wait_ge(conv_done, t - 1)
                for g, (a, b) in enumerate(GROUPS):
                    act.wait_ge(patch_turned, 2 * t + g + 1)
                    nc.scalar.activation(patch_hi[0:K, t % 2, a:b, :],
                                         psum[0:K, PATCH_BANK[(2 * t + g) % 3], 0:(b - a) * P],
                                         ACT.Copy).then_inc(patch_hi_done, 1)

            def copy_centred(t):
                act.wait_ge(conv_done, t + 1)
                if t >= CEN_RING:
                    act.wait_ge(turned, turn_order.index(("kv", t - CEN_RING)) + 1)
                    act.wait_ge(sumsq_done, t - CEN_RING + 1)
                    act.wait_ge(red_summed, t - CEN_RING + 1)
                nc.scalar.activation(cen[:, t % CEN_RING, :], psum[:, CONV_BANK[t % 2], 0:CW], ACT.Copy).then_inc(cen_copied, 1)

            def copy_turned(item):
                i = turn_order.index(item)
                act.wait_ge(turned, i + 1)
                if item[0] == "kv":
                    if item[1] >= 2:
                        act.wait_ge(projected, result_order.index(("kv", item[1] - 2, 0)) + 1)
                    dst = turn_hi[:, item[1] % 2, :]
                else:
                    dst = turn_f[:, plain_turns[i] % 3, :]
                nc.scalar.activation(dst, psum[:, TURN_BANK, 0:C], ACT.Copy).then_inc(turn_copied, 1)

            def copy_result(kind, w, part):
                i = result_order.index((kind, w, part))
                act.wait_ge(projected, i + 1)
                src = psum[:, RESULT_BANK[i % 2], :]
                if kind == "kv":
                    v, n = divmod(w, NP)
                    if v >= 2 and n == 0:
                        act.wait_ge(agg_done, v - 1)
                        act.wait_ge(pool_weighed, v - 1)
                    nc.scalar.activation(kv[:, v % 2, n, :], src, ACT.Copy).then_inc(result_copied, 1)
                elif kind == "query":
                    nc.scalar.activation(q_sb[:, w % 2, :], src[:, 0:C], ACT.Copy, scale=C ** -0.5
                                         ).then_inc(result_copied, 1)
                elif kind == "gquery":
                    nc.scalar.activation(gq_sb[:], src[:, 0:C], ACT.Copy, scale=C ** -0.5).then_inc(result_copied, 1)
                elif kind == "gkv":
                    nc.scalar.activation(gkv_sb[:, w, :], src[:, 0:H8 + C], ACT.Copy).then_inc(result_copied, 1)
                elif kind == "qkv":
                    dst = qkv_res[:, 0:2 * C] if part == 0 else qkv_res[:, 2 * C:3 * C]
                    if w >= 1:
                        act.wait_ge(qkv_done, w)
                    nc.scalar.activation(dst, src[:, 0:dst.shape[1]], ACT.Copy).then_inc(result_copied, 1)
                else:
                    nc.scalar.activation(res[:, ("proj", "mod", "gproj").index(kind), :], src[:, 0:C],
                                         ACT.Copy).then_inc(result_copied, 1)

            for s in range(STEPS):
                if s < NT:
                    patch_highs(s)
                if s == 0:
                    act.wait_ge(kv_bias_made, 1)
                    nc.scalar.activation(kv_bias[:], psum[:, RESULT_BANK[1], :], ACT.Copy).then_inc(kv_bias_copied, 1)
                if 0 <= s - KV_LAG < NT:
                    copy_turned(("kv", s - KV_LAG))
                if 0 <= s - 1 < NT:
                    copy_centred(s - 1)
                if 0 <= s - KV_LAG - 1 < NT:
                    copy_result("kv", s - KV_LAG - 1, 0)
                for kind, w in extras(s - 1):
                    copy_result(kind, w, 0)
                    if kind == "qkv":
                        copy_result(kind, w, 1)
                for item in extras(s):
                    copy_turned(item)
                for w in range(NW):
                    if s == NP * w + SCORE + 2:
                        act.wait_ge(shifted, w + 1)
                        nc.scalar.activation(score[:, 2], score[:, 1], ACT.Exp).then_inc(exp_done, 1)
                if SPLIT0 <= s < SPLIT0 + J:
                    j = s - SPLIT0
                    act.wait_ge(w1_loaded if j < J // 2 else w2_loaded, 16)
                    raw, hi, _ = piece(j)
                    nc.scalar.activation(hi(0), raw, ACT.Copy).then_inc(w_hi_done, 1)
                if s == GATT:
                    act.wait_ge(shifted, NW + 1)
                    nc.scalar.activation(gscore[:, 2], gscore[:, 1], ACT.Exp).then_inc(exp_done, 1)

            act.wait_ge(shifted, NW + 2)
            nc.scalar.activation(att_s[:, 2], att_s[:, 1], ACT.Exp).then_inc(exp_done, 1)
            for n, i in enumerate(XT_ORDER):
                act.wait_ge(xt_turned, n + 1)
                src = psum[:, XT_BANK[n % 3], 0:C].rearrange("p (k t) -> p k t", k=KC)
                nc.scalar.activation(xt_hi[:, :, i * P:(i + 1) * P], src, ACT.Copy)
                nc.scalar.activation(xt_f[:, :, i * P:(i + 1) * P], src, ACT.Copy).then_inc(xt_copied, 1)
            act.wait_ge(shifted, NW + 3)
            nc.scalar.activation(g8[:, 2], g8[:, 1], ACT.Exp).then_inc(exp_done, 1)

            def relu(j):
                act.wait_ge(hidden_done, j + 1)
                if j >= 2:
                    act.wait_ge(h_split, j - 1)
                b = HIDDEN_BANK[j % 2]
                nc.scalar.activation(h_f[:, j % 2, :].rearrange("p (a t) -> p a t", a=2),
                                     psum[:, b:b + 2, 0:HALF], ACT.Relu,
                                     bias=b1_cols[:, DENSE, j:j + 1]).then_inc(relu_done, 1)

            def block_relu(k, e, j):
                act.wait_ge(hidden_done, J * k + j + 1)
                act.wait_ge(h_split, J * k + j - 3)
                nc.scalar.activation(chunk(h_f, j), psum[:, j % 4, 0:BLOCK], ACT.Relu,
                                     bias=b1_cols[:, bass.ds(e, 1), j]).then_inc(relu_done, 1)

            def split_high(k, u, j):
                raw, hi, _ = piece(j)
                if j == 0:
                    act.wait_ge(w1_loaded, 16 * k + 16)
                if j == J // 2:
                    act.wait_ge(w2_loaded, 16 * k + 16)
                nc.scalar.activation(hi(u), raw, ACT.Copy).then_inc(w_hi_done, 1)

            def pair_exp():
                act.wait_ge(shifted, NW + 4)
                nc.scalar.activation(gt[:, 6], gt[:, 5], ACT.Exp).then_inc(exp_done, 1)

            def tokens_high(b, u):
                act.wait_ge(x_turned, b + 1)
                nc.scalar.activation(xb_hi[:, u], psum[:, GATE_BANK, :].rearrange("p (k t) -> p k t", k=KC), ACT.Copy
                                     ).then_inc(xb_hi_done, 1)

            def copy_outputs(b, u):
                act.wait_ge(hidden_used, J * (b + 2))
                act.wait_ge(y_stored, 16 * b + 16)
                nc.scalar.activation(y_block[:, u], psum[:, EXPERT_BANK + u, :].rearrange("p (a c) -> p a c", a=2),
                                     ACT.Copy).then_inc(bank_free, 1)

            def expert_at(b):
                return act.value_load(table[0:1, bass.ds(b, 1)], min_val=0, max_val=E - 1)

            def block(b, u, more=True):
                e = expert_at(b)
                for j in range(2, J):
                    block_relu(b + 1, e, j)
                    if more:
                        split_high(b + 2, u, j - 2)
                        if j == 5:
                            tokens_high(b + 1, 1 - u)
                if more:
                    next_e = expert_at(b + 1)
                    for j in range(2):
                        block_relu(b + 2, next_e, j)
                        split_high(b + 2, u, J - 2 + j)
                copy_outputs(b, u)

            pair_exp()
            for j in range(J):
                relu(j)
                split_high(1, 1, j)
            tokens_high(0, 0)
            for j in range(2):
                block_relu(1, E - 1, j)
            act.wait_ge(table_made, 1)
            loops = act.value_load(table[0:1, COUNT:COUNT + 1], min_val=1, max_val=PAIRS - 1)
            with act.Fori(0, loops) as i:
                block(2 * i, 0)
                block(2 * i + 1, 1)
            block(2 * loops, 0)
            block(2 * loops + 1, 1, more=False)

        @block.tensor
        def _(pe):
            pe.wait_ge(ident_made, 1)
            pe.wait_ge(first_loaded, 16)
            for k in range(NK):
                for h in range(KC):
                    last = nc.tensor.transpose(psum[0:K, k, h * P:(h + 1) * P],
                                               conv_raw[:, h, START[k] * PS:START[k] * PS + K], ident[:])
            last.then_inc(conv_w_turned, 1)
            pe.wait_ge(early_loaded, 16 * 3)
            n = E * J + 2 * KC
            nc.tensor.transpose(psum[:, RESULT_BANK[0], 0:n], rows_in[:], ident[0:n, 0:n]).then_inc(cols_turned, 1)

            def kv_bias_product():
                pe.wait_ge(kvb_widened, 1)
                pe.wait_ge(wkv_loaded, 16)
                for k in range(KC):
                    last = nc.tensor.matmul(psum[:, RESULT_BANK[1], :], kvb_wide[:, k, :], wkv_raw[:, k, :],
                                            start=(k == 0), stop=(k == KC - 1))
                last.then_inc(kv_bias_made, 1)

            def turn_patches(t):
                pe.wait_ge(patches_gathered, t + 1)
                for g, (a, b) in enumerate(GROUPS):
                    bank = PATCH_BANK[(2 * t + g) % 3]
                    if 2 * t + g < 3:
                        pe.wait_ge(conv_w_centred, 2 * t + g + 1)
                    else:
                        pe.wait_ge(patch_lo_done, 2 * t + g - 2)
                    for k in range(a, b):
                        last = nc.tensor.transpose(psum[0:K, bank, (k - a) * P:(k - a + 1) * P],
                                                   patches[:, t % 3, START[k] * PS:START[k] * PS + K], ident[:])
                    last.then_inc(patch_turned, 1)

            def convolve(t):
                pe.wait_ge(patch_lo_done, 2 * t + 2)
                if t == 0:
                    pe.wait_ge(conv_w_split, 2)
                if t >= 2:
                    pe.wait_ge(cen_copied, t - 1)
                dst = psum[:, CONV_BANK[t % 2], 0:CW]
                passes = [(p, w) for k in range(NK) for p, w in
                          ((patch_hi[0:K, t % 2, k, :], conv_hi[0:K, k, :]),
                           (patch_hi[0:K, t % 2, k, :], conv_lo[0:K, k, :]),
                           (patch_lo[0:K, t % 2, k, :], conv_hi[0:K, k, :]))]
                for m, (p, w) in enumerate(passes):
                    last = nc.tensor.matmul(dst, p, w, start=(m == 0), stop=(m == len(passes) - 1))
                last.then_inc(conv_done, 1)

            def turn(item):
                i = turn_order.index(item)
                kind, w = item
                if i >= 1:
                    pe.wait_ge(turn_copied, i)
                    if turn_order[i - 1][0] == "kv":
                        pe.wait_ge(turn_lo_done, kv_turns[i])
                if kind == "kv":
                    pe.wait_ge(cen_copied, w + 1)
                    src = cen[:, w % CEN_RING, 0:C]
                elif kind == "query":
                    pe.wait_ge(redln_done, w + 1)
                    src = redln[:]
                elif kind == "proj":
                    pe.wait_ge(agg_done, w + 1)
                    src = agg[:]
                elif kind == "mod":
                    pe.wait_ge(local_done, w + 1)
                    src = local[:, w % 2, :]
                elif kind == "gkv":
                    pe.wait_ge(kvln_done, w + 1)
                    src = kvln[:]
                elif kind == "gquery":
                    pe.wait_ge(class_ln_done, 1)
                    src = class_ln[:]
                elif kind == "gproj":
                    pe.wait_ge(gagg_done, 1)
                    src = gagg[:]
                else:
                    pe.wait_ge(token_done, w + 1)
                    src = hs[:, w, :]
                for k in range(KC):
                    last = nc.tensor.transpose(psum[:, TURN_BANK, k * P:(k + 1) * P],
                                               src[:, k * P:(k + 1) * P], ident[:])
                last.then_inc(turned, 1)

            def project(kind, w, part):
                i = result_order.index((kind, w, part))
                ti = turn_order.index((kind, w))
                pe.wait_ge(turn_copied, ti + 1)
                if i >= 2:
                    pe.wait_ge(result_copied, i - 1)
                elif i == 0:
                    pe.wait_ge(cols_copied, 1)
                else:
                    pe.wait_ge(kv_bias_copied, 1)
                bank = RESULT_BANK[i % 2]
                if kind == "kv":
                    pe.wait_ge(turn_lo_done, w + 1)
                    if w == 0:
                        pe.wait_ge(wkv_split, 1)
                    b = w % 2
                    passes = [(p, wt) for k in range(KC) for p, wt in
                              ((turn_hi[:, b, k * P:(k + 1) * P], wkv_hi[:, k, :]),
                               (turn_hi[:, b, k * P:(k + 1) * P], wkv_lo[:, k, :]),
                               (turn_lo[:, b, k * P:(k + 1) * P], wkv_hi[:, k, :]))]
                    width = 2 * C
                else:
                    b = plain_turns[ti] % 3
                    wt, width = {"query": (wq_sb[:], C), "proj": (proj_sb[:], C), "mod": (mod_sb[:], C),
                                 "gkv": (gwv_sb[:], H8 + C), "gquery": (gwq_sb[:], C), "gproj": (gproj_sb[:], C),
                                 "qkv": (qkv_w[:, :, 0:2 * C] if part == 0 else qkv_w[:, :, 2 * C:3 * C],
                                         2 * C if part == 0 else C)}[kind]
                    passes = [(turn_f[:, b, k * P:(k + 1) * P], wt[:, k, :]) for k in range(KC)]
                if kind == "gkv" and w == 0:
                    pe.wait_ge(class_keys_done, 1)
                for m, (p, m_w) in enumerate(passes):
                    last = nc.tensor.matmul(psum[:, bank, 0:width], p, m_w, start=(m == 0),
                                            stop=(m == len(passes) - 1))
                last.then_inc(projected, 1)

            def keep_warm(n):
                for _ in range(n):
                    nc.tensor.matmul(psum[:, WARM_BANK, 0:P], ident[:], ident[:], start=True, stop=True)

            for s in range(STEPS):
                if s < NT:
                    turn_patches(s)
                if s == 0:
                    kv_bias_product()
                if s == CLASSQ:
                    pe.wait_ge(late_loaded, 16 * LATE)
                if 0 <= s - KV_LAG < NT:
                    turn(("kv", s - KV_LAG))
                if 0 <= s - 1 < NT:
                    convolve(s - 1)
                if 0 <= s - KV_LAG - 1 < NT:
                    project("kv", s - KV_LAG - 1, 0)
                for kind, w in extras(s - 1):
                    project(kind, w, 0)
                    if kind == "qkv":
                        project(kind, w, 1)
                for item in extras(s):
                    turn(item)
                keep_warm(WARM.get(s, 0))
            keep_warm(WARM_ATTEND)

            for n, i in enumerate(PE_SUMS):
                if i in POOL_QUERIES:
                    pe.wait_ge(pool_valued, POOL_QUERIES.index(i) + 1)
                else:
                    pe.wait_ge(dve_valued, DVE_QUERIES.index(i) + 1)
                pe.wait_ge(token_done, T)
                nc.tensor.matmul(psum[:, n, 0:C], ident[:], hs[:, i, :], start=True, stop=False)
                for j in range(T):
                    last = nc.tensor.matmul(psum[:, n, 0:C], ident[:], att_prod[:, i, j, :], start=False,
                                            stop=(j == T - 1))
                last.then_inc(values_summed, 1)

            keep_warm(WARM_TURN)

            for n, i in enumerate(XT_ORDER):
                pe.wait_ge(h1_done, n + 1)
                if n >= 3:
                    pe.wait_ge(xt_copied, n - 2)
                    pe.wait_ge(xt_split, n - 2)
                for k in range(KC):
                    last = nc.tensor.transpose(psum[:, XT_BANK[n % 3], k * P:(k + 1) * P],
                                               h1[:, i, k * P:(k + 1) * P], ident[:])
                last.then_inc(xt_turned, 1)
            pe.wait_ge(xt_copied, T)
            for i in range(T):
                for k in range(KC):
                    last = nc.tensor.matmul(psum[:, GATE_BANK, i * E:(i + 1) * E],
                                            xt_f[:, k, i * P:(i + 1) * P], wg_sb[:, k, :],
                                            start=(k == 0), stop=(k == KC - 1))
            last.then_inc(gate_scored, 1)
            pe.wait_ge(xt_split, T)

            def hidden(j):
                if j >= 2:
                    pe.wait_ge(relu_done, j - 1)
                b = HIDDEN_BANK[j % 2]
                cut = slice(j * P, (j + 1) * P)
                passes = [(w, xt) for k in range(KC) for w, xt in
                          ((w1_hi[0][:, k, cut], xt_hi[:, k, :]), (w1_hi[0][:, k, cut], xt_lo[:, k, :]),
                           (w1_lo[0][:, k, cut], xt_hi[:, k, :]))]
                for m, (w, xt) in enumerate(passes):
                    for a in range(2):
                        last = nc.tensor.matmul(psum[:, b + a, 0:HALF], w, xt[:, a * HALF:(a + 1) * HALF],
                                                start=(m == 0), stop=(m == len(passes) - 1))
                last.then_inc(hidden_done, 1)

            def outer(j):
                pe.wait_ge(h_split, j + 1)
                if j == 0:
                    pe.wait_ge(pool_lo_done, J)
                for i in range(T):
                    dst = psum[:, EXPERT_BANK + i // 2, (i % 2) * C:(i % 2 + 1) * C]
                    cut = slice(i * P, (i + 1) * P)
                    passes = ((h_hi[:, j % 2, cut], w2_hi[0][:, j, :]), (h_hi[:, j % 2, cut], w2_lo[0][:, j, :]),
                              (h_lo[:, j % 2, cut], w2_hi[0][:, j, :]))
                    for m, (h, w) in enumerate(passes):
                        last = nc.tensor.matmul(dst, h, w, start=(j == 0 and m == 0 and i % 2 == 0),
                                                stop=(j == J - 1 and m == 2), skip_group_check=True)
                last.then_inc(hidden_used, 1)

            def turn_tokens(b, u):
                pe.wait_ge(x_loaded[u], 8 * b + 16 - 8 * u)
                for k in range(KC):
                    for a in range(2):
                        last = nc.tensor.transpose(psum[:, GATE_BANK, k * BLOCK + a * P:k * BLOCK + (a + 1) * P],
                                                   x_block[:, u, a, k * P:(k + 1) * P], ident[:])
                last.then_inc(x_turned, 1)

            def block_hidden(b, u, j):
                if j == 0:
                    pe.wait_ge(xb_split, b + 1)
                    pe.wait_ge(w_lo_done, J // 2 * b + J // 4)
                pe.wait_ge(relu_done, J * b + J + j - 3)
                w_u = 1 - u
                cut = slice(j * P, (j + 1) * P)
                passes = [(w, xt) for k in range(KC) for w, xt in
                          ((w1_hi[w_u][:, k, cut], xb_hi[:, u, k, :]), (w1_hi[w_u][:, k, cut], xb_lo[:, u, k, :]),
                           (w1_lo[w_u][:, k, cut], xb_hi[:, u, k, :]))]
                for m, (w, xt) in enumerate(passes):
                    last = nc.tensor.matmul(psum[:, j % 4, 0:BLOCK], w, xt, start=(m == 0), stop=(m == len(passes) - 1))
                last.then_inc(hidden_done, 1)

            def block_outer(b, u, j):
                pe.wait_ge(h_split, J * b + J + j + 1)
                if j == 0:
                    pe.wait_ge(bank_free, b + 1)
                if j in (0, J // 2):
                    pe.wait_ge(w_lo_done, J // 2 * b + (3 if j == 0 else 4))
                w_u = 1 - u
                for a in range(2):
                    cut = slice(a * P, (a + 1) * P)
                    for m, (h, w) in enumerate(((h_hi, w2_hi), (h_hi, w2_lo), (h_lo, w2_hi))):
                        last = nc.tensor.matmul(psum[:, EXPERT_BANK + u, a * C:(a + 1) * C], chunk(h, j)[:, cut],
                                                w[w_u][:, j, :], start=(j == 0 and m == 0 and a == 0),
                                                stop=(j == J - 1 and m == 2), skip_group_check=True)
                last.then_inc(hidden_used, 1)

            def second_bias(tiles):
                cut = slice(tiles[0], tiles[-1] + 1)
                nc.tensor.matmul(psum[:, BIAS_BANK, 0:len(tiles) * C], gates_t[:],
                                 b2_wide[:, cut, :].rearrange("r t c -> r (t c)"),
                                 start=True, stop=True).then_inc(gate_bias_done, 1)

            def rank_tokens():
                pe.wait_ge(chosen_made, 1)
                for n in range(T + 1):
                    last = nc.tensor.matmul(psum[:, GATE_BANK, n * E:(T + 1) * E], before[:] if n == 0 else all_ones[:],
                                            chosen[:, 0:T + 1 - n, :].rearrange("p t e -> p (t e)"),
                                            start=(n == 0), stop=(n == T), skip_group_check=True)
                last.then_inc(ranked, 1)

            pe.wait_ge(pool_lo_done, J // 2)
            hidden(0)
            for j in range(1, J):
                hidden(j)
                outer(j - 1)
                if j == 1:
                    rank_tokens()
                if j == 3:
                    pe.wait_ge(gates_done, 1)
                    pe.wait_ge(rows_found, 1)
                    nc.tensor.transpose(psum[0:T * E, GATE_BANK, 0:P], gates.rearrange("p t e -> p (t e)"), ident[:]
                                        ).then_inc(gates_turned, 1)
            pe.wait_ge(gates_t_copied, 1)
            turn_tokens(0, 0)
            outer(J - 1)
            block_hidden(0, 0, 0)
            block_hidden(0, 0, 1)

            def block(b, u, more=True, beside=lambda j: None):
                for j in range(2, J):
                    block_hidden(b, u, j)
                    block_outer(b, u, j - 2)
                    if more and j == 5:
                        pe.wait_ge(xb_split, b + 1)
                        turn_tokens(b + 1, 1 - u)
                    beside(j)
                for j in range(2):
                    if more:
                        block_hidden(b + 1, 1 - u, j)
                    block_outer(b, u, J - 2 + j)

            def beside(n):
                if n == 2:
                    pe.wait_ge(b2_loaded, 16 * T)
                    pe.wait_ge(dense_added, T - 2)
                    second_bias(range(0, 2))
                if n == 7:
                    pe.wait_ge(gate_bias_used, 1)
                    second_bias(range(2, 4))
                if n == J + 4:
                    pe.wait_ge(gate_bias_used, 2)
                    second_bias(range(4, T))

            pe.wait_ge(table_made, 1)
            loops = pe.value_load(table[0:1, COUNT:COUNT + 1], min_val=1, max_val=PAIRS - 1)
            with pe.Fori(0, loops) as i:
                block(2 * i, 0)
                block(2 * i + 1, 1)
            block(2 * loops, 0, beside=beside)
            block(2 * loops + 1, 1, more=False, beside=lambda j: beside(J + j))

        @block.gpsimd
        def _(pool):
            chain = [0]

            def link(ins):
                chain[0] += 1
                ins.then_inc(pool_chain, 1)
                pool.wait_ge(pool_chain, chain[0])

            link(nc.gpsimd.memset(ident[:], 0.0))
            nc.gpsimd.affine_select(out=ident[:], in_=ident[:], compare_op=ALU.not_equal, fill=1.0, base=0,
                                    pattern=[[-1, P]], channel_multiplier=1).then_inc(ident_made, 1)
            nc.gpsimd.memset(minus_half[:], -0.5)
            link(nc.gpsimd.memset(before[:], 1.0))
            link(nc.gpsimd.affine_select(out=before[:], in_=before[:], compare_op=ALU.is_gt, fill=0.0, base=0,
                                         pattern=[[1, P]], channel_multiplier=-1))
            nc.gpsimd.memset(all_ones[:], 1.0)
            nc.gpsimd.memset(zeros[:], 0.0).then_inc(zeros_made, 1)
            link(nc.gpsimd.iota(spare_i[:], pattern=[[P, T]], base=SPARE, channel_multiplier=1))
            link(nc.gpsimd.tensor_copy(spare[:], spare_i[:]))
            link(nc.gpsimd.iota(blocks_i[:], pattern=[[1, MAX_BLOCKS]], base=0, channel_multiplier=0))
            link(nc.gpsimd.tensor_copy(block_no[:], blocks_i[:]))
            nc.gpsimd.iota(iota8i[:], pattern=[[1, E]], base=0, channel_multiplier=0).then_inc(consts_made, 1)
            pool.wait_ge(consts_made, 1)
            nc.gpsimd.tensor_copy(iota8[:], iota8i[:]).then_inc(consts_made, 1)
            def power(dst, src, done):
                nc.gpsimd.tensor_tensor(dst, src, minus_half[:, 0:src.shape[1]], ALU.pow).then_inc(done, 1)

            def sum_reduced(t):
                w, n = divmod(t, NP)
                pool.wait_ge(cen_copied, t + 1)
                if n == 0:
                    nc.gpsimd.tensor_copy(redsum[:, w % 2, :], cen[:, t % CEN_RING, :]).then_inc(red_summed, 1)
                else:
                    pool.wait_ge(red_summed, t)
                    nc.gpsimd.tensor_tensor(redsum[:, w % 2, :], redsum[:, w % 2, :], cen[:, t % CEN_RING, :], ALU.add
                                            ).then_inc(red_summed, 1)

            def gather_patches(t):
                r, col = slot_of(t)
                w, n = divmod(t, NP)
                if n % CS == 0:
                    pool.wait_ge(lines_loaded[r], 16 * (w // 2 + 1))
                if t >= 3:
                    pool.wait_ge(patch_turned, 2 * (t - 2))
                nc.gpsimd.tensor_scalar(patches[:, t % 3, :].rearrange("p (l x) -> p l x", x=PS),
                                        lines[:, r, :, col:col + PS], 1.0, 0.0, ALU.mult, ALU.add
                                        ).then_inc(patches_gathered, 1)

            gather_patches(0)
            pool.wait_ge(cols_copied, 1)
            for k in range(KC):
                last = nc.gpsimd.tensor_copy(kvb_wide[:, k, :], kvb_cols[:, k:k + 1].broadcast_to([P, P]))
            last.then_inc(kvb_widened, 1)
            for s in range(STEPS):
                if s + 1 < NT:
                    gather_patches(s + 1)
                if 0 <= s - 1 < NT:
                    sum_reduced(s - 1)
                for w in range(NW):
                    at = s - NP * w
                    if at == RED:
                        pool.wait_ge(var_done, VAR_ORDER.index(("red", w)) + 1)
                        if w < NW - 1:
                            power(rstd[:, w, :], var_eps[:, w, :], rstd_done)
                        else:
                            power(rstd[:, w, NP:], var_eps[:, w, NP:], rstd_done)
                            power(rstd[:, w, 0:NP], var_eps[:, w, 0:NP], last_rstd_done)
                        link(nc.gpsimd.tensor_scalar(mu9[:, w:w + 1], redsum[:, w % 2, C:C + 1], 1.0 / NP, None,
                                                     ALU.mult))
                        link(nc.gpsimd.tensor_scalar(redp[:, w % 2, :], redsum[:, w % 2, 0:C], 1.0 / NP,
                                                     mu9[:, w:w + 1], ALU.mult, ALU.add))
                        if w == 0:
                            pool.wait_ge(late_loaded, 16 * LATE)
                        nc.gpsimd.tensor_tensor(redp[:, w % 2, :], redp[:, w % 2, :], row["proj_b"][:], ALU.add
                                                ).then_inc(redp_done, 1)
                    if at == SCORE:
                        pool.wait_ge(result_copied, copied("query", w))
                        pool.wait_ge(result_copied, copied("kv", NP * w + NP - 1))
                        if w >= 1:
                            pool.wait_ge(agg_done, w)
                        scored = sum(pairs_step(v) < s for v in range(T))
                        if scored:
                            pool.wait_ge(pairs_scored, scored)
                        nc.gpsimd.tensor_tensor(prod[:, 6:9, :], kv[:, w % 2, 6:9, 0:C],
                                                q_sb[:, w % 2, :].unsqueeze(1).broadcast_to([P, 3, C]), ALU.mult
                                                ).then_inc(pool_scored, 1)
                    if at == WEIGH:
                        pool.wait_ge(probs_done, w + 1)
                        nc.gpsimd.tensor_tensor(
                            prod[:, 6:9, :].rearrange("p n (h d) -> p n h d", h=H8),
                            kv[:, w % 2, 6:9, C:2 * C].rearrange("p n (h d) -> p n h d", h=H8),
                            probe[:, 1, 6:9, :].unsqueeze(3).broadcast_to([P, 3, H8, DH]), ALU.mult
                        ).then_inc(pool_weighed, 1)
                    if s == LOCAL_STEP[w]:
                        pool.wait_ge(var_done, VAR_ORDER.index(("local", w)) + 1)
                        power(rs[:, w:w + 1], ve[:, w:w + 1], rstd_done)
                for w in range(1, T):
                    if s == pairs_step(w):
                        pool.wait_ge(qkv_done, w + 1)
                        pool.wait_ge(pairs_scored, w)
                        pool.wait_ge(agg_done, sum(NP * v + SUM + 1 < s for v in range(NW)))
                        if GATT < s:
                            pool.wait_ge(gagg_done, 1)
                        pair_products(nc.gpsimd, w, False, max(0, w - POOL_PAIRS), w).then_inc(pool_paired, 1)
                if s == CLASSQ - 1:
                    pool.wait_ge(var_done, VAR_ORDER.index(("class", 0)) + 1)
                    power(rs[:, NW:T], ve[:, NW:T], rstd_done)
                if SPLIT0 <= s < SPLIT0 + J:
                    j = s - SPLIT0
                    raw, hi, lo = piece(j)
                    pool.wait_ge(w_hi_done, j + 1)
                    nc.gpsimd.tensor_tensor(lo(0), raw, hi(0).bitcast(F32), ALU.subtract).then_inc(pool_lo_done, 1)

            pool.wait_ge(probs_done, NW + 2)
            for i in POOL_QUERIES:
                weigh_tokens(nc.gpsimd, i).then_inc(pool_valued, 1)
            pool.wait_ge(var_done, VAR_ORDER.index("attention") + 1)
            power(rs[:, 1:T], ve[:, 1:T], rstd_done)
            pool.wait_ge(var_done, VAR_ORDER.index("attention_last") + 1)
            power(rs[:, 0:1], ve[:, 0:1], rstd_done)
            pool.wait_ge(h1_done, T)
            nc.gpsimd.memset(chosen[:, T, :], 0.0)
            nc.gpsimd.memset(b2_wide[:], 0.0).then_inc(b2_cleared, 1)
            for b in range(BANKS):
                cut = slice(2 * b, min(2 * b + 2, T))
                nc.gpsimd.tensor_copy(acc[:, cut, :], h1[:, cut, :]).then_inc(acc_ready, 1)

            def split_low(k, u, j):
                raw, hi, lo = piece(j)
                pool.wait_ge(w_hi_done, J * k + j + 1)
                nc.gpsimd.tensor_tensor(lo(u), raw, hi(u).bitcast(F32), ALU.subtract).then_inc(pool_lo_done, 1)

            for j in (0, 2):
                split_low(1, 1, j)
            pool.wait_ge(rows_found, 1)
            pool.wait_ge(x_cleared, 16)
            for k in range(2):
                for i in range(T):
                    nc.gpsimd.indirect_dma_start(x_rows, bass.IndirectOffsetOnAxis(ap=row_to[:, k, i:i + 1], axis=0),
                                                 h1[:, i, :], None).then_inc(rows_sent, 16)
            for j in (4, 6):
                split_low(1, 1, j)
            pool.wait_ge(table_made, 1)
            loops = pool.value_load(table[0:1, COUNT:COUNT + 1], min_val=1, max_val=PAIRS - 1)
            with pool.Fori(0, loops) as i:
                for u in range(2):
                    for j in range(0, J, 2):
                        split_low(2 * i + 2 + u, u, j)
            for j in range(0, J, 2):
                split_low(2 * loops + 2, 0, j)
            pool.wait_ge(y_stored, 32 * loops + 48)
            link(nc.gpsimd.tensor_tensor(ve[:, 0:1], all_ones[:, 0:1], all_ones[:, 0:1], ALU.mult))
            pool.wait_ge(rows_found, 2)
            for i in range(T):
                for k in range(2):
                    nc.gpsimd.indirect_dma_start(att_prod[:, i, k, :], None, y_rows,
                                                 bass.IndirectOffsetOnAxis(ap=row_from[:, k, i:i + 1], axis=0)
                                                 ).then_inc(rows_fetched[i], 16)
            pool.wait_ge(var_done, VAR_ORDER.index("output") + 1)
            power(rs[:, 0:T - 1], ve[:, 0:T - 1], rstd_done)
            pool.wait_ge(var_done, VAR_ORDER.index("output_last") + 1)
            power(rs[:, T - 1:T], ve[:, T - 1:T], rstd_done)

        @block.vector
        def _(dve):
            chain = [0]

            def link(ins):
                chain[0] += 1
                return ins.then_inc(dve_chain, 1)

            def settle():
                dve.wait_ge(dve_chain, chain[0])

            V = nc.vector
            dve.wait_ge(conv_w_turned, 1)
            link(V.tensor_reduce(conv_mean[0:K, 0, :], psum[0:K, 0:NK, 0:C], AX_X, ALU.add))
            settle()
            V.tensor_scalar(conv_mean[0:K, 1, :], conv_mean[0:K, 0, :], -1.0 / C, None, ALU.mult
                            ).then_inc(conv_mean_made, 1)
            link(V.tensor_scalar(conv_mean[0:K, 0, :], conv_mean[0:K, 0, :], 1.0 / C, None, ALU.mult))
            dve.wait_ge(conv_mean_made, 1)
            settle()
            mean_twice = conv_mean[0:K, 0, :].unsqueeze(2).broadcast_to([K, NK, 2])
            link(V.tensor_copy(conv_hi[0:K, :, C:CW], mean_twice))
            settle()
            link(V.tensor_tensor(conv_lo[0:K, :, C:CW], mean_twice, conv_hi[0:K, :, C:CW].bitcast(F32), ALU.subtract))
            for k in range(NK):
                dve.wait_ge(conv_hi_done, k + 1)
                V.scalar_tensor_tensor(out=conv_lo[0:K, k, 0:C], in0=psum[0:K, k, 0:C],
                                       scalar=conv_mean[0:K, 1, k:k + 1], in1=conv_hi[0:K, k, 0:C].bitcast(F32),
                                       op0=ALU.add, op1=ALU.subtract).then_inc(conv_w_centred, 1)
            dve.wait_ge(conv_w_centred, NK)
            settle()
            V.memset(conv_hi[0:OVER, NK - 1, :].bitcast(F32), 0.0).then_inc(conv_w_split, 1)
            V.memset(conv_lo[0:OVER, NK - 1, :].bitcast(F32), 0.0).then_inc(conv_w_split, 1)

            def split_wkv():
                dve.wait_ge(wkv_loaded, 16)
                dve.wait_ge(cols_copied, 1)
                for k in range(KC):
                    link(V.tensor_scalar(wkv_hi[:, k, :], wkv_raw[:, k, :], kvg_cols[:, k:k + 1], None, ALU.mult))
                settle()
                for k in range(KC):
                    last = V.scalar_tensor_tensor(out=wkv_lo[:, k, :], in0=wkv_raw[:, k, :], scalar=kvg_cols[:, k:k + 1],
                                                  in1=wkv_hi[:, k, :].bitcast(F32), op0=ALU.mult, op1=ALU.subtract)
                last.then_inc(wkv_split, 1)

            def patch_lows(t):
                for g, (a, b) in enumerate(GROUPS):
                    dve.wait_ge(patch_hi_done, 2 * t + g + 1)
                    V.tensor_tensor(patch_lo[0:K, t % 2, a:b, :],
                                    psum[0:K, PATCH_BANK[(2 * t + g) % 3], 0:(b - a) * P].rearrange(
                                        "p (k t) -> p k t", t=P),
                                    patch_hi[0:K, t % 2, a:b, :].bitcast(F32), ALU.subtract).then_inc(patch_lo_done, 1)

            def turn_low(t):
                dve.wait_ge(turn_copied, turn_order.index(("kv", t)) + 1)
                V.tensor_tensor(turn_lo[:, t % 2, :], psum[:, TURN_BANK, 0:C], turn_hi[:, t % 2, :].bitcast(F32),
                                ALU.subtract).then_inc(turn_lo_done, 1)

            def square_sum(t):
                w, n = divmod(t, NP)
                dve.wait_ge(cen_copied, t + 1)
                if t >= 1:
                    dve.wait_ge(sumsq_done, t)
                c = cen[:, t % CEN_RING, 0:C]
                V.tensor_tensor_reduce(junk[:], c, c, 1.0, 0.0, ALU.mult, ALU.add,
                                       sumsq[:, w, n:n + 1]).then_inc(sumsq_done, 1)

            def layer_norm_stats(src, i):
                link(V.bn_stats(bn[:, i, :], src))
                settle()
                link(V.bn_aggr(mv[:, i, :], bn[:, i, :]))
                settle()
                V.tensor_scalar(ve[:, i:i + 1], mv[:, i, 1:2], EPS, None, ALU.add).then_inc(var_done, 1)

            def layer_norm(dst, src, i, gain, bias, done):
                link(V.tensor_scalar(work[:], src, mv[:, i, 0:1], rs[:, i:i + 1], ALU.subtract, ALU.mult))
                settle()
                link(V.tensor_tensor(work[:], work[:], gain, ALU.mult))
                settle()
                V.tensor_tensor(dst, work[:], bias, ALU.add).then_inc(done, 1)

            def reduced_query(w):
                dve.wait_ge(rstd_done, VAR_ORDER.index(("red", w)) + 1)
                link(V.tensor_scalar(work[:], redsum[:, w % 2, 0:C], 1.0 / NP, rstd[:, w, NP:NP + 1], ALU.mult, ALU.mult))
                settle()
                link(V.tensor_tensor(work[:], work[:], row["q_g"][:], ALU.mult))
                settle()
                V.tensor_tensor(redln[:], work[:], row["q_b"][:], ALU.add).then_inc(redln_done, 1)

            def heads(ap):
                return ap.rearrange("p n (h d) -> p n h d", h=H8)

            def score_products(w, c):
                n = slice(3 * c, 3 * c + 3)
                if c == 2:
                    dve.wait_ge(pool_scored, w + 1)
                else:
                    link(V.tensor_tensor(prod[:, n, :], kv[:, w % 2, n, 0:C],
                                         q_sb[:, w % 2, :].unsqueeze(1).broadcast_to([P, 3, C]), ALU.mult))
                    settle()
                link(V.tensor_reduce(score[:, 0, n, :], heads(prod[:, n, :]), AX_X, ALU.add))

            def softmax_shift(w):
                by_patch = rstd[:, w, 0:NP].unsqueeze(2).broadcast_to([P, NP, H8])
                settle()
                if w == NW - 1:
                    dve.wait_ge(last_rstd_done, 1)
                link(V.tensor_tensor(score[:, 0], score[:, 0], by_patch, ALU.mult))
                settle()
                link(V.tensor_tensor(score[:, 0], score[:, 0], qbk[:].unsqueeze(1).broadcast_to([P, NP, H8]), ALU.add))
                settle()
                link(V.tensor_reduce(stat8[:, 0, :], score[:, 0].rearrange("p n h -> p h n"), AX_X, ALU.max))
                settle()
                V.tensor_tensor(score[:, 1], score[:, 0], stat8[:, 0, :].unsqueeze(1).broadcast_to([P, NP, H8]),
                                ALU.subtract).then_inc(shifted, 1)

            def softmax_weights(w):
                dve.wait_ge(exp_done, w + 1)
                link(V.tensor_reduce(stat8[:, 1, :], score[:, 2].rearrange("p n h -> p h n"), AX_X, ALU.add))
                settle()
                link(V.reciprocal(stat8[:, 2, :], stat8[:, 1, :]))
                settle()
                link(V.tensor_tensor(probe[:, 0], score[:, 2],
                                     stat8[:, 2, :].unsqueeze(1).broadcast_to([P, NP, H8]), ALU.mult))
                settle()
                V.tensor_tensor(probe[:, 1], probe[:, 0], rstd[:, w, 0:NP].unsqueeze(2).broadcast_to([P, NP, H8]),
                                ALU.mult).then_inc(probs_done, 1)

            def weigh_values(w, c):
                n = slice(3 * c, 3 * c + 3)
                dve.wait_ge(probs_done, w + 1)
                link(V.tensor_tensor(heads(prod[:, n, :]), heads(kv[:, w % 2, n, C:2 * C]),
                                     probe[:, 1, n, :].unsqueeze(3).broadcast_to([P, 3, H8, DH]), ALU.mult))

            def sum_values(w, part):
                cut = slice(part * C // 2, (part + 1) * C // 2)
                settle()
                dve.wait_ge(pool_weighed, w + 1)
                link(V.tensor_reduce(agg[:, cut], prod[:, :, cut].rearrange("p n c -> p c n"), AX_X, ALU.add))
                if part == 1:
                    settle()
                    V.tensor_tensor(agg[:], agg[:], kv_bias[:, C:2 * C], ALU.add).then_inc(agg_done, 1)

            def take_qkv(w):
                dve.wait_ge(result_copied, copied("qkv", w, 1))
                V.tensor_tensor(aq[:, w, :], qkv_res[:, 0:C], row["qkv_b"][:, 0:C], ALU.add)
                V.tensor_tensor(akv[:, T - 1 - w, :], qkv_res[:, C:3 * C], row["qkv_b"][:, C:3 * C], ALU.add
                                ).then_inc(qkv_done, 1)

            def score_pairs(w):
                dve.wait_ge(qkv_done, w + 1)
                first = max(0, w - POOL_PAIRS)
                if w:
                    dve.wait_ge(pairs_scored, w)
                settle()
                link(pair_products(V, w, True, 0, w + 1))
                if first:
                    link(pair_products(V, w, False, 0, first))
                settle()
                by_head = prod.rearrange("p n (h d) -> p n h d", h=H16)
                ins = V.tensor_reduce(att_raw[:, w, :, T - 1 - w:T].rearrange("p h j -> p j h"),
                                      by_head[:, 0:w + 1], AX_X, ALU.add)
                if w:
                    link(ins)
                    dve.wait_ge(pool_paired, w)
                    ins = V.tensor_reduce(att_raw[:, 0:w, :, T - 1 - w], by_head[:, w + 1:2 * w + 1], AX_X, ALU.add)
                ins.then_inc(pairs_scored, 1)

            for s in range(STEPS):
                if s < NT:
                    patch_lows(s)
                if s == 0:
                    split_wkv()
                if 0 <= s - KV_LAG < NT:
                    turn_low(s - KV_LAG)
                if 0 <= s - 1 < NT:
                    square_sum(s - 1)
                if s == CLASSQ - 1:
                    dve.wait_ge(late_loaded, 16 * LATE)
                    layer_norm_stats(row["class"][:], NW)
                if s == CLASSQ + 4:
                    dve.wait_ge(result_copied, copied("gquery", 0))
                    for k in range(KC):
                        settle()
                        link(V.tensor_tensor(work[:], gwk_sb[:, k, :], gq_sb[:], ALU.mult))
                        settle()
                        last = V.tensor_reduce(gwv_sb[:, k, 0:H8], work[:].rearrange("p (h d) -> p h d", h=H8), AX_X, ALU.add)
                        if k < KC - 1:
                            link(last)
                    last.then_inc(class_keys_done, 1)
                    dve.wait_ge(class_keys_done, 1)
                if s == CLASSQ:
                    dve.wait_ge(rstd_done, VAR_ORDER.index(("class", 0)) + 1)
                    layer_norm(class_ln[:], row["class"][:], NW, row["gq_g"][:], row["gq_b"][:], class_ln_done)
                for w in range(NW):
                    at = s - NP * w
                    if at == RED:
                        dve.wait_ge(sumsq_done, NP * (w + 1))
                        dve.wait_ge(red_summed, NP * (w + 1))
                        link(V.tensor_tensor_reduce(work[:], redsum[:, w % 2, 0:C], redsum[:, w % 2, 0:C], 1.0, 0.0, ALU.mult,
                                                    ALU.add, sumsq[:, w, NP:NP + 1]))
                        link(V.tensor_scalar(var_eps[:, w, 0:NP], sumsq[:, w, 0:NP], 1.0 / C, EPS, ALU.mult, ALU.add))
                        settle()
                        V.tensor_scalar(var_eps[:, w, NP:NP + 1], sumsq[:, w, NP:NP + 1], 1.0 / (C * NP * NP), EPS,
                                        ALU.mult, ALU.add).then_inc(var_done, 1)
                    if at == RED + 1:
                        reduced_query(w)
                    if at == SCORE:
                        dve.wait_ge(result_copied, copied("query", w))
                        if w == 0:
                            dve.wait_ge(kv_bias_copied, 1)
                        link(V.tensor_tensor(work[:], q_sb[:, w % 2, :], kv_bias[:, 0:C], ALU.mult))
                        settle()
                        link(V.tensor_reduce(qbk[:], work[:].rearrange("p (h d) -> p h d", h=H8), AX_X, ALU.add))
                        score_products(w, 0)
                    if at == SCORE + 1:
                        score_products(w, 1)
                    if at == SCORE + 2:
                        score_products(w, 2)
                        softmax_shift(w)
                    if at == WEIGH:
                        softmax_weights(w)
                        weigh_values(w, 0)
                    if at == WEIGH + 1:
                        weigh_values(w, 1)
                    if at == SUM:
                        sum_values(w, 0)
                    if at == SUM + 1:
                        sum_values(w, 1)
                    if s == LOCAL_STEP[w]:
                        dve.wait_ge(result_copied, copied("proj", w))
                        dve.wait_ge(redp_done, w + 1)
                        V.tensor_tensor(local[:, w % 2, :], res[:, 0, :], redp[:, w % 2, :], ALU.add).then_inc(local_done, 1)
                        dve.wait_ge(local_done, w + 1)
                        layer_norm_stats(local[:, w % 2, :], w)
                    if s == LOCAL_STEP[w] + 1:
                        dve.wait_ge(rstd_done, VAR_ORDER.index(("local", w)) + 1)
                        layer_norm(kvln[:], local[:, w % 2, :], w, row["gkv_g"][:], row["gkv_b"][:], kvln_done)
                    if s == TOKEN_STEP[w]:
                        dve.wait_ge(result_copied, copied("mod", w))
                        V.tensor_tensor(hs[:, w, :], res[:, 1, :], row["mod_b"][:], ALU.add).then_inc(token_done, 1)
                    if s == TAKE_STEP[w]:
                        take_qkv(w)
                if s == GATT:
                    dve.wait_ge(result_copied, copied("gkv", NW - 1))
                    settle()
                    scores = gkv_sb[:, :, 0:H8]
                    link(V.tensor_reduce(gstat[:, 0, :], scores.rearrange("p n h -> p h n"), AX_X, ALU.max))
                    settle()
                    V.tensor_tensor(gscore[:, 1], scores, gstat[:, 0, :].unsqueeze(1).broadcast_to([P, NW, H8]),
                                    ALU.subtract).then_inc(shifted, 1)
                    dve.wait_ge(exp_done, NW + 1)
                    link(V.tensor_reduce(gstat[:, 1, :], gscore[:, 2].rearrange("p n h -> p h n"), AX_X, ALU.add))
                    settle()
                    link(V.reciprocal(gstat[:, 2, :], gstat[:, 1, :]))
                    settle()
                    V.tensor_tensor(gprob[:], gscore[:, 2], gstat[:, 2, :].unsqueeze(1).broadcast_to([P, NW, H8]),
                                    ALU.mult).then_inc(probs_done, 1)
                    dve.wait_ge(probs_done, NW + 1)
                    link(V.tensor_tensor(heads(prod[:, 0:NW, :]), heads(gkv_sb[:, :, H8:]),
                                         gprob[:].unsqueeze(3).broadcast_to([P, NW, H8, DH]), ALU.mult))
                    settle()
                    V.tensor_reduce(gagg[:], prod[:, 0:NW, :].rearrange("p n c -> p c n"), AX_X, ALU.add
                                    ).then_inc(gagg_done, 1)
                if s == CLASSO + 2:
                    dve.wait_ge(result_copied, copied("gproj", 0))
                    link(V.tensor_tensor(work[:], res[:, 2, :], row["gproj_b"][:], ALU.add))
                    settle()
                    V.tensor_tensor(hs[:, NW, :], work[:], row["class"][:], ALU.add).then_inc(token_done, 1)
                if s == CLASSO + 5:
                    take_qkv(NW)
                for w in range(T):
                    if s == pairs_step(w):
                        score_pairs(w)

            settle()
            dve.wait_ge(pairs_scored, T)
            over_keys = [P, T, H16, T]
            for k in range(T):
                link(V.scalar_tensor_tensor(out=att_s[:, 0, k], in0=att_raw[:, k], scalar=DK ** -0.5,
                                            in1=rel_rows[:, :, k:k + T], op0=ALU.mult, op1=ALU.add))
            settle()
            link(V.tensor_reduce(att_m[:, 0], att_s[:, 0], AX_X, ALU.max))
            settle()
            V.tensor_tensor(att_s[:, 1], att_s[:, 0], att_m[:, 0].unsqueeze(3).broadcast_to(over_keys),
                            ALU.subtract).then_inc(shifted, 1)
            dve.wait_ge(exp_done, NW + 2)
            link(V.tensor_reduce(att_m[:, 1], att_s[:, 2], AX_X, ALU.add))
            settle()
            link(V.reciprocal(att_m[:, 2], att_m[:, 1]))
            settle()
            V.tensor_tensor(att_s[:, 1], att_s[:, 2], att_m[:, 2].unsqueeze(3).broadcast_to(over_keys),
                            ALU.mult).then_inc(probs_done, 1)
            dve.wait_ge(probs_done, NW + 2)
            for i in DVE_QUERIES:
                weigh_tokens(V, i).then_inc(dve_valued, 1)
            for n, i in enumerate(DVE_SUMS):
                dve.wait_ge(dve_valued, DVE_QUERIES.index(i) + 1)
                link(V.tensor_reduce(att_o[:, n, :], att_prod[:, i].rearrange("p j c -> p c j"), AX_X, ALU.add))
            settle()
            dve.wait_ge(token_done, T)
            link(V.tensor_tensor(att_o[:], att_o[:], hs[:, DVE_SUMS[0]:DVE_SUMS[-1] + 1, :], ALU.add))
            settle()

            def attended(i):
                return psum[:, PE_SUMS.index(i), 0:C] if i in PE_SUMS else att_o[:, DVE_SUMS.index(i), :]

            def stats(i):
                if i in PE_SUMS:
                    dve.wait_ge(values_summed, PE_SUMS.index(i) + 1)
                link(V.bn_stats(bn[:, i, :], attended(i)))
                settle()
                link(V.bn_aggr(mv[:, i, :], bn[:, i, :]))

            for i in DVE_SUMS + PE_SUMS[:-1]:
                stats(i)
            settle()
            V.tensor_scalar(ve[:, 1:T], mv[:, 1:T, 1], EPS, None, ALU.add).then_inc(var_done, 1)
            stats(0)
            settle()
            V.tensor_scalar(ve[:, 0:1], mv[:, 0:1, 1], EPS, None, ALU.add).then_inc(var_done, 1)
            dve.wait_ge(rstd_done, VAR_ORDER.index("attention") + 1)
            for n, i in enumerate(XT_ORDER):
                if i == 0:
                    dve.wait_ge(rstd_done, VAR_ORDER.index("attention_last") + 1)
                V.tensor_scalar(h1[:, i, :], attended(i), mv[:, i, 0:1], rs[:, i:i + 1], ALU.subtract, ALU.mult
                                ).then_inc(h1_done, 1)
            for n, i in enumerate(XT_ORDER):
                dve.wait_ge(xt_copied, n + 1)
                V.tensor_tensor(xt_lo[:, :, i * P:(i + 1) * P],
                                psum[:, XT_BANK[n % 3], 0:C].rearrange("p (k t) -> p k t", k=KC),
                                xt_hi[:, :, i * P:(i + 1) * P].bitcast(F32), ALU.subtract).then_inc(xt_split, 1)

            per_token = [P, T, E]

            def gate_logits():
                dve.wait_ge(gate_scored, 1)
                link(V.tensor_tensor(g8[:, 0], psum[:, GATE_BANK, 0:T * E].rearrange("p (t e) -> p t e", e=E),
                                     row["bg"][:].unsqueeze(1).broadcast_to(per_token), ALU.add))
                settle()
                link(V.tensor_reduce(gt[:, 0], g8[:, 0], AX_X, ALU.max))
                settle()
                V.tensor_tensor(g8[:, 1], g8[:, 0], gt[:, 0].unsqueeze(2).broadcast_to(per_token), ALU.subtract
                                ).then_inc(shifted, 1)

            def gate_probs():
                dve.wait_ge(exp_done, NW + 3)
                link(V.tensor_reduce(gt[:, 1], g8[:, 2], AX_X, ALU.add))
                settle()
                link(V.reciprocal(gt[:, 2], gt[:, 1]))
                settle()
                link(V.tensor_tensor(g8[:, 3], g8[:, 2], gt[:, 2].unsqueeze(2).broadcast_to(per_token), ALU.mult))
                settle()
                for i in range(T):
                    link(V.max(g8[:, 4, i], g8[:, 3, i]))
                settle()

            def gate_choice():
                for i in range(T):
                    link(V.max_index(top_at[:, i], g8[:, 4, i], g8[:, 3, i]))
                V.tensor_tensor(gt[:, 5], g8[:, 4, :, 1], g8[:, 4, :, 0], ALU.subtract).then_inc(shifted, 1)
                settle()
                link(V.tensor_copy(gt[:, 3:5], top_at[:, :, 0:2].rearrange("p t k -> p k t")))

            def pair_softmax():
                dve.wait_ge(exp_done, NW + 4)
                link(V.tensor_scalar(gt[:, 7], gt[:, 6], 1.0, None, ALU.add))
                settle()
                link(V.reciprocal(gt[:, 8], gt[:, 7]))
                settle()
                link(V.tensor_tensor(gt[:, 9], gt[:, 6], gt[:, 8], ALU.mult))
                settle()

            def mark_choices():
                for k in range(2):
                    link(V.tensor_tensor(choice[:, k], iota8[:].unsqueeze(1).broadcast_to(per_token),
                                         gt[:, 3 + k].unsqueeze(2).broadcast_to(per_token), ALU.is_equal))
                settle()
                dve.wait_ge(b2_cleared, 1)
                V.tensor_tensor(chosen[:, 0:T, :], choice[:, 0], choice[:, 1], ALU.add).then_inc(chosen_made, 1)

            def make_gates():
                for k in range(2):
                    link(V.tensor_tensor(g8[:, 5 * (1 - k)], choice[:, k], gt[:, 8 + k].unsqueeze(2).broadcast_to(per_token),
                                         ALU.mult))
                settle()
                V.tensor_tensor(gates[:], g8[:, 0], g8[:, 5], ALU.add).then_inc(gates_done, 1)

            def find_rows():
                dve.wait_ge(ranked, 1)
                rank = psum[:, GATE_BANK, 0:(T + 1) * E].rearrange("p (t e) -> p t e", e=E)
                users = rank[:, T, :]
                link(V.tensor_scalar(need[:, 0, :], users, 0.0, None, ALU.is_gt))
                settle()
                link(V.memset(need[:, 0, E - 1:E], 1.0))
                for n in range(1, -(-TOK // BLOCK)):
                    settle()
                    link(V.scalar_tensor_tensor(out=need[:, n, :], in0=users, scalar=float(n * BLOCK), in1=need[:, n - 1, :],
                                                op0=ALU.is_gt, op1=ALU.add))
                blocks = need[:, n, :]
                settle()
                link(V.memset(need[:, n, DENSE:DENSE + 1], 0.0))
                settle()
                link(V.tensor_tensor(later[:], later[:], blocks.unsqueeze(1).broadcast_to([P, E, E]), ALU.mult))
                settle()
                link(V.tensor_reduce(need[:, 3, :], later[:], AX_X, ALU.add))
                settle()
                link(V.tensor_scalar(need[:, 5, :], need[:, 3, :], float(BLOCK), None, ALU.mult))
                link(V.tensor_tensor(need[:, 4, :], need[:, 3, :], blocks, ALU.add))
                settle()
                link(V.tensor_tensor(place[:], rank[:, 0:T, :], need[:, 5, :].unsqueeze(1).broadcast_to(per_token), ALU.add))
                settle()
                link(V.tensor_copy(place[:, :, DENSE], spare[:]))
                settle()
                link(V.tensor_tensor(placed[:], choice[:], place[:].unsqueeze(1).broadcast_to([P, 2, T, E]), ALU.mult))
                settle()
                link(V.tensor_reduce(found[:, 0], placed[:], AX_X, ALU.add))
                settle()
                V.tensor_copy(row_to[:], found[:, 0]).then_inc(rows_found, 1)

            def find_sources():
                link(V.tensor_scalar(found[:, 1], found[:, 0], float(SPARE), None, ALU.is_lt))
                settle()
                link(V.tensor_tensor(found[:, 2], found[:, 0], found[:, 1], ALU.mult))
                link(V.tensor_tensor(found[:, 3], gt[:, 8:10, :], found[:, 1], ALU.mult))
                settle()
                V.tensor_copy(row_from[:], found[:, 2]).then_inc(rows_found, 1)

            def make_table():
                link(V.tensor_tensor(passed[:], block_no[:].unsqueeze(2).broadcast_to([1, MAX_BLOCKS, E]),
                                     need[0:1, 4, :].unsqueeze(1).broadcast_to([1, MAX_BLOCKS, E]), ALU.is_ge))
                settle()
                link(V.tensor_reduce(order[0:1, 0, 0:MAX_BLOCKS], passed[:], AX_X, ALU.add))
                settle()
                link(V.tensor_scalar(order[0:1, 0, 0:MAX_BLOCKS], order[0:1, 0, 0:MAX_BLOCKS], -1.0, float(E - 1),
                                     ALU.mult, ALU.add))
                settle()
                link(V.tensor_scalar(order[0:1, 0, 0:MAX_BLOCKS], order[0:1, 0, 0:MAX_BLOCKS], 0.0, None, ALU.max))
                late = slice(4, MAX_BLOCKS, 2)
                link(V.tensor_scalar(order[0:1, 1, late], block_no[0:1, late], need[0:1, 4, 0:1], None, ALU.is_lt))
                settle()
                link(V.tensor_reduce(order[0:1, 0, COUNT:COUNT + 1], order[0:1, 1, late], AX_X, ALU.add))
                settle()
                link(V.tensor_scalar(order[0:1, 0, COUNT:COUNT + 1], order[0:1, 0, COUNT:COUNT + 1], 1.0, None, ALU.add))
                settle()
                V.tensor_copy(table[0:1, :], order[0:1, 0, :]).then_inc(table_made, 1)

            def split_hidden(j):
                dve.wait_ge(relu_done, j + 1)
                if j >= 2:
                    dve.wait_ge(hidden_used, j - 1)
                V.tensor_copy(h_hi[:, j % 2, :], h_f[:, j % 2, :]).then_inc(h_hi_done, 1)
                dve.wait_ge(h_hi_done, j + 1)
                V.tensor_tensor(h_lo[:, j % 2, :], h_f[:, j % 2, :], h_hi[:, j % 2, :].bitcast(F32), ALU.subtract
                                ).then_inc(h_split, 1)

            def split_low(k, u, j):
                if j % 2 == 0:
                    return
                raw, hi, lo = piece(j)
                dve.wait_ge(w_hi_done, J * k + j + 1)
                dve.wait_ge(pool_lo_done, J // 2 * k + J // 2 + (j + 1) // 2)
                V.tensor_tensor(lo(u), raw, hi(u).bitcast(F32), ALU.subtract).then_inc(w_lo_done, 1)

            def block_split(k, j):
                dve.wait_ge(relu_done, J * k + j + 1)
                dve.wait_ge(hidden_used, J * k + j - 3)
                V.tensor_copy(chunk(h_hi, j), chunk(h_f, j)).then_inc(h_hi_done, 1)
                dve.wait_ge(h_hi_done, J * k + j + 1)
                V.tensor_tensor(chunk(h_lo, j), chunk(h_f, j), chunk(h_hi, j).bitcast(F32), ALU.subtract
                                ).then_inc(h_split, 1)

            def tokens_low(b, u):
                dve.wait_ge(xb_hi_done, b + 1)
                V.tensor_tensor(xb_lo[:, u], psum[:, GATE_BANK, :].rearrange("p (k t) -> p k t", k=KC),
                                xb_hi[:, u].bitcast(F32), ALU.subtract).then_inc(xb_split, 1)

            def add_dense(tiles):
                for i in tiles:
                    V.scalar_tensor_tensor(out=acc[:, i, :],
                                           in0=psum[:, EXPERT_BANK + i // 2, (i % 2) * C:(i % 2 + 1) * C],
                                           scalar=gates[:, i, DENSE:DENSE + 1], in1=acc[:, i, :],
                                           op0=ALU.mult, op1=ALU.add
                                           ).then_inc(bank_free if i in (1, 3) else dense_added, 1)

            def block(b, u, more=True, beside=lambda j: None):
                for j in range(2, J):
                    block_split(b + 1, j)
                    if more:
                        split_low(b + 2, u, j - 2)
                        if j == 5:
                            tokens_low(b + 1, 1 - u)
                    beside(j)
                if more:
                    for j in range(2):
                        block_split(b + 2, j)
                        split_low(b + 2, u, J - 2 + j)

            def beside(n):
                if n in (5, J + 2, J + 6):
                    r = (5, J + 2, J + 6).index(n)
                    a, b = 2 * r, min(2 * r + 2, T)
                    dve.wait_ge(gate_bias_done, r + 1)
                    if r == 0:
                        dve.wait_ge(dense_added, T - 2)
                        dve.wait_ge(bank_free, 2)
                    V.tensor_tensor(acc[:, a:b, :], psum[:, BIAS_BANK, 0:(b - a) * C].rearrange("p (i c) -> p i c", c=C),
                                    acc[:, a:b, :], ALU.add).then_inc(gate_bias_used, 1)

            dve.wait_ge(consts_made, 2)
            link(V.tensor_tensor(later[:], iota8[:].unsqueeze(1).broadcast_to([P, E, E]),
                                 iota8[:].unsqueeze(2).broadcast_to([P, E, E]), ALU.is_gt))
            gate_logits()
            gate_probs()
            gate_choice()
            pair_softmax()
            mark_choices()
            for j in range(J):
                split_hidden(j)
                split_low(1, 1, j)
                if j == 0:
                    make_gates()
                if j == 1:
                    find_rows()
                if j == 2:
                    find_sources()
                if j == 3:
                    make_table()
                if j == 4:
                    dve.wait_ge(gates_turned, 1)
                    V.tensor_copy(gates_t[:], psum[0:T * E, GATE_BANK, 0:P]).then_inc(gates_t_copied, 1)
            tokens_low(0, 0)
            dve.wait_ge(hidden_used, J)
            dve.wait_ge(acc_ready, BANKS)
            dve.wait_ge(gates_done, 1)
            add_dense((0, 1))
            block_split(1, 0)
            add_dense((2, 3))
            block_split(1, 1)
            add_dense((4,))
            dve.wait_ge(table_made, 1)
            loops = dve.value_load(table[0:1, COUNT:COUNT + 1], min_val=1, max_val=PAIRS - 1)
            with dve.Fori(0, loops) as i:
                block(2 * i, 0)
                block(2 * i + 1, 1)
            block(2 * loops, 0, beside=beside)
            block(2 * loops + 1, 1, more=False, beside=lambda j: beside(J + j))

            dve.wait_ge(gate_bias_used, BANKS)
            dve.wait_ge(rows_found, 2)
            for i in range(T):
                dve.wait_ge(rows_fetched[i], 2 * 16)
                for k in range(2):
                    link(V.scalar_tensor_tensor(out=acc[:, i, :], in0=att_prod[:, i, k, :], scalar=found[:, 3, k, i:i + 1],
                                                in1=acc[:, i, :], op0=ALU.mult, op1=ALU.add))
                    settle()
                link(V.bn_stats(bn[:, i, :], acc[:, i, :]))
                settle()
                link(V.bn_aggr(mv[:, i, :], bn[:, i, :]))
                if i == T - 2:
                    settle()
                    V.tensor_scalar(ve[:, 0:T - 1], mv[:, 0:T - 1, 1], EPS, None, ALU.add).then_inc(var_done, 1)
            settle()
            V.tensor_scalar(ve[:, T - 1:T], mv[:, T - 1:T, 1], EPS, None, ALU.add).then_inc(var_done, 1)
            dve.wait_ge(rstd_done, VAR_ORDER.index("output") + 1)
            for i in range(T):
                if i == T - 1:
                    dve.wait_ge(rstd_done, VAR_ORDER.index("output_last") + 1)
                V.tensor_scalar(fin[:, i, :], acc[:, i, :], mv[:, i, 0:1], rs[:, i:i + 1], ALU.subtract, ALU.mult
                                ).then_inc(fin_done, 1)


_INS = [
    "x", "L0_tok_conv_w", "L0_tok_class_emb", "L0_tok_la_ln_q_g", "L0_tok_la_ln_q_b", "L0_tok_la_wq",
    "L0_tok_la_ln_kv_g", "L0_tok_la_ln_kv_b", "L0_tok_la_wkv", "L0_tok_la_proj_w", "L0_tok_la_proj_b",
    "L0_tok_ga_ln_q_g", "L0_tok_ga_ln_q_b", "L0_tok_ga_wq", "L0_tok_ga_ln_kv_g", "L0_tok_ga_ln_kv_b",
    "L0_tok_ga_wkv", "L0_tok_ga_proj_w", "L0_tok_ga_proj_b", "L0_tok_mod_w", "L0_tok_mod_b",
    "L0_attn_Wq", "L0_attn_bq", "L0_attn_Wk", "L0_attn_bk", "L0_attn_Wv", "L0_attn_bv", "L0_attn_rel_emb",
    "L0_ffn_W1", "L0_ffn_b1", "L0_ffn_W2", "L0_ffn_b2", "L0_ffn_Wg", "L0_ffn_bg",
]
_OUT_SHAPE = (128, 5, 256)


def kernel(**inputs):
    import numpy as _np
    import concourse.bacc as _bacc
    from concourse import mybir as _mybir
    from concourse.bass_utils import run_bass_kernel_spmd as _run

    nc = _bacc.Bacc("TRN2", target_bir_lowering=False, num_devices=1,
                    dynamic_dma_scratch_size=1024)
    arrays, args = {}, []
    for name in _INS:
        a = _np.ascontiguousarray(inputs[name])
        arrays[f"in_{name}_dram"] = a
        args.append(nc.dram_tensor(f"in_{name}_dram", a.shape, _mybir.dt.from_np(a.dtype), kind="ExternalInput").ap())
    args.append(nc.dram_tensor("out_0_dram", _OUT_SHAPE, _mybir.dt.float32, kind="ExternalOutput").ap())
    build(nc, *args)
    r = _run(nc, [arrays], core_ids=[0])
    return r.results[0]["out_0_dram"]
```
